# Optimizing a Trainium2 kernel written in Bass

```python
import numpy as np
import jax
import jax.numpy as jnp

def _softmax(x, axis=-1):
    return jax.nn.softmax(x, axis=axis)

def _gelu(x):
    return jax.nn.gelu(x, approximate=True)

def _silu(x):
    return jax.nn.silu(x)

def _sigmoid(x):
    return jax.nn.sigmoid(x)

def _layernorm(x, axis=-1, eps=1e-05):
    m = jnp.mean(x, axis=axis, keepdims=True)
    v = jnp.var(x, axis=axis, keepdims=True)
    return (x - m) / jnp.sqrt(v + eps)

def _scatter_add(tgt, idx, src, axis=0):
    return tgt.at[idx].add(src)

def _segment_sum(src, seg, n):
    return jax.ops.segment_sum(src, seg, n)
kernel_name = 'mk_xattn_ffn_d1_seqx_r4_d2e700'

def setup_inputs(seed: int=0):
    np.random.seed(seed)
    _w = jnp.asarray

    def _rec_inputs():
        import jax
        import jax.numpy as jnp
        _rk = jax.random.key(seed)
        x = -0.0002928 + 1 * jax.random.normal(jax.random.fold_in(_rk, 1), (4, 512, 256), jnp.float32)
        _lenS = 512 - jax.random.randint(jax.random.fold_in(_rk, 7), (4,), 0, max(1, 512 // 4) + 1, jnp.int32)
        _lenS2 = 64 - jax.random.randint(jax.random.fold_in(_rk, 8), (4,), 0, max(1, 64 // 4) + 1, jnp.int32)
        _ctx_1024P = jax.random.normal(jax.random.fold_in(_rk, 11), (4, 16, 256), jnp.float32)
        _ctx_1024c = jax.random.dirichlet(jax.random.fold_in(_rk, 511), 0.3 * jnp.ones((16,), jnp.float32), (4, 64))
        _ctx_1024t = jnp.einsum('bsk,bkd->bsd', _ctx_1024c, _ctx_1024P)
        _ctx_1024t = _ctx_1024t * jax.lax.rsqrt(jnp.mean(jnp.square(_ctx_1024t)) + 1e-12) * 0.953939
        ctx_1024 = -1.39393e-06 + 0.999914 * (_ctx_1024t + 0.3 * jax.random.normal(jax.random.fold_in(_rk, 611), (4, 64, 256), jnp.float32))
        return (x, ctx_1024)
    x, ctx_1024 = _rec_inputs()

    def _L0_xattn_setup():
        import jax, jax.numpy as jnp
        import numpy as np
        D_MODEL = 256
        N_HEADS = 16
        key = jax.random.key(seed)
        ks = jax.random.split(key, 11)
        B, L, S, D = (2, 512, 512, D_MODEL)
        s = 1.0 / np.sqrt(D)
        return {'Q': jax.random.normal(ks[0], (B, L, D), jnp.float32), 'K': jax.random.normal(ks[1], (B, S, D), jnp.float32), 'V': jax.random.normal(ks[2], (B, S, D), jnp.float32), 'Wq': jax.random.normal(ks[3], (D, D), jnp.float32) * s, 'bq': jnp.zeros((D,), jnp.float32), 'Wk': jax.random.normal(ks[4], (D, D), jnp.float32) * s, 'bk': jnp.zeros((D,), jnp.float32), 'Wv': jax.random.normal(ks[5], (D, D), jnp.float32) * s, 'bv': jnp.zeros((D,), jnp.float32), 'We': jax.random.normal(ks[6], (D, D), jnp.float32) * s, 'be': jnp.zeros((D,), jnp.float32)}
    _L0_xattn_all = _L0_xattn_setup()
    _L0_xattn_in = {k: v for k, v in _L0_xattn_all.items() if k in ('Wq', 'bq', 'Wk', 'bk', 'Wv', 'bv', 'We', 'be')}
    del _L0_xattn_all

    def _L0_ffn_setup():
        import jax, jax.numpy as jnp
        import numpy as np
        D_MODEL = 256
        N_EXPERTS = 8
        TOP_K = 2
        key = jax.random.key(seed)
        k1, k2, k3, k4 = jax.random.split(key, 4)
        B, S, D, E = (4, 512, D_MODEL, N_EXPERTS)
        dff = 4 * D
        lim = float(np.sqrt(6.0 / (D + dff)))
        return {'x': jax.random.normal(k1, (B, S, D), dtype=jnp.float32), 'router_w': jax.random.normal(k2, (D, E), dtype=jnp.float32) * (1.0 / np.sqrt(D)), 'router_b': jnp.zeros((E,), dtype=jnp.float32), 'expert_up': jax.random.uniform(k3, (E, dff, D), dtype=jnp.float32, minval=-lim, maxval=lim), 'expert_down': jax.random.uniform(k4, (E, D, dff), dtype=jnp.float32, minval=-lim, maxval=lim)}
    _L0_ffn_all = _L0_ffn_setup()
    _L0_ffn_in = {k: v for k, v in _L0_ffn_all.items() if k in ('router_w', 'router_b', 'expert_up', 'expert_down')}
    del _L0_ffn_all
    return {'x': x, 'ctx_1024': ctx_1024, 'L0_xattn_Wq': _L0_xattn_in['Wq'], 'L0_xattn_bq': _L0_xattn_in['bq'], 'L0_xattn_Wk': _L0_xattn_in['Wk'], 'L0_xattn_bk': _L0_xattn_in['bk'], 'L0_xattn_Wv': _L0_xattn_in['Wv'], 'L0_xattn_bv': _L0_xattn_in['bv'], 'L0_xattn_We': _L0_xattn_in['We'], 'L0_xattn_be': _L0_xattn_in['be'], 'L0_ffn_router_w': _L0_ffn_in['router_w'], 'L0_ffn_router_b': _L0_ffn_in['router_b'], 'L0_ffn_expert_up': _L0_ffn_in['expert_up'], 'L0_ffn_expert_down': _L0_ffn_in['expert_down']}

def reference(x, ctx_1024, L0_xattn_Wq, L0_xattn_bq, L0_xattn_Wk, L0_xattn_bk, L0_xattn_Wv, L0_xattn_bv, L0_xattn_We, L0_xattn_be, L0_ffn_router_w, L0_ffn_router_b, L0_ffn_expert_up, L0_ffn_expert_down):
    import jax
    import jax.numpy as jnp

    def _L0_xattn_ref(Q, K, V, Wq, bq, Wk, bk, Wv, bv, We, be):
        import jax, jax.numpy as jnp
        import numpy as np
        D_MODEL = 256
        N_HEADS = 16
        B, L, D = Q.shape
        S = K.shape[1]
        H = N_HEADS
        E = D // H
        q = (Q @ Wq + bq).reshape(B, L, H, E)
        k = (K @ Wk + bk).reshape(B, S, H, E)
        v = (V @ Wv + bv).reshape(B, S, H, E)
        scale = 1.0 / np.sqrt(E)
        scores = jnp.einsum('blhe,bshe->bhls', q, k)
        A = jax.nn.softmax(scale * scores, axis=-1)
        out = jnp.einsum('bhls,bshd->blhd', A, v).reshape(B, L, H * E)
        return out @ We + be

    def _L0_ffn_ref(x, router_w, router_b, expert_up, expert_down):
        import jax, jax.numpy as jnp
        import numpy as np
        D_MODEL = 256
        N_EXPERTS = 8
        TOP_K = 2
        B, S, D = x.shape
        E = expert_up.shape[0]
        x_flat = x.reshape(-1, D)
        logits = x_flat @ router_w + router_b
        probs = jax.nn.softmax(logits, axis=-1)
        top_w, top_idx = jax.lax.top_k(probs, TOP_K)
        comb = jnp.sum(top_w[..., None] * jax.nn.one_hot(top_idx, E, dtype=x.dtype), axis=1)
        output = jnp.zeros_like(x_flat)
        for e in range(E):
            h = jax.nn.gelu(x_flat @ expert_up[e].T, approximate=False)
            out_e = h @ expert_down[e].T
            output = output + comb[:, e:e + 1] * out_e
        return output.reshape(B, S, D)
    x = x + _L0_xattn_ref(_layernorm(x, axis=-1), ctx_1024, ctx_1024, L0_xattn_Wq, L0_xattn_bq, L0_xattn_Wk, L0_xattn_bk, L0_xattn_Wv, L0_xattn_bv, L0_xattn_We, L0_xattn_be)
    x = x + _L0_ffn_ref(_layernorm(x, axis=-1), L0_ffn_router_w, L0_ffn_router_b, L0_ffn_expert_up, L0_ffn_expert_down)
    return x

_drawn_inputs = setup_inputs


def setup_inputs(seed=0):
    import zlib

    import numpy as np

    out = dict(_drawn_inputs(seed))
    spreads = {'L0_xattn_bq': (0.0, 0.282),
     'L0_xattn_bk': (0.0, 0.8),
     'L0_xattn_bv': (0.0, 0.1),
     'L0_xattn_be': (0.0, 0.1),
     'L0_ffn_router_b': (0.0, 0.1)}
    factors = {}
    for name, (base, spread) in spreads.items():
        noise = np.random.default_rng([zlib.crc32(name.encode()), seed]).standard_normal(out[name].shape)
        drawn = base * np.exp(spread * noise) if base else spread * noise
        out[name] = jnp.asarray(drawn.astype(out[name].dtype))
    for name, factor in factors.items():
        out[name] = (out[name] * factor).astype(out[name].dtype)
    return out
```

```python
from contextlib import ExitStack

import concourse.bass as bass
from concourse import mybir
from concourse.alu_op_type import AluOpType as ALU

F32 = mybir.dt.float32
F32R = mybir.dt.float32r
BF16 = mybir.dt.bfloat16
I32 = mybir.dt.int32
U32 = mybir.dt.uint32
ACT = mybir.ActivationFunctionType
AX_X = mybir.AxisListType.X

P = 128
B, L, D = 4, 512, 256
S, H, HE = 64, 16, 16
NE, FF, TOPK = 8, 1024, 2
T = B * L
LT = L // P
NTOK = T // P
KD = D // P
KF = FF // P
MINT = 2
NT = T * TOPK // P + MINT * NE
NTAB = NT + 3
EPS = 1e-5
SCALE = HE ** -0.5
XROW = D + NE
COLS = NTOK
MAPC = NE * COLS + 32

_at = 0
CONST = {}
for _name, _n in (("ident", P), ("iota", P), ("upper", P), ("ones", P), ("head", 8), ("sel", 8 * P),
                  ("feat", KD * P), ("densel", 2 * 32), ("tile", NTAB), ("step", COLS - 1),
                  ("flip", NE), ("token", NTOK), ("spare", 1), ("power", 16), ("expert", NE)):
    CONST[_name] = (_at, _at + _n)
    _at += _n
NCONST = _at


def constants():
    import numpy as np

    c = np.zeros((P, NCONST), np.float32)
    p = np.arange(P)

    def part(name):
        a, b = CONST[name]
        return c[:, a:b]

    part("ident")[:] = np.eye(P)
    part("iota")[:] = np.arange(P)
    part("upper")[:] = p[:, None] < p[None, :]
    part("ones")[:] = 1
    part("head")[:] = p[:, None] // HE == np.arange(8)
    sel = part("sel").reshape(P, 8, P)
    feat = part("feat").reshape(P, KD, P)
    for r in range(32):
        for j in range(8):
            sel[r, j] = (r % H) == 2 * j + p // S
        for k in range(KD):
            feat[r, k] = (r % H) == 8 * k + p // HE
    for k in range(2):
        for h in range(2):
            part("densel").reshape(P, 2, 32)[h * S:(h + 1) * S, k, 2 * k + h] = 1
    part("tile")[:] = np.arange(NTAB)
    part("step")[:] = P * np.arange(1, COLS)
    part("flip")[:] = [0] + [1 if e % 2 else -1 for e in range(1, NE)]
    part("token")[:] = P * np.arange(NTOK) + p[:, None] - T
    part("spare")[:] = T + p[:, None]
    part("power")[:] = -0.5
    part("expert")[:] = np.arange(NE)
    return c


def build(nc, x, ctx_t, ctx_t2, wq, wk, wv, we, bqkv, be, router_w, router_b, up, down, const, out, rows):
    with ExitStack() as ctx:
        def sb(name, shape, dt=F32):
            return ctx.enter_context(nc.sbuf_tensor(name, shape, dt))

        def ps(name, shape, dt=F32):
            return ctx.enter_context(nc.psum_tensor(name, shape, dt))

        def sem(name):
            return ctx.enter_context(nc.semaphore(name))

        cst = sb("cst", [P, NCONST])

        def c(name):
            a, b = CONST[name]
            return cst[:, a:b]

        sel_r = sb("sel_r", [P, 8, P], F32R)
        feat_r = sb("feat_r", [P, KD, P], F32R)
        zero_r = sb("zero_r", [P, P], F32R)
        upper_bf = sb("upper_bf", [P, P], BF16)
        ones_bf = sb("ones_bf", [P, P], BF16)
        wq_h, wq_l = sb("wq_h", [P, KD, D], F32R), sb("wq_l", [P, KD, D], F32R)
        we_h, we_l = sb("we_h", [P, KD, D], F32R), sb("we_l", [P, KD, D], F32R)
        rw = sb("rw", [P, KD, NE])
        rb = sb("rb", [P, NE])
        be_b = sb("be_b", [P, D])
        bias = sb("bias", [P, 3, KD])
        ctxT = sb("ctxT", [P, KD, B * S])
        ctxT2 = sb("ctxT2", [P, KD, B, 2 * S])
        kT_h, kT_l = sb("kT_h", [P, KD, B * S]), sb("kT_l", [P, KD, B * S])
        v_all = sb("v_all", [P, B, D])
        xall = sb("xall", [P, NTOK, D])
        stat1 = sb("stat1", [P, NTOK, 6])
        mv1 = sb("mv1", [P, NTOK, 2])
        var1 = sb("var1", [P, NTOK])
        rstd1 = sb("rstd1", [P, NTOK])
        xn = sb("xn", [P, LT, D])
        xnT_h, xnT_l = sb("xnT_h", [P, KD, L], F32R), sb("xnT_l", [P, KD, L], F32R)
        q_h, q_l = sb("q_h", [P, KD, L], F32R), sb("q_l", [P, KD, L], F32R)
        kbd_h, kbd_l = sb("kbd_h", [P, KD, 8, S], F32R), sb("kbd_l", [P, KD, 8, S], F32R)
        vbd = sb("vbd", [P, 8, 32])
        nmax = sb("nmax", [P, LT, H])
        nmx = sb("nmx", [P, LT, P])
        nmxT = sb("nmxT", [P, L], F32R)
        prob = sb("prob", [P, 4, L])
        wraw = prob
        av = sb("av", [P, KD, L])
        den = sb("den", [P, L])
        rden = sb("rden", [P, LT, 4, 4])
        rdm = sb("rdm", [P, LT, P])
        rdT = sb("rdT", [P, L], F32R)
        at_h, at_l = sb("at_h", [P, KD, L], F32R), sb("at_l", [P, KD, L], F32R)
        stat2 = sb("stat2", [P, LT, 6])
        mv2 = sb("mv2", [P, LT, 2])
        var2 = sb("var2", [P, LT])
        rstd2 = sb("rstd2", [P, LT])
        xr = sb("xr", [P, LT, XROW])
        x2T = sb("x2T", [P, LT, KD, P])
        lg, lgs, ex, pr = (sb(n, [P, LT, NE]) for n in ("lg", "lgs", "ex", "pr"))
        lmax, lsum, lrec = (sb(n, [P, LT]) for n in ("lmax", "lsum", "lrec"))
        v8 = sb("v8", [P, LT, 8])
        i8 = sb("i8", [P, LT, 8], U32)
        ef = sb("ef", [P, TOPK, LT])
        mk = sb("mk", [P, TOPK, LT, NE])
        msum = sb("msum", [P, LT, NE])
        msum_bf = sb("msum_bf", [P, LT, NE], BF16)
        seen = sb("seen", [P, LT + 1, NE])
        seen_bf = sb("seen_bf", [P, LT, NE], BF16)
        pk = sb("pk", [P, TOPK, LT, NE])
        rank = sb("rank", [P, TOPK * LT])
        cmp = sb("cmp", [P, TOPK * LT, COLS - 1])
        ltile, lrow, key, val = (sb(n, [P, TOPK * LT]) for n in ("ltile", "lrow", "key", "val"))
        hot = sb("hot", [P, 4, P], F32R)
        put = sb("put", [P, 4, P], F32R)
        slot_f = sb("slot_f", [P, NE * COLS])
        slot = sb("slot", [P, MAPC], I32)
        ntile, tend, tbeg = (sb(n, [P, NE]) for n in ("ntile", "tend", "tbeg"))
        big = sb("big", [P, NE, COLS - 1])
        on = sb("on", [1, NTAB, NE])
        onx = sb("onx", [1, NTAB, NE])
        te, tb, tcol, tpar, tone, tsp = (sb(n, [1, NTAB]) for n in ("te", "tb", "tcol", "tpar", "tone", "tsp"))
        te_i, tcol_i, tpar_i, tsp_i, traw_i = (sb(n, [1, NTAB], I32)
                                                for n in ("te_i", "tcol_i", "tpar_i", "tsp_i", "traw_i"))
        raw01 = sb("raw01", [P, 2, 1024])
        up_w = sb("up_w", [P, 2, 2, KD, FF], F32R)
        dn_w = sb("dn_w", [P, 2, KF, 2, D], F32R)
        idx_g = sb("idx_g", [P, 1], I32)
        idx_s = sb("idx_s", [P, 1], I32)
        gate = sb("gate", [P, NTAB])
        nt_i = sb("nt_i", [1, 2], I32)
        prime = sb("prime", [P, 14])
        raw = xall[:, :, :].rearrange("p t d -> p (t d)")
        hbuf = raw01[:, 0, :]
        y = x2T[:, 0, :, :].rearrange("p k l -> p (k l)")
        osb = x2T[:, 1, :, :].rearrange("p k l -> p (k l)")
        xT_h, xT_l = xnT_h[:, 0, 0:D], xnT_l[:, 0, 0:D]
        hT_h = q_h[:, :, :].rearrange("p k l -> p (k l)")
        hT_l = q_l[:, :, :].rearrange("p k l -> p (k l)")

        bankM = ps("bankM", [P, 512])
        bankA = ps("bankA", [P, 2, 512])
        bankB0 = ps("bankB0", [P, 512])
        bankB1 = ps("bankB1", [P, 512])
        bankC = ps("bankC", [P, 3, 512])
        bankB = [bankB0, bankB1]

        d_const, d_w, d_x0, d_x, d_zero = (sem(n) for n in ("d_const", "d_w", "d_x0", "d_x", "d_zero"))
        d_x1, d_rows = sem("d_x1"), sem("d_rows")
        d_raw01, d_rawu, d_rawd = sem("d_raw01"), sem("d_rawu"), sem("d_rawd")
        d_gather, d_add = sem("d_gather"), sem("d_add")
        names = ("a_const a_wsplit v_wsplit g_zero v_zero p_kv a_k v_k a_v g_kbd g_vbd "
                 "v_stat1 v_var1 g_rstd1 g_res v_xn p_xT a_xT v_xT p_q a_q v_q p_s v_max v_nmh v_nml p_nmT a_nmT "
                 "p_sT a_exp p_av a_av a_den p_denT v_rden v_rdh v_rdl p_rdT a_rdT p_bc v_att a_at v_at "
                 "p_proj v_x1 v_stat2 v_var2 g_rstd2 v_xn2 p_x2T a_x2T p_lg v_lg a_ex v_pr v_top v_mk v_msum v_seen "
                 "v_comb v_mbf p_pos v_pos v_key v_hot p_map a_w01 g_w01 "
                 "p_fin v_tab v_slot v_done "
                 "g_gi g_si p_fxT a_fxT v_fxT v_gate p_fhT a_fhT v_fhT p_up a_gelu p_dn a_osb v_y a_whi v_wlo").split()
        s = {n: sem(n) for n in names}

        block = ctx.enter_context(nc.Block())

        def w(eng, name, value):
            eng.wait_ge(s[name], value)

        @block.sync
        def _(sp):
            x_t = x.rearrange("(t p) d -> p t d", p=P)
            sp.dma_start(xall[:, 0:LT, :], x_t[:, 0:LT, :]).then_inc(d_x0, 16)
            sp.dma_start(cst[:, :], const).then_inc(d_const, 16)
            for n, a in enumerate((wq, wk, wv, we)):
                sp.dma_start(wraw[:, n, :].rearrange("p (k n) -> p k n", k=KD),
                             a.rearrange("(k p) n -> p k n", p=P)).then_inc(d_w, 16)
            sp.dma_start(ctxT[:, :, :], ctx_t.rearrange("(k p) n -> p k n", p=P)).then_inc(d_w, 16)
            sp.dma_start(ctxT2[:, :, :, :].rearrange("p k b s -> p k (b s)"),
                         ctx_t2.rearrange("(k p) n -> p k n", p=P)).then_inc(d_w, 16)
            sp.dma_start(rw[:, :, :], router_w.rearrange("(k p) n -> p k n", p=P)).then_inc(d_w, 16)
            sp.dma_start(bias[:, :, :], bqkv.rearrange("p (j k) -> p j k", k=KD)).then_inc(d_w, 16)
            sp.dma_start(be_b[:, :], be.rearrange("(a n) -> a n", a=1).broadcast_to([P, D])).then_inc(d_w, 16)
            sp.dma_start(rb[:, :], router_b.rearrange("(a n) -> a n", a=1).broadcast_to([P, NE])).then_inc(d_w, 16)
            sp.dma_start(xall[:, LT:NTOK, :], x_t[:, LT:NTOK, :]).then_inc(d_x, 16)
            w(sp, "g_zero", 2)
            zeros = zero_r[:, :].bitcast(F32)
            zeros_d = zeros.rearrange("p (a n) -> p a n", a=1).broadcast_to([P, KD, P])
            sp.dma_start(rows[T:T + P, 0:D].rearrange("p (a n) -> p a n", a=KD), zeros_d).then_inc(d_zero, 16)
            sp.dma_start(rows[T:T + P, D:XROW], zeros[:, 0:NE]).then_inc(d_zero, 16)
            sp.dma_start(out[T:T + P, :].rearrange("p (a n) -> p a n", a=KD), zeros_d).then_inc(d_zero, 16)

            def load01(i):
                if not (isinstance(i, int) and i == 0):
                    w(sp, "g_w01", 2 * i)
                sp.dma_start(raw01[:, 0, :], up[bass.ds(i, 1)].rearrange("a p n -> (a p) n")).then_inc(d_raw01, 16)
                sp.dma_start(raw01[:, 1, :], down[bass.ds(i, 1)].rearrange("a p n -> (a p) n")).then_inc(d_raw01, 16)

            def store(g):
                w(sp, "v_x1", 2 * g + 2)
                sp.dma_start(out[bass.ds(g * L, L), :].rearrange("(t p) d -> p t d", p=P),
                             xall[:, bass.ds(g * LT, LT), :]).then_inc(d_x1, 16)
                w(sp, "v_comb", g + 1)
                sp.dma_start(rows[bass.ds(g * L, L), :].rearrange("(t p) d -> p t d", p=P),
                             xr[:, :, :]).then_inc(d_rows, 16)

            load01(0)
            with sp.Fori(1, B) as i:
                load01(i)
                store(i - 1)
            store(B - 1)
            sp.wait_ge(d_x1, 16 * B)
            for e in range(2, NE):
                if e > 2:
                    w(sp, "v_wlo", 8 + 4 * (e - 2))
                sp.dma_start(raw[:, 0:2048].rearrange("p (h n) -> p h n", h=2), up[2 * e:2 * e + 2].rearrange("h p n -> p h n")).then_inc(d_rawu, 16)
                sp.dma_start(raw[:, 2048:4096].rearrange("p (h n) -> p h n", h=2), down[2 * e:2 * e + 2].rearrange("h p n -> p h n")).then_inc(d_rawd, 16)

        @block.gpsimd
        def _(pool):
            g = nc.gpsimd
            g.memset(prime[:, 3:4], 0.0).then_inc(s["g_zero"], 1)
            g.memset(zero_r[:, :].bitcast(F32), 0.0).then_inc(s["g_zero"], 1)
            g.memset(nmx[:, :, :], 0.0).then_inc(s["g_zero"], 1)
            g.memset(rdm[:, :, :], 0.0).then_inc(s["g_zero"], 1)

            def rstd(name, out_, var_, n):
                g.tensor_tensor(out_, var_, c("power")[:, 0:n], ALU.pow).then_inc(s[name], 1)

            def key_blocks(b):
                w(pool, "a_k", 2)
                w(pool, "v_k", 2)
                if not (isinstance(b, int) and b == 0):
                    w(pool, "p_sT", 8 * b)
                for part, src in ((kbd_h, kT_h), (kbd_l, kT_l)):
                    for k in range(KD):
                        cols = src[:, k, bass.ds(b * S, S)].rearrange("p (a s) -> p a s", a=1)
                        g.tensor_tensor(part[:, k, :, :], cols.broadcast_to([P, 8, S]),
                                        c("head").rearrange("p (h a) -> p h a", a=1).broadcast_to([P, 8, S]),
                                        ALU.mult).then_inc(s["g_kbd"], 1)

            def value_blocks(b):
                w(pool, "a_v", 2)
                if not (isinstance(b, int) and b == 0):
                    w(pool, "p_av", 16 * b)
                g.tensor_tensor(vbd[:, :, :].rearrange("p j (h e) -> p j h e", h=2),
                                v_all[:, bass.ds(b, 1), :].rearrange("p a (j h e) -> p (a j) h e", h=2, e=HE),
                                c("densel")[:, 0:2].rearrange("p (a h b) -> p a h b", a=1, b=1)
                                .broadcast_to([P, 8, 2, HE]), ALU.mult).then_inc(s["g_vbd"], 1)

            def low01(i):
                pool.wait_ge(d_raw01, 32 * (i + 1))
                w(pool, "a_w01", 2 * (i + 1))
                g.tensor_tensor(up_flat[:, 1, bass.ds(i, 1), :], raw01[:, 0:1, :],
                                up_flat[:, 0, bass.ds(i, 1), :].bitcast(F32), ALU.subtract).then_inc(s["g_w01"], 1)
                g.tensor_tensor(dn_flat[:, bass.ds(4 * i, 4), 1, :],
                                raw01[:, 1, :].rearrange("p (c n) -> p c n", c=4),
                                dn_flat[:, bass.ds(4 * i, 4), 0, :].bitcast(F32), ALU.subtract).then_inc(s["g_w01"], 1)

            up_flat = up_w[:, :, :, :, :].rearrange("p h b k n -> p h (b k) n")
            dn_flat = dn_w[:, :, :, :, :].rearrange("p b k h n -> p (b k) h n")

            def residual(b):
                w(pool, "v_xn", LT * (b + 1))
                g.tensor_tensor(xall[:, bass.ds(b * LT, LT), :], xall[:, bass.ds(b * LT, LT), :],
                                be_b[:, :].rearrange("p (a n) -> p a n", a=1).broadcast_to([P, LT, D]),
                                ALU.add).then_inc(s["g_res"], 1)

            pool.wait_ge(d_const, 16)
            w(pool, "v_var1", 1)
            rstd("g_rstd1", rstd1[:, 0:LT], var1[:, 0:LT], LT)
            w(pool, "g_zero", 4)
            pool.wait_ge(d_w, 160)
            key_blocks(0)
            w(pool, "v_var1", 2)
            rstd("g_rstd1", rstd1[:, LT:NTOK], var1[:, LT:NTOK], NTOK - LT)
            value_blocks(0)
            residual(0)
            low01(0)
            with pool.Fori(1, B) as i:
                key_blocks(i)
                residual(i)
                w(pool, "v_var2", i)
                rstd("g_rstd2", rstd2[:, :], var2[:, :], LT)
                value_blocks(i)
                low01(i)
            w(pool, "v_var2", B)
            rstd("g_rstd2", rstd2[:, :], var2[:, :], LT)

            w(pool, "v_tab", 1)
            w(pool, "v_slot", 2)
            pool.wait_ge(d_rows, 16 * B)
            pool.wait_ge(d_zero, 48)
            pool.wait_ge(d_x1, 16 * B)

            def settle():
                g.tensor_tensor(prime[0:1, 2:3], prime[0:1, 3:4], prime[0:1, 3:4], ALU.add)

            def gather(t, ring, first=False):
                col = pool.value_load(tcol_i[0:1, bass.ds(t, 1)], min_val=0, max_val=MAPC - 1)
                if not first:
                    pool.wait_ge(d_gather, 16 * t)
                g.tensor_copy(idx_g[:, :], slot[:, bass.ds(col, 1)]).then_inc(s["g_gi"], 1)
                w(pool, "g_gi", t + 1)
                if not (isinstance(t, int) and t < 2):
                    w(pool, "p_fxT", t - 1)
                    w(pool, "v_gate", t - 1)
                settle()
                g.indirect_dma_start(xr[:, ring, :], None, rows, bass.IndirectOffsetOnAxis(idx_g[:, 0:1], 0),
                                     bounds_check=T + P - 1).then_inc(d_gather, 16)

            def add(t):
                col = pool.value_load(tcol_i[0:1, bass.ds(t, 1)], min_val=0, max_val=MAPC - 1)
                if not (isinstance(t, int) and t == 0):
                    pool.wait_ge(d_add, 16 * t)
                g.tensor_copy(idx_s[:, :], slot[:, bass.ds(col, 1)]).then_inc(s["g_si"], 1)
                w(pool, "g_si", t + 1)
                w(pool, "v_y", t + 1)
                settle()
                g.indirect_dma_start(out, bass.IndirectOffsetOnAxis(idx_s[:, 0:1], 0), y, None,
                                     bounds_check=T + P - 1, compute_op=ALU.add).then_inc(d_add, 16)

            nt = pool.value_load(nt_i[0:1, 0:1], min_val=MINT * NE, max_val=NT)
            gather(0, 0, first=True)
            gather(1, 1)
            gather(2, 0)
            with pool.Fori(1, NT, 2) as u:
                for r in range(2):
                    t = u + r
                    with pool.If(nt > t):
                        gather(t + 2, 1 - r)
                        add(t - 1)
            last = pool.value_load(nt_i[0:1, 1:2], min_val=MINT * NE - 1, max_val=NT - 1)
            add(last)
            pool.wait_ge(d_gather, 16 * (last + 3))
            pool.wait_ge(d_add, 16 * (last + 1))

        @block.scalar
        def _(act):
            a = nc.scalar

            def copy(out_, in_, name, **kw):
                a.activation(out_, in_, ACT.Identity, **kw).then_inc(s[name], 1)

            act.wait_ge(d_const, 16)
            copy(sel_r[:, :, :], c("sel").rearrange("p (j n) -> p j n", j=8), "a_const")
            copy(feat_r[:, :, :], c("feat").rearrange("p (j n) -> p j n", j=KD), "a_const")
            copy(upper_bf[:, :], c("upper"), "a_const")
            copy(ones_bf[:, :], c("ones"), "a_const")
            act.wait_ge(d_w, 160)
            copy(wq_h[:, :, :], wraw[:, 0, :].rearrange("p (k n) -> p k n", k=KD), "a_wsplit")
            copy(we_h[:, :, :], wraw[:, 3, :].rearrange("p (k n) -> p k n", k=KD), "a_wsplit")

            def keys():
                for k in range(KD):
                    w(act, "p_kv", k + 1)
                    copy(kT_h[:, k, :].bitcast(F32R), bankC[:, k, 0:B * S], "a_k", bias=bias[:, 1, k:k + 1])

            def values():
                for n in range(2):
                    w(act, "p_kv", 3 + n)
                    copy(v_all[:, 2 * n:2 * n + 2, :].rearrange("p b d -> p (b d)"), bankB[n][:, :], "a_v")

            def x_high(b):
                for n in range(2):
                    w(act, "p_xT", 2 * b + n + 1)
                    copy(xnT_h[:, :, n * 256:(n + 1) * 256].rearrange("p k (t l) -> p t k l", t=2),
                         bankA[:, n, :].rearrange("p (t k l) -> p t k l", t=2, k=KD), "a_xT")

            def q_high(b):
                for k in range(KD):
                    w(act, "p_q", KD * b + k + 1)
                    copy(q_h[:, k, :], bankB[k][:, :], "a_q", bias=bias[:, 0, k:k + 1])

            def max_turn(b):
                w(act, "p_nmT", b + 1)
                copy(nmxT[:, :], bankC[:, 2, :], "a_nmT")

            def exps(b, js):
                for j in js:
                    w(act, "p_sT", 8 * b + j + 1)
                    if j >= 4:
                        w(act, "p_av", 16 * b + 2 * (j - 3))
                    elif not (isinstance(b, int) and b == 0):
                        w(act, "p_av", 16 * b)
                    a.activation(prob[:, j % 4, :], bankC[:, j % 3, :], ACT.Exp, scale=SCALE).then_inc(s["a_exp"], 1)

            def den_copy(b):
                w(act, "p_av", 16 * b + 16)
                copy(den[:, :], bankB0[:, :], "a_den")

            def av_copy(b):
                for k in range(KD):
                    w(act, "p_av", 16 * b + 8 * k + 8)
                    copy(av[:, k, :], bankA[:, k, :], "a_av")

            def rden_turn(b):
                w(act, "p_rdT", b + 1)
                copy(rdT[:, :], bankB0[:, :], "a_rdT")

            def att_high(b):
                for k in range(KD):
                    w(act, "v_att", KD * b + k + 1)
                    copy(at_h[:, k, :], av[:, k, :], "a_at", bias=bias[:, 2, k:k + 1])

            def x2_turn(b):
                for n in range(2):
                    w(act, "p_x2T", 2 * b + n + 1)
                    copy(x2T[:, 2 * n:2 * n + 2, :, :].rearrange("p t k l -> p (t k l)"), bankA[:, n, :], "a_x2T")

            def router_exp(b):
                w(act, "v_lg", 3 * b + 3)
                a.activation(ex[:, :, :], lgs[:, :, :], ACT.Exp).then_inc(s["a_ex"], 1)

            def high01(i):
                act.wait_ge(d_raw01, 32 * (i + 1))
                copy(up_flat[:, 0, bass.ds(i, 1), :], raw01[:, 0:1, :], "a_w01")
                copy(dn_flat[:, bass.ds(4 * i, 4), 0, :], raw01[:, 1, :].rearrange("p (c n) -> p c n", c=4), "a_w01")

            up_flat = up_w[:, :, :, :, :].rearrange("p h b k n -> p h (b k) n")
            dn_flat = dn_w[:, :, :, :, :].rearrange("p b k h n -> p (b k) h n")

            keys()
            values()
            x_high(0)
            q_high(0)
            w(act, "v_wsplit", 2)
            w(act, "p_kv", 4)
            high01(0)
            max_turn(0)
            exps(0, range(4))

            with act.Fori(1, B) as i:
                exps(i - 1, range(4, 8))
                av_copy(i - 1)
                den_copy(i - 1)
                x_high(i)
                q_high(i)
                rden_turn(i - 1)
                att_high(i - 1)
                high01(i)
                max_turn(i)
                exps(i, range(4))
                x2_turn(i - 1)
                router_exp(i - 1)
            exps(B - 1, range(4, 8))
            den_copy(B - 1)
            av_copy(B - 1)
            rden_turn(B - 1)
            att_high(B - 1)
            x2_turn(B - 1)
            router_exp(B - 1)

            w(act, "v_tab", 1)
            a.activation(prime[:, 0:1], c("ones")[:, 0:1], ACT.Identity).then_inc(s["a_whi"], 8)

            nt = act.value_load(nt_i[0:1, 0:1], min_val=MINT * NE, max_val=NT)

            def x_high_f(t):
                w(act, "p_fxT", t + 1)
                copy(xT_h, bankA[:, 0, 0:D], "a_fxT")

            def h_high(t):
                for n in range(2):
                    w(act, "p_fhT", 2 * t + n + 1)
                    copy(hT_h[:, n * 512:(n + 1) * 512], bankB[n][:, :], "a_fhT")

            def gelu(t, n):
                w(act, "p_up", 2 * t + n + 1)
                a.activation(hbuf[:, n * 512:(n + 1) * 512], bankC[:, n, :], ACT.Gelu).then_inc(s["a_gelu"], 1)

            def low_part(t):
                w(act, "p_dn", t + 1)
                w(act, "v_gate", t + 1)
                copy(osb, bankC[:, 2, D:2 * D], "a_osb", scale=gate[:, bass.ds(t, 1)])

            def weights_high(t, half):
                sp_e = act.value_load(tsp_i[0:1, bass.ds(t, 1)], min_val=0, max_val=NE - 1)
                with act.If(sp_e > 1):
                    nraw = act.value_load(traw_i[0:1, bass.ds(t, 1)], min_val=1, max_val=NE - 2)
                    par = act.value_load(tpar_i[0:1, bass.ds(t, 1)], min_val=0, max_val=1)
                    other = 1 - par
                    act.wait_ge(d_rawd if half else d_rawu, 16 * nraw)
                    for n in range(2):
                        if half:
                            copy(dn_w[:, bass.ds(other, 1), 4 * n:4 * n + 4, 0, :].rearrange("p a c n -> p (a c) n"),
                                 raw[:, 2048 + n * 1024:2048 + (n + 1) * 1024].rearrange("p (c n) -> p c n", c=4),
                                 "a_whi")
                        else:
                            copy(up_w[:, 0, bass.ds(other, 1), n, :], raw[:, n * FF:(n + 1) * FF], "a_whi")

            x_high_f(0)
            gelu(0, 0)
            x_high_f(1)
            gelu(0, 1)
            h_high(0)
            with act.Fori(1, NT, 2) as u:
                for r in range(2):
                    t = u + r
                    with act.If(nt > t):
                        gelu(t, 0)
                        x_high_f(t + 1)
                        gelu(t, 1)
                        weights_high(t, 0)
                        low_part(t - 1)
                        h_high(t)
                        weights_high(t, 1)
            last = act.value_load(nt_i[0:1, 1:2], min_val=MINT * NE - 1, max_val=NT - 1)
            low_part(last)

        @block.vector
        def _(dve):
            v = nc.vector

            def inc(ins, name):
                ins.then_inc(s[name], 1)

            inc(v.memset(seen[:, 0, :], 0.0), "v_zero")

            def settle(n):
                v.memset(prime[:, n:n + 1], 0.0)

            def stats1(t0, n, tiles_per):
                for k in range(n):
                    inc(v.bn_stats(stat1[:, t0 + k, :], xall[:, t0 + k, :]), "v_stat1")

            def aggr1(t0, n, base):
                for k in range(n):
                    w(dve, "v_stat1", base + k + 1)
                    inc(v.bn_aggr(mv1[:, t0 + k, :], stat1[:, t0 + k, :]), "v_stat1")
                w(dve, "v_stat1", base + 2 * n)
                inc(v.tensor_scalar(var1[:, t0:t0 + n], mv1[:, t0:t0 + n, 1], EPS, None, ALU.add), "v_var1")

            def norm1(b):
                if isinstance(b, int) and b == 0:
                    w(dve, "g_rstd1", 1)
                else:
                    w(dve, "g_rstd1", 2)
                    w(dve, "p_xT", 2 * b)
                for k in range(LT):
                    tt = b * LT + k
                    inc(v.tensor_scalar(xn[:, k, :], xall[:, bass.ds(tt, 1), :].rearrange("p a d -> p (a d)"),
                                        mv1[:, bass.ds(tt, 1), 0], rstd1[:, bass.ds(tt, 1)],
                                        ALU.subtract, ALU.mult), "v_xn")

            def x_low(b):
                for n in range(2):
                    w(dve, "a_xT", 2 * b + n + 1)
                    o = slice(n * 256, (n + 1) * 256)
                    inc(v.tensor_tensor(xnT_l[:, :, o].rearrange("p k (t l) -> p t k l", t=2),
                                        bankA[:, n, :].rearrange("p (t k l) -> p t k l", t=2, k=KD),
                                        xnT_h[:, :, o].bitcast(F32).rearrange("p k (t l) -> p t k l", t=2),
                                        ALU.subtract), "v_xT")

            def q_low(b):
                for k in range(KD):
                    w(dve, "a_q", KD * b + k + 1)
                    inc(v.scalar_tensor_tensor(out=q_l[:, k, :], in0=bankB[k][:, :], scalar=bias[:, 0, k:k + 1],
                                               in1=q_h[:, k, :].bitcast(F32), op0=ALU.add, op1=ALU.subtract), "v_q")

            def maxima(b, t):
                for k in range(KD):
                    n = KD * t + k
                    w(dve, "p_s", 8 * b + n + 1)
                    inc(v.tensor_reduce(nmax[:, t, 8 * k:8 * k + 8],
                                        bankC[:, n % 3, :].rearrange("p (h s) -> p h s", h=8), AX_X, ALU.max,
                                        negate=True), "v_max")

            def max_split(b):
                w(dve, "v_max", 8 * b + 8)
                inc(v.tensor_copy(nmx[:, :, 0:H].bitcast(F32R), nmax[:, :, :]), "v_nmh")
                w(dve, "v_nmh", b + 1)
                inc(v.tensor_tensor(nmx[:, :, H:2 * H].bitcast(F32R), nmax[:, :, :], nmx[:, :, 0:H], ALU.subtract), "v_nml")

            def rden_split(b):
                w(dve, "p_denT", b + 1)
                dv = bankB1[:, :].rearrange("p (t i r) -> p t i r", t=LT, i=4)[:, :, :, 0:4]
                inc(v.reciprocal(rden[:, :, :, :], dv), "v_rden")
                w(dve, "v_rden", b + 1)
                for k in range(KD):
                    src = rden[:, :, :, 2 * k:2 * k + 2]
                    hi = rdm[:, :, 8 * k:8 * k + 8].rearrange("p t (i h) -> p t i h", h=2)
                    lo = rdm[:, :, H + 8 * k:H + 8 * k + 8].rearrange("p t (i h) -> p t i h", h=2)
                    inc(v.tensor_copy(hi.bitcast(F32R), src), "v_rdh")
                    w(dve, "v_rdh", KD * b + k + 1)
                    inc(v.tensor_tensor(lo.bitcast(F32R), src, hi, ALU.subtract), "v_rdl")

            def att(b):
                for k in range(KD):
                    w(dve, "a_av", KD * b + k + 1)
                    w(dve, "p_bc", KD * b + k + 1)
                    inc(v.tensor_tensor(av[:, k, :], bankA[:, k, :], av[:, k, :], ALU.mult), "v_att")

            def att_low(b):
                for k in range(KD):
                    w(dve, "a_at", KD * b + k + 1)
                    inc(v.scalar_tensor_tensor(out=at_l[:, k, :], in0=av[:, k, :], scalar=bias[:, 2, k:k + 1],
                                               in1=at_h[:, k, :].bitcast(F32), op0=ALU.add, op1=ALU.subtract), "v_at")

            def residual(b):
                w(dve, "g_res", b + 1)
                for n in range(2):
                    w(dve, "p_proj", 2 * b + n + 1)
                    xs = xall[:, bass.ds(b * LT + 2 * n, 2), :]
                    inc(v.tensor_tensor(xs, bankB[n][:, :].rearrange("p (t d) -> p t d", t=2), xs, ALU.add), "v_x1")

            def norm2(b):
                w(dve, "v_x1", 2 * b + 2)
                settle(5)
                for k in range(LT):
                    inc(v.bn_stats(stat2[:, k, :], xall[:, bass.ds(b * LT + k, 1), :].rearrange("p a d -> p (a d)")), "v_stat2")
                w(dve, "v_stat2", 8 * b + LT)
                settle(6)
                for k in range(LT):
                    inc(v.bn_aggr(mv2[:, k, :], stat2[:, k, :]), "v_stat2")
                w(dve, "v_stat2", 8 * b + 8)
                inc(v.tensor_scalar(var2[:, :], mv2[:, :, 1], EPS, None, ALU.add), "v_var2")
                w(dve, "g_rstd2", b + 1)
                if not (isinstance(b, int) and b == 0):
                    dve.wait_ge(d_rows, 16 * b)
                for k in range(LT):
                    inc(v.tensor_scalar(xr[:, k, 0:D], xall[:, bass.ds(b * LT + k, 1), :].rearrange("p a d -> p (a d)"),
                                        mv2[:, k, 0:1], rstd2[:, k:k + 1], ALU.subtract, ALU.mult), "v_xn2")

            def bc3(ap, n):
                return ap.rearrange("p (q a) -> p q a", a=1).broadcast_to([P, ap.shape[1], n])

            def router(b):
                w(dve, "p_lg", b + 1)
                inc(v.tensor_tensor(lg[:, :, :], bankB0[:, 0:LT * NE].rearrange("p (t e) -> p t e", t=LT),
                                    rb[:, :].rearrange("p (a e) -> p a e", a=1).broadcast_to([P, LT, NE]), ALU.add), "v_lg")
                w(dve, "v_lg", 3 * b + 1)
                inc(v.tensor_reduce(lmax[:, :], lg[:, :, :], AX_X, ALU.max, negate=True), "v_lg")
                w(dve, "v_lg", 3 * b + 2)
                inc(v.tensor_tensor(lgs[:, :, :], lg[:, :, :], bc3(lmax[:, :], NE), ALU.add), "v_lg")
                w(dve, "a_ex", b + 1)
                inc(v.tensor_reduce(lsum[:, :], ex[:, :, :], AX_X, ALU.add), "v_pr")
                w(dve, "v_pr", 3 * b + 1)
                inc(v.reciprocal(lrec[:, :], lsum[:, :]), "v_pr")
                w(dve, "v_pr", 3 * b + 2)
                inc(v.tensor_tensor(pr[:, :, :], ex[:, :, :], bc3(lrec[:, :], NE), ALU.mult), "v_pr")
                w(dve, "v_pr", 3 * b + 3)
                settle(7)
                for t in range(LT):
                    inc(v.max(out=v8[:, t, :], in_=pr[:, t, :]), "v_top")
                w(dve, "v_top", 8 * b + LT)
                settle(8)
                for t in range(LT):
                    inc(v.max_index(i8[:, t, :], v8[:, t, :], pr[:, t, :]), "v_top")
                w(dve, "v_top", 8 * b + 8)
                inc(v.tensor_copy(ef[:, :, :], i8[:, :, 0:TOPK].rearrange("p t k -> p k t")), "v_mk")
                w(dve, "v_mk", 2 * b + 1)
                inc(v.tensor_tensor(mk[:, :, :, :].rearrange("p k t e -> p (k t) e"),
                                    c("expert").rearrange("p (a e) -> p a e", a=1).broadcast_to([P, TOPK * LT, NE]),
                                    bc3(ef[:, :, :].rearrange("p k t -> p (k t)"), NE), ALU.is_equal), "v_mk")
                w(dve, "v_mk", 2 * b + 2)
                inc(v.tensor_tensor(msum[:, :, :], mk[:, 0, :, :], mk[:, 1, :, :], ALU.add), "v_msum")
                w(dve, "v_msum", b + 1)
                inc(v.tensor_copy(msum_bf[:, :, :], msum[:, :, :]), "v_mbf")
                for t in range(LT):
                    inc(v.tensor_tensor(seen[:, t + 1, :], seen[:, t, :], msum[:, t, :], ALU.add), "v_seen")
                    w(dve, "v_seen", 5 * b + t + 1)
                inc(v.tensor_copy(seen_bf[:, :, :], seen[:, 0:LT, :]), "v_mbf")
                w(dve, "v_mbf", 2 * b + 2)
                inc(v.tensor_copy(seen[:, 0, :], seen[:, LT, :]), "v_seen")
                w(dve, "v_seen", 5 * b + 5)
                inc(v.tensor_tensor(xr[:, :, D:XROW], pr[:, :, :], msum[:, :, :], ALU.mult), "v_comb")

            def ranks(b):
                w(dve, "p_pos", b + 1)
                inc(v.tensor_tensor(pk[:, :, :, :], mk[:, :, :, :],
                                    bankB1[:, 0:LT * NE].rearrange("p (a t e) -> p a t e", a=1, t=LT)
                                    .broadcast_to([P, TOPK, LT, NE]), ALU.mult), "v_pos")
                w(dve, "v_pos", 4 * b + 1)
                inc(v.tensor_reduce(rank[:, :], pk[:, :, :, :].rearrange("p k t e -> p (k t) e"), AX_X, ALU.add), "v_pos")
                w(dve, "v_pos", 4 * b + 2)
                inc(v.tensor_tensor(cmp[:, :, :], bc3(rank[:, :], COLS - 1),
                                    c("step").rearrange("p (a n) -> p a n", a=1).broadcast_to([P, TOPK * LT, COLS - 1]),
                                    ALU.is_ge), "v_pos")
                w(dve, "v_pos", 4 * b + 3)
                inc(v.tensor_reduce(ltile[:, :], cmp[:, :, :], AX_X, ALU.add), "v_pos")
                w(dve, "v_pos", 4 * b + 4)
                inc(v.scalar_tensor_tensor(out=lrow[:, :], in0=ltile[:, :], scalar=-float(P), in1=rank[:, :],
                                           op0=ALU.mult, op1=ALU.add), "v_key")
                inc(v.scalar_tensor_tensor(out=key[:, :], in0=ef[:, :, :].rearrange("p k t -> p (k t)"),
                                           scalar=float(COLS), in1=ltile[:, :], op0=ALU.mult, op1=ALU.add), "v_key")
                w(dve, "v_key", 3 * b + 1)
                a0 = CONST["token"][0]
                tok = cst[:, bass.ds(a0 + b * LT, LT)].rearrange("p (a t) -> p a t", a=1).broadcast_to([P, TOPK, LT])
                inc(v.tensor_tensor(val[:, :].rearrange("p (k t) -> p k t", k=TOPK), tok,
                                    lrow[:, :].rearrange("p (k t) -> p k t", k=TOPK), ALU.subtract), "v_key")
                w(dve, "v_key", 3 * b + 3)
                for q in range(TOPK * LT):
                    if q >= 4:
                        w(dve, "p_map", 8 * b + q - 3)
                    elif not (isinstance(b, int) and b == 0):
                        w(dve, "p_map", 8 * b)
                    inc(v.tensor_scalar(hot[:, q % 4, :], c("iota"), lrow[:, q:q + 1], None, ALU.is_equal), "v_hot")
                    inc(v.tensor_scalar(put[:, q % 4, :], c("iota"), key[:, q:q + 1], val[:, q:q + 1],
                                        ALU.is_equal, ALU.mult), "v_hot")

            dve.wait_ge(d_x0, 16)
            stats1(0, LT, LT)
            aggr1(0, LT, 0)
            dve.wait_ge(d_const, 16)
            norm1(0)
            dve.wait_ge(d_w, 160)
            w(dve, "a_wsplit", 2)
            inc(v.tensor_tensor(wq_l[:, :, :], wraw[:, 0, :].rearrange("p (k n) -> p k n", k=KD),
                                wq_h[:, :, :].bitcast(F32), ALU.subtract), "v_wsplit")
            inc(v.tensor_tensor(we_l[:, :, :], wraw[:, 3, :].rearrange("p (k n) -> p k n", k=KD),
                                we_h[:, :, :].bitcast(F32), ALU.subtract), "v_wsplit")
            for k in range(KD):
                w(dve, "a_k", k + 1)
                inc(v.scalar_tensor_tensor(out=kT_l[:, k, :].bitcast(F32R), in0=bankC[:, k, 0:B * S],
                                           scalar=bias[:, 1, k:k + 1], in1=kT_h[:, k, :],
                                           op0=ALU.add, op1=ALU.subtract), "v_k")
            x_low(0)
            q_low(0)
            dve.wait_ge(d_x, 16)
            stats1(LT, NTOK - LT, LT)
            aggr1(LT, NTOK - LT, 2 * LT)
            w(dve, "g_zero", 4)
            w(dve, "v_zero", 1)
            for t in range(LT):
                maxima(0, t)
            max_split(0)

            with dve.Fori(1, B) as i:
                norm1(i)
                x_low(i)
                q_low(i)
                maxima(i, 0)
                rden_split(i - 1)
                maxima(i, 1)
                maxima(i, 2)
                att(i - 1)
                maxima(i, 3)
                att_low(i - 1)
                max_split(i)
                residual(i - 1)
                norm2(i - 1)
                router(i - 1)
                ranks(i - 1)
            rden_split(B - 1)
            att(B - 1)
            att_low(B - 1)
            residual(B - 1)
            norm2(B - 1)
            router(B - 1)
            ranks(B - 1)

            w(dve, "p_fin", 1)
            inc(v.tensor_tensor(big[:, :, :], bc3(bankB1[:, 64:64 + NE], COLS - 1),
                                c("step").rearrange("p (a n) -> p a n", a=1).broadcast_to([P, NE, COLS - 1]),
                                ALU.is_gt), "v_done")
            w(dve, "v_done", 1)
            inc(v.tensor_reduce(ntile[:, :], big[:, :, :], AX_X, ALU.add), "v_done")
            w(dve, "v_done", 2)
            inc(v.tensor_scalar(ntile[:, :], ntile[:, :], 1.0, float(MINT), ALU.add, ALU.max), "v_done")
            w(dve, "v_done", 3)
            inc(v.tensor_tensor_scan(tend[:, :], c("ones")[:, 0:NE], ntile[:, :], 0.0, ALU.mult, ALU.add), "v_done")
            w(dve, "v_done", 4)
            inc(v.tensor_tensor(tbeg[:, :], tend[:, :], ntile[:, :], ALU.subtract), "v_done")
            w(dve, "v_done", 5)
            tiles = c("tile")[0:1, :].rearrange("p (t a) -> p t a", a=1).broadcast_to([1, NTAB, NE])
            begs = tbeg[0:1, :].rearrange("p (a e) -> p a e", a=1).broadcast_to([1, NTAB, NE])
            inc(v.tensor_tensor(on[:, :, :], tiles, begs, ALU.is_ge), "v_done")
            w(dve, "v_done", 6)
            inc(v.tensor_reduce(te[:, :], on[:, :, :], AX_X, ALU.add), "v_done")
            inc(v.tensor_tensor(onx[:, :, :], on[:, :, :], begs, ALU.mult), "v_done")
            w(dve, "v_done", 8)
            inc(v.tensor_reduce(tb[:, :], onx[:, :, :], AX_X, ALU.max), "v_done")
            w(dve, "v_done", 9)
            flips = c("flip")[0:1, :].rearrange("p (a e) -> p a e", a=1).broadcast_to([1, NTAB, NE])
            inc(v.tensor_tensor(onx[:, :, :], on[:, :, :], flips, ALU.mult), "v_done")
            w(dve, "v_done", 10)
            inc(v.tensor_reduce(tpar[:, :], onx[:, :, :], AX_X, ALU.add), "v_done")
            inc(v.tensor_scalar(te[:, :], te[:, :], -1.0, None, ALU.add), "v_done")
            inc(v.tensor_tensor(tone[:, :], c("tile")[0:1, :], tb[:, :], ALU.subtract), "v_done")
            w(dve, "v_done", 13)
            inc(v.scalar_tensor_tensor(out=tcol[:, :], in0=te[:, :], scalar=float(COLS), in1=tone[:, :],
                                       op0=ALU.mult, op1=ALU.add), "v_done")
            inc(v.tensor_scalar(tone[:, :], tone[:, :], 0.0, None, ALU.is_equal), "v_done")
            inc(v.memset(tsp[:, 0:1], 0.0), "v_done")
            w(dve, "v_done", 15)
            inc(v.scalar_tensor_tensor(out=tsp[:, 1:NTAB], in0=te[:, 0:NTAB - 1], scalar=1.0, in1=tone[:, 0:NTAB - 1],
                                       op0=ALU.add, op1=ALU.mult), "v_done")
            w(dve, "v_done", 17)
            inc(v.tensor_scalar(onx[:, :, 0], tsp[:, :], float(NE) - 0.5, None, ALU.is_lt), "v_done")
            w(dve, "v_done", 18)
            inc(v.tensor_tensor(tsp[:, :], tsp[:, :], onx[:, :, 0], ALU.mult), "v_done")
            w(dve, "v_done", 19)
            inc(v.tensor_copy(nt_i[:, 0:1], tend[0:1, NE - 1:NE]), "v_done")
            inc(v.tensor_scalar(nt_i[:, 1:2], tend[0:1, NE - 1:NE], -1.0, None, ALU.add), "v_done")
            inc(v.tensor_copy(te_i[:, :], te[:, :]), "v_done")
            inc(v.tensor_copy(tcol_i[:, :], tcol[:, :]), "v_done")
            inc(v.tensor_copy(tpar_i[:, :], tpar[:, :]), "v_done")
            inc(v.tensor_scalar(traw_i[:, :], tsp[:, :], -1.0, None, ALU.add), "v_done")
            inc(v.tensor_copy(tsp_i[:, :], tsp[:, :]), "v_tab")
            inc(v.tensor_scalar(slot[:, 0:NE * COLS], bankM[:, 0:NE * COLS], c("spare"), None, ALU.add), "v_slot")
            inc(v.tensor_scalar(slot[:, NE * COLS:MAPC], c("iota")[:, 0:32], 0.0, c("spare"), ALU.mult, ALU.add), "v_slot")

            w(dve, "v_tab", 1)

            nt = dve.value_load(nt_i[0:1, 0:1], min_val=MINT * NE, max_val=NT)

            def x_low_f(t, ring):
                e = dve.value_load(te_i[0:1, bass.ds(t, 1)], min_val=0, max_val=NE - 1)
                dve.wait_ge(d_gather, 16 * (t + 1))
                inc(v.tensor_copy(gate[:, bass.ds(t, 1)], xr[:, ring, bass.ds(D + e, 1)]), "v_gate")
                w(dve, "a_fxT", t + 1)
                inc(v.tensor_tensor(xT_l, bankA[:, 0, 0:D], xT_h.bitcast(F32), ALU.subtract), "v_fxT")

            def h_low(t):
                for n in range(2):
                    w(dve, "a_fhT", 2 * t + n + 1)
                    o = slice(n * 512, (n + 1) * 512)
                    inc(v.tensor_tensor(hT_l[:, o], bankB[n][:, :], hT_h[:, o].bitcast(F32), ALU.subtract), "v_fhT")

            def result(t):
                w(dve, "a_osb", t + 1)
                if not (isinstance(t, int) and t == 0):
                    dve.wait_ge(d_add, 16 * t)
                inc(v.scalar_tensor_tensor(out=y, in0=bankC[:, 2, 0:D], scalar=gate[:, bass.ds(t, 1)],
                                           in1=osb, op0=ALU.mult, op1=ALU.add), "v_y")

            def weights_low(t, half):
                e = dve.value_load(tsp_i[0:1, bass.ds(t, 1)], min_val=0, max_val=NE - 1)
                with dve.If(e > 1):
                    par = dve.value_load(tpar_i[0:1, bass.ds(t, 1)], min_val=0, max_val=1)
                    other = 1 - par
                    for n in range(2):
                        w(dve, "a_whi", 4 * e + 2 * half + n + 1)
                        settle(10 + 2 * half + n)
                        if half:
                            dst = dn_w[:, bass.ds(other, 1), 4 * n:4 * n + 4, :, :].rearrange("p a c h n -> p (a c) h n")
                            inc(v.tensor_tensor(dst[:, :, 1, :],
                                                raw[:, 2048 + n * 1024:2048 + (n + 1) * 1024]
                                                .rearrange("p (c n) -> p c n", c=4),
                                                dst[:, :, 0, :].bitcast(F32), ALU.subtract), "v_wlo")
                        else:
                            inc(v.tensor_tensor(up_w[:, 1, bass.ds(other, 1), n, :].rearrange("p a n -> p (a n)"),
                                                raw[:, n * FF:(n + 1) * FF],
                                                up_w[:, 0, bass.ds(other, 1), n, :].bitcast(F32)
                                                .rearrange("p a n -> p (a n)"), ALU.subtract), "v_wlo")

            w(dve, "g_w01", 8)
            v.memset(prime[:, 1:2], 0.0).then_inc(s["v_wlo"], 8)
            x_low_f(0, 0)
            x_low_f(1, 1)
            h_low(0)
            with dve.Fori(1, NT, 2) as u:
                for r in range(2):
                    t = u + r
                    with dve.If(nt > t):
                        x_low_f(t + 1, r)
                        weights_low(t, 0)
                        result(t - 1)
                        h_low(t)
                        weights_low(t, 1)
            last = dve.value_load(nt_i[0:1, 1:2], min_val=MINT * NE - 1, max_val=NT - 1)
            result(last)

        @block.tensor
        def _(pe):
            mm = nc.tensor.matmul
            ident = c("ident")

            def three(out_, left_h, left_l, right_h, right_l, first, last):
                mm(out_, left_h, right_h, start=first, stop=False)
                mm(out_, left_h, right_l, start=False, stop=False)
                return mm(out_, left_l, right_h, start=False, stop=last)

            pe.wait_ge(d_w, 160)
            for k in range(KD):
                for d in range(KD):
                    last = mm(bankC[:, k, 0:B * S], wraw[:, 1, d * D + k * P:d * D + (k + 1) * P], ctxT[:, d, :],
                              start=(d == 0), stop=(d == KD - 1))
                last.then_inc(s["p_kv"], 1)
            for n in range(2):
                for h in range(2):
                    for d in range(KD):
                        last = mm(bankB[n][:, h * D:(h + 1) * D], ctxT2[:, d, 2 * n + h, :],
                                  wraw[:, 2, d * D:(d + 1) * D], start=(d == 0), stop=(d == KD - 1))
                last.then_inc(s["p_kv"], 1)
            w(pe, "g_zero", 4)
            mm(bankM[:, 0:P], zero_r[:, :], zero_r[:, :], start=True, stop=False, skip_group_check=True)
            pe.wait_ge(d_const, 16)

            def x_turn(b):
                for n in range(2):
                    if not (isinstance(b, int) and b == 0):
                        w(pe, "a_av", KD * (b - 1) + n + 1)
                    for t in range(2):
                        w(pe, "v_xn", LT * b + 2 * n + t + 1)
                        for k in range(KD):
                            o = (t * KD + k) * P
                            last = nc.tensor.transpose(bankA[:, n, o:o + P], xn[:, 2 * n + t, k * P:(k + 1) * P], ident)
                    last.then_inc(s["p_xT"], 1)

            def project_q(b):
                w(pe, "v_xT", 2 * b + 2)
                if isinstance(b, int) and b == 0:
                    w(pe, "v_wsplit", 1)
                    w(pe, "a_v", 2)
                else:
                    w(pe, "a_den", b)
                for k in range(KD):
                    o = slice(k * P, (k + 1) * P)
                    for d in range(KD):
                        last = three(bankB[k][:, :], wq_h[:, d, o], wq_l[:, d, o], xnT_h[:, d, :], xnT_l[:, d, :],
                                     d == 0, d == KD - 1)
                    last.then_inc(s["p_q"], 1)

            def scores(b, t):
                for k in range(KD):
                    n = KD * t + k
                    if n == 0:
                        w(pe, "v_q", KD * b + 2)
                        w(pe, "g_kbd", 4 * b + 4)
                    if n >= 3:
                        w(pe, "v_max", 8 * b + n - 2)
                    o = slice(t * P, (t + 1) * P)
                    three(bankC[:, n % 3, :], q_h[:, k, o], q_l[:, k, o],
                          kbd_h[:, k, :, :].rearrange("p h s -> p (h s)"), kbd_l[:, k, :, :].rearrange("p h s -> p (h s)"),
                          True, True).then_inc(s["p_s"], 1)

            def max_turn(b):
                w(pe, "v_nml", b + 1)
                for t in range(LT):
                    last = nc.tensor.transpose(bankC[:, 2, t * P:(t + 1) * P], nmx[:, t, :], ident)
                last.then_inc(s["p_nmT"], 1)

            def scores_turned(b, js):
                for j in js:
                    k, i = j // 4, j % 4
                    if j == 0:
                        w(pe, "a_nmT", b + 1)
                        w(pe, "a_const", 4)
                    if j >= 3:
                        w(pe, "a_exp", 8 * b + j - 2)
                    kh = kbd_h[:, k, 2 * i:2 * i + 2, :].rearrange("p h s -> p (h s)")
                    kl = kbd_l[:, k, 2 * i:2 * i + 2, :].rearrange("p h s -> p (h s)")
                    three(bankC[:, j % 3, :], kh, kl, q_h[:, k, :], q_l[:, k, :], True, False)
                    mm(bankC[:, j % 3, :], sel_r[:, j, :], nmxT[:, :], start=False, stop=True).then_inc(s["p_sT"], 1)

            def values(b, js):
                for j in js:
                    k, i = j // 4, j % 4
                    if j == 0:
                        w(pe, "g_vbd", b + 1)
                    w(pe, "a_exp", 8 * b + j + 1)
                    o = slice(32 * i, 32 * i + 32)
                    mm(bankA[o, k, :], vbd[:, j, :], prob[:, i, :], start=True, stop=True).then_inc(s["p_av"], 1)
                    mm(bankB0[o, :], c("densel")[:, 32 * k:32 * k + 32], prob[:, i, :], start=(k == 0),
                       stop=(k == 1), skip_group_check=True).then_inc(s["p_av"], 1)

            def den_turn(b):
                w(pe, "a_den", b + 1)
                for t in range(LT):
                    last = nc.tensor.transpose(bankB1[:, t * P:(t + 1) * P], den[:, t * P:(t + 1) * P], ident)
                last.then_inc(s["p_denT"], 1)

            def rden_turn(b):
                w(pe, "v_rdl", KD * b + 2)
                for t in range(LT):
                    last = nc.tensor.transpose(bankB0[:, t * P:(t + 1) * P], rdm[:, t, :], ident)
                last.then_inc(s["p_rdT"], 1)

            def spread(b):
                w(pe, "a_rdT", b + 1)
                w(pe, "a_av", KD * b + 2)
                for k in range(KD):
                    mm(bankA[:, k, :], feat_r[:, k, :], rdT[:, :], start=True, stop=True).then_inc(s["p_bc"], 1)

            def project_out(b):
                w(pe, "v_at", KD * b + 2)
                for n in range(2):
                    for h in range(2):
                        o = slice((2 * n + h) * P, (2 * n + h + 1) * P)
                        for k in range(KD):
                            last = three(bankB[n][:, h * D:(h + 1) * D], at_h[:, k, o], at_l[:, k, o],
                                         we_h[:, k, :], we_l[:, k, :], k == 0, k == KD - 1)
                    last.then_inc(s["p_proj"], 1)

            def x2_turn(b):
                for n in range(2):
                    for t in range(2):
                        w(pe, "v_xn2", LT * b + 2 * n + t + 1)
                        for k in range(KD):
                            o = (t * KD + k) * P
                            last = nc.tensor.transpose(bankA[:, n, o:o + P], xr[:, 2 * n + t, k * P:(k + 1) * P], ident)
                    last.then_inc(s["p_x2T"], 1)

            def logits(b):
                w(pe, "a_x2T", 2 * b + 2)
                w(pe, "v_x1", 2 * b + 2)
                for t in range(LT):
                    for k in range(KD):
                        last = mm(bankB0[:, t * NE:(t + 1) * NE], x2T[:, t, k, :], rw[:, k, :],
                                  start=(k == 0), stop=(k == KD - 1))
                last.then_inc(s["p_lg"], 1)

            def positions(b):
                w(pe, "v_mbf", 2 * b + 2)
                mm(bankB1[:, 0:LT * NE], upper_bf[:, :], msum_bf[:, :, :].rearrange("p t e -> p (t e)"), start=True, stop=False)
                mm(bankB1[:, 0:LT * NE], ones_bf[:, :], seen_bf[:, :, :].rearrange("p t e -> p (t e)"), start=False,
                   stop=True).then_inc(s["p_pos"], 1)

            def slots(b):
                for q in range(TOPK * LT):
                    w(pe, "v_hot", 16 * b + 2 * q + 2)
                    mm(bankM[:, 0:P], hot[:, q % 4, :], put[:, q % 4, :], start=False, stop=False,
                       skip_group_check=True).then_inc(s["p_map"], 1)

            x_turn(0)
            project_q(0)
            for t in range(LT):
                scores(0, t)
            max_turn(0)
            scores_turned(0, range(4))

            with pe.Fori(1, B) as i:
                values(i - 1, range(4))
                scores_turned(i - 1, range(4, 8))
                values(i - 1, range(4, 8))
                x_turn(i)
                project_q(i)
                scores(i, 0)
                den_turn(i - 1)
                scores(i, 1)
                rden_turn(i - 1)
                scores(i, 2)
                spread(i - 1)
                scores(i, 3)
                project_out(i - 1)
                max_turn(i)
                scores_turned(i, range(4))
                x2_turn(i - 1)
                logits(i - 1)
                positions(i - 1)
                slots(i - 1)
            values(B - 1, range(4))
            scores_turned(B - 1, range(4, 8))
            values(B - 1, range(4, 8))
            den_turn(B - 1)
            rden_turn(B - 1)
            spread(B - 1)
            project_out(B - 1)
            x2_turn(B - 1)
            logits(B - 1)
            positions(B - 1)
            w(pe, "v_pos", 4 * (B - 1) + 1)
            w(pe, "v_seen", 5 * B)
            mm(bankB1[:, 64:64 + NE], c("ones"), seen[:, 0, :], start=True, stop=True)
            slots(B - 1)
            mm(bankM[:, 0:P], zero_r[:, :], zero_r[:, :], start=False, stop=True, skip_group_check=True)\
                .then_inc(s["p_fin"], 1)

            def x_turn_f(t, ring):
                pe.wait_ge(d_gather, 16 * (t + 1))
                for k in range(KD):
                    last = nc.tensor.transpose(bankA[:, 0, k * P:(k + 1) * P], xr[:, ring, k * P:(k + 1) * P], ident)
                last.then_inc(s["p_fxT"], 1)

            def h_turn(t):
                for n in range(2):
                    w(pe, "a_gelu", 2 * t + n + 1)
                    for m in range(4):
                        o = (4 * n + m) * P
                        last = nc.tensor.transpose(bankB[n][:, m * P:(m + 1) * P], hbuf[:, o:o + P], ident)
                    last.then_inc(s["p_fhT"], 1)

            def up_product(t, par):
                w(pe, "v_fxT", t + 1)
                for n in range(2):
                    o = slice(n * 512, (n + 1) * 512)
                    for k in range(KD):
                        x_o = slice(k * P, (k + 1) * P)
                        last = three(bankC[:, n, :], xT_h[:, x_o], xT_l[:, x_o],
                                     up_w[:, 0, bass.ds(par, 1), k, o].rearrange("p a n -> p (a n)"),
                                     up_w[:, 1, bass.ds(par, 1), k, o].rearrange("p a n -> p (a n)"),
                                     k == 0, k == KD - 1)
                    last.then_inc(s["p_up"], 1)

            def down_product(t, par):
                for m in range(KF):
                    if m % 4 == 0:
                        w(pe, "v_fhT", 2 * t + m // 4 + 1)
                    o = slice(m * P, (m + 1) * P)
                    wd = dn_w[:, bass.ds(par, 1), m, :, :].rearrange("p a h n -> p (a h n)")
                    mm(bankC[:, 2, :], hT_h[:, o], wd, start=(m == 0), stop=False)
                    last = mm(bankC[:, 2, 0:D], hT_l[:, o], wd[:, 0:D], start=False, stop=(m == KF - 1))
                last.then_inc(s["p_dn"], 1)

            w(pe, "v_tab", 1)
            w(pe, "v_wlo", 8)
            nt = pe.value_load(nt_i[0:1, 0:1], min_val=MINT * NE, max_val=NT)
            x_turn_f(0, 0)
            up_product(0, 0)
            x_turn_f(1, 1)
            h_turn(0)
            up_product(1, 0)
            with pe.Fori(1, NT, 2) as u:
                for r in range(2):
                    t = u + r
                    with pe.If(nt > t):
                        x_turn_f(t + 1, r)
                        par_before = pe.value_load(tpar_i[0:1, bass.ds(t - 1, 1)], min_val=0, max_val=1)
                        down_product(t - 1, par_before)
                        h_turn(t)
                        e = pe.value_load(te_i[0:1, bass.ds(t + 1, 1)], min_val=0, max_val=NE - 1)
                        par = pe.value_load(tpar_i[0:1, bass.ds(t + 1, 1)], min_val=0, max_val=1)
                        w(pe, "v_wlo", 4 * e + 4)
                        up_product(t + 1, par)
            last = pe.value_load(nt_i[0:1, 1:2], min_val=MINT * NE - 1, max_val=NT - 1)
            par_last = pe.value_load(tpar_i[0:1, bass.ds(last, 1)], min_val=0, max_val=1)
            down_product(last, par_last)


def kernel(**inputs):
    import numpy as np
    import concourse.bacc as bacc
    from concourse.bass_utils import run_bass_kernel_spmd

    a = {k: np.asarray(v_) for k, v_ in inputs.items()}
    ctx_ = a["ctx_1024"]
    up = a["L0_ffn_expert_up"].transpose(0, 2, 1).reshape(2 * NE, P, FF)
    down = a["L0_ffn_expert_down"].transpose(0, 2, 1).reshape(NE, 2, 4, P, D).transpose(0, 1, 3, 2, 4)
    arrays = {
        "x": a["x"].reshape(T, D),
        "ctx_t": ctx_.transpose(2, 0, 1).reshape(D, B * S),
        "ctx_t2": np.concatenate([ctx_, ctx_], axis=1).transpose(2, 0, 1).reshape(D, B * 2 * S),
        "wq": a["L0_xattn_Wq"], "wk": a["L0_xattn_Wk"], "wv": a["L0_xattn_Wv"], "we": a["L0_xattn_We"],
        "bqkv": np.stack([a[f"L0_xattn_b{n}"].reshape(KD, P) for n in "qkv"]).transpose(2, 0, 1).reshape(P, 3 * KD),
        "be": a["L0_xattn_be"],
        "router_w": a["L0_ffn_router_w"], "router_b": a["L0_ffn_router_b"],
        "up": up, "down": down.reshape(2 * NE, P, 4 * D),
        "const": constants(),
    }
    arrays = {k: np.ascontiguousarray(v_) for k, v_ in arrays.items()}
    nc = bacc.Bacc("TRN2", target_bir_lowering=False, num_devices=1)
    args = [nc.dram_tensor(k, v_.shape, mybir.dt.from_np(v_.dtype), kind="ExternalInput").ap()
            for k, v_ in arrays.items()]
    out = nc.dram_tensor("out", (T + P, D), F32, kind="ExternalOutput").ap()
    rows = nc.dram_tensor("rows", (T + P, XROW), F32, kind="Internal").ap()
    build(nc, *args, out, rows)
    r = run_bass_kernel_spmd(nc, [arrays], core_ids=[0])
    return r.results[0]["out"][0:T].reshape(B, L, D)
```

```python
from contextlib import ExitStack

import concourse.bass as bass
from concourse import mybir
from concourse.alu_op_type import AluOpType as ALU

F32 = mybir.dt.float32
F32R = mybir.dt.float32r
BF16 = mybir.dt.bfloat16
I32 = mybir.dt.int32
U32 = mybir.dt.uint32
ACT = mybir.ActivationFunctionType
AX_X = mybir.AxisListType.X

P = 128
B, L, D = 4, 512, 256
S, H, HE = 64, 16, 16
NE, FF, TOPK = 8, 1024, 2
T = B * L
LT = L // P
NTOK = T // P
KD = D // P
KF = FF // P
MINT = 2
NT = T * TOPK // P + MINT * (NE - TOPK)
NTAB = NT + 3
EPS = 1e-5
SCALE = HE ** -0.5
XROW = D + NE
COLS = NTOK
MAPC = NE * COLS + 32

_at = 0
CONST = {}
for _name, _n in (("ident", P), ("iota", P), ("upper", P), ("ones", P), ("head", 8), ("densel", 2 * 32), ("tile", 1), ("step", COLS - 1),
                  ("flip", NE), ("token", NTOK), ("spare", 1), ("power", 16), ("expert", NE),
                  ("sel", 8 * P), ("feat", KD * P)):
    CONST[_name] = (_at, _at + _n)
    _at += _n
NCONST = _at
EARLY = CONST["sel"][0]


def constants():
    import numpy as np

    c = np.zeros((P, NCONST), np.float32)
    p = np.arange(P)

    def part(name):
        a, b = CONST[name]
        return c[:, a:b]

    part("ident")[:] = np.eye(P)
    part("iota")[:] = np.arange(P)
    part("upper")[:] = p[:, None] < p[None, :]
    part("ones")[:] = 1
    part("head")[:] = p[:, None] // HE == np.arange(8)
    sel = part("sel").reshape(P, 8, P)
    feat = part("feat").reshape(P, KD, P)
    for r in range(32):
        for j in range(8):
            sel[r, j] = (r % H) == 2 * j + p // S
        head = 8 * (r // 2 % 2) + 2 * (r // 4 % 4) + r % 2
        for k in range(KD):
            feat[r, k] = head == 8 * k + p // HE
    for k in range(2):
        for h in range(2):
            part("densel").reshape(P, 2, 32)[h * S:(h + 1) * S, k, 2 * k + h] = 1
    part("tile")[:] = p[:, None]
    part("step")[:] = P * np.arange(1, COLS)
    part("flip")[:] = [0] + [1 if e % 2 else -1 for e in range(1, NE)]
    part("token")[:] = P * np.arange(NTOK) + p[:, None] - T
    part("spare")[:] = T + p[:, None]
    part("power")[:] = -0.5
    part("expert")[:] = np.arange(NE)
    return c


def build(nc, x, ctx_t, ctx_t2, wq, wk, wv, we, bqkv, be, router_w, router_b, up, down, const, out, rows):
    with ExitStack() as ctx:
        def sb(name, shape, dt=F32):
            return ctx.enter_context(nc.sbuf_tensor(name, shape, dt))

        def ps(name, shape, dt=F32):
            return ctx.enter_context(nc.psum_tensor(name, shape, dt))

        def sem(name):
            return ctx.enter_context(nc.semaphore(name))

        cst = sb("cst", [P, NCONST])

        def c(name):
            a, b = CONST[name]
            return cst[:, a:b]

        sel_r = sb("sel_r", [P, 8, P], F32R)
        feat_r = sb("feat_r", [P, KD, P], F32R)
        zero_r = sb("zero_r", [P, P], F32R)
        upper_bf = sb("upper_bf", [P, P], BF16)
        ones_bf = sb("ones_bf", [P, P], BF16)
        wq_h, wq_l = sb("wq_h", [P, KD, D], F32R), sb("wq_l", [P, KD, D], F32R)
        we_h, we_l = sb("we_h", [P, KD, D], F32R), sb("we_l", [P, KD, D], F32R)
        rw = sb("rw", [P, KD, 32])
        rb = sb("rb", [P, NE])
        be_b = sb("be_b", [P, D])
        bias = sb("bias", [P, 3, KD])
        ctxT = sb("ctxT", [P, KD, B * S])
        ctxT2 = sb("ctxT2", [P, KD, B, 2 * S])
        kT_h, kT_l = sb("kT_h", [P, KD, B * S]), sb("kT_l", [P, KD, B * S])
        v_all = sb("v_all", [P, B, D])
        xall = sb("xall", [P, NTOK, D])
        stat1 = sb("stat1", [P, NTOK, 6])
        mv1 = sb("mv1", [P, NTOK, 2])
        var1 = sb("var1", [P, NTOK])
        rstd1 = sb("rstd1", [P, NTOK])
        xn = sb("xn", [P, LT, D])
        xnT_h, xnT_l = sb("xnT_h", [P, KD, L], F32R), sb("xnT_l", [P, KD, L], F32R)
        q_h, q_l = sb("q_h", [P, KD, L], F32R), sb("q_l", [P, KD, L], F32R)
        kbd_h, kbd_l = sb("kbd_h", [P, KD, 8, S], F32R), sb("kbd_l", [P, KD, 8, S], F32R)
        vbd = sb("vbd", [P, 8, 32])
        nmax = sb("nmax", [P, LT, H])
        nmx = sb("nmx", [P, LT, P])
        nmxT = sb("nmxT", [P, L], F32R)
        prob = sb("prob", [P, 4, L])
        wraw = prob
        av = sb("av", [P, KD, L])
        den = sb("den", [P, L])
        rden = sb("rden", [P, LT, 4, 4])
        rdm = sb("rdm", [P, LT, P])
        rdT = sb("rdT", [P, L], F32R)
        at_h, at_l = sb("at_h", [P, KD, L], F32R), sb("at_l", [P, KD, L], F32R)
        stat2 = sb("stat2", [P, LT, 6])
        mv2 = sb("mv2", [P, LT, 2])
        var2 = sb("var2", [P, LT])
        rstd2 = sb("rstd2", [P, LT])
        xr = sb("xr", [P, LT, XROW])
        x2T = sb("x2T", [P, LT, KD, P])
        lg, lgs, ex, pr = (sb(n, [P, LT, NE]) for n in ("lg", "lgs", "ex", "pr"))
        lmax, lsum, lrec = (sb(n, [P, LT]) for n in ("lmax", "lsum", "lrec"))
        v8 = sb("v8", [P, LT, 8])
        i8 = sb("i8", [P, LT, 8], U32)
        ef = sb("ef", [P, TOPK, LT])
        mk = sb("mk", [P, TOPK, LT, NE])
        msum = sb("msum", [P, LT, NE])
        msum_bf = sb("msum_bf", [P, LT, NE], BF16)
        mtot = sb("mtot", [P, NE])
        seen = sb("seen", [P, NE])
        seen_bf = sb("seen_bf", [P, NE], BF16)
        lgT = sb("lgT", [P, P])
        pk = sb("pk", [P, TOPK, LT, NE])
        rank = sb("rank", [P, TOPK * LT])
        cmp = sb("cmp", [P, TOPK * LT, COLS - 1])
        ltile, lrow, key, val = (sb(n, [P, TOPK * LT]) for n in ("ltile", "lrow", "key", "val"))
        hot = sb("hot", [P, 4, P], F32R)
        put = sb("put", [P, 4, P], F32R)
        slot_f = sb("slot_f", [P, NE * COLS])
        slot = sb("slot", [P, MAPC], I32)
        ntile, tend, tbeg = (sb(n, [P, NE]) for n in ("ntile", "tend", "tbeg"))
        big = sb("big", [P, NE, COLS - 1])
        on = sb("on", [P, NE])
        onb = sb("onb", [P, NE])
        onf = sb("onf", [P, NE])
        te1, tb, tone, tsec, tlt = (sb(n, [P, 1]) for n in ("te1", "tb", "tone", "tsec", "tlt"))
        pack = sb("pack", [P, 8])
        tab = sb("tab", [8, NTAB], I32)
        te_i, tcol_i, tpar_i, tsp_i, traw_i = (tab[i:i + 1, :] for i in range(5))
        nt_i = tab[5:6, 0:1]
        raw01 = sb("raw01", [P, 2, 1024])
        up_w = sb("up_w", [P, 2, 2, KD, FF], F32R)
        dn_w = sb("dn_w", [P, 2, KF, 2, D], F32R)
        idx_g = sb("idx_g", [P, 2], I32)
        idx_s = sb("idx_s", [P, 1], I32)
        gate = sb("gate", [P, NTAB])
        prime = sb("prime", [P, 14])
        raw = xall[:, :, :].rearrange("p t d -> p (t d)")
        hbuf = raw01[:, 0, :]
        y = x2T[:, 0, :, :].rearrange("p k l -> p (k l)")
        osb = x2T[:, 1, :, :].rearrange("p k l -> p (k l)")
        xT_h, xT_l = xnT_h[:, 0, 0:D], xnT_l[:, 0, 0:D]
        hT_h = q_h[:, :, :].rearrange("p k l -> p (k l)")
        hT_l = q_l[:, :, :].rearrange("p k l -> p (k l)")

        bankM = ps("bankM", [P, 512])
        bankA = ps("bankA", [P, 2, 512])
        bankB0 = ps("bankB0", [P, 512])
        bankB1 = ps("bankB1", [P, 512])
        bankC = ps("bankC", [P, 3, 512])
        bankB = [bankB0, bankB1]

        d_const, d_sel, d_x0, d_x, d_zero = (sem(n) for n in ("d_const", "d_sel", "d_x0", "d_x", "d_zero"))
        d_k, d_q, d_v, d_we, d_w = (sem(n) for n in ("d_k", "d_q", "d_v", "d_we", "d_w"))
        d_x1, d_rows = sem("d_x1"), sem("d_rows")
        d_raw01, d_rawu, d_rawd = sem("d_raw01"), sem("d_rawu"), sem("d_rawd")
        d_gather = [sem("d_gather0"), sem("d_gather1")]
        d_add = sem("d_add")
        a_const, a_wsplit, a_k, a_v, a_xT, a_q, a_nmT, a_exp = (
            sem(n) for n in "a_const a_wsplit a_k a_v a_xT a_q a_nmT a_exp".split())
        a_av, a_den, a_rdT, a_at, a_x2T, a_ex, a_lgT, a_w01 = (
            sem(n) for n in "a_av a_den a_rdT a_at a_x2T a_ex a_lgT a_w01".split())
        a_fxT, a_fhT, a_gelu, a_osb, a_whi = (
            sem(n) for n in "a_fxT a_fhT a_gelu a_osb a_whi".split())
        v_wsplit, v_k, v_stat1, v_var1, v_xn, v_xT, v_q, v_max = (
            sem(n) for n in "v_wsplit v_k v_stat1 v_var1 v_xn v_xT v_q v_max".split())
        v_nmh, v_nml, v_rden, v_rdh, v_rdl, v_att, v_at, v_x1 = (
            sem(n) for n in "v_nmh v_nml v_rden v_rdh v_rdl v_att v_at v_x1".split())
        v_stat2, v_var2, v_xn2, v_lg, v_pr, v_top, v_mk, v_msum = (
            sem(n) for n in "v_stat2 v_var2 v_xn2 v_lg v_pr v_top v_mk v_msum".split())
        v_seen, v_comb, v_mbf, v_mtot, v_pos, v_key, v_hot, v_put = (
            sem(n) for n in "v_seen v_comb v_mbf v_mtot v_pos v_key v_hot v_put".split())
        v_pack, v_tab, v_slot, v_done, v_fxT, v_gate, v_fhT, v_y = (
            sem(n) for n in "v_pack v_tab v_slot v_done v_fxT v_gate v_fhT v_y".split())
        v_wlo, = (
            sem(n) for n in "v_wlo".split())
        g_zero, g_kbd, g_vbd, g_rstd1, g_res, g_rstd2, g_rw, g_w01 = (
            sem(n) for n in "g_zero g_kbd g_vbd g_rstd1 g_res g_rstd2 g_rw g_w01".split())
        g_gi, g_si = (
            sem(n) for n in "g_gi g_si".split())
        p_kv, p_xT, p_q, p_s, p_nmT, p_sT, p_av, p_denT = (
            sem(n) for n in "p_kv p_xT p_q p_s p_nmT p_sT p_av p_denT".split())
        p_rdT, p_bc, p_proj, p_x2T, p_lg, p_pos, p_map, p_lgT = (
            sem(n) for n in "p_rdT p_bc p_proj p_x2T p_lg p_pos p_map p_lgT".split())
        p_fin, p_tab, p_fxT, p_fhT, p_up, p_dn = (
            sem(n) for n in "p_fin p_tab p_fxT p_fhT p_up p_dn".split())

        block = ctx.enter_context(nc.Block())

        @block.sync
        def _(sp):
            x_t = x.rearrange("(t p) d -> p t d", p=P)
            sp.dma_start(xall[:, 0:LT, :], x_t[:, 0:LT, :]).then_inc(d_x0, 16)
            sp.dma_start(cst[:, 0:EARLY], const[:, 0:EARLY]).then_inc(d_const, 16)

            def rows_of(a):
                return a.rearrange("(k p) n -> p k n", p=P)

            def raw_w(n):
                return wraw[:, n, :].rearrange("p (k n) -> p k n", k=KD)

            sp.dma_start(raw_w(1), rows_of(wk)).then_inc(d_k, 16)
            sp.dma_start(ctxT[:, :, :], rows_of(ctx_t)).then_inc(d_k, 16)
            sp.dma_start(bias[:, :, :], bqkv.rearrange("p (j k) -> p j k", k=KD)).then_inc(d_k, 16)
            sp.dma_start(raw_w(0), rows_of(wq)).then_inc(d_q, 16)
            sp.dma_start(xall[:, LT:NTOK, :], x_t[:, LT:NTOK, :]).then_inc(d_x, 16)
            sp.dma_start(raw_w(2), rows_of(wv)).then_inc(d_v, 16)
            sp.dma_start(ctxT2[:, :, :, :].rearrange("p k b s -> p k (b s)"), rows_of(ctx_t2)).then_inc(d_v, 16)
            sp.dma_start(raw_w(3), rows_of(we)).then_inc(d_we, 16)
            sp.dma_start(cst[:, EARLY:NCONST], const[:, EARLY:NCONST]).then_inc(d_sel, 16)
            sp.wait_ge(g_rw, 1)
            sp.dma_start(rw[:, :, 0:NE], rows_of(router_w)).then_inc(d_w, 16)
            sp.dma_start(be_b[:, :], be.rearrange("(a n) -> a n", a=1).broadcast_to([P, D])).then_inc(d_w, 16)
            sp.dma_start(rb[:, :], router_b.rearrange("(a n) -> a n", a=1).broadcast_to([P, NE])).then_inc(d_w, 16)
            sp.wait_ge(g_zero, 2)
            zeros = zero_r[:, :].bitcast(F32)
            zeros_d = zeros.rearrange("p (a n) -> p a n", a=1).broadcast_to([P, KD, P])
            sp.dma_start(rows[T:T + P, 0:D].rearrange("p (a n) -> p a n", a=KD), zeros_d).then_inc(d_zero, 16)
            sp.dma_start(rows[T:T + P, D:XROW], zeros[:, 0:NE]).then_inc(d_zero, 16)
            sp.dma_start(out[T:T + P, :].rearrange("p (a n) -> p a n", a=KD), zeros_d).then_inc(d_zero, 16)

            def load01(i):
                if not (isinstance(i, int) and i == 0):
                    sp.wait_ge(g_w01, 2 * i)
                sp.dma_start(raw01[:, 0, :], up[bass.ds(i, 1)].rearrange("a p n -> (a p) n")).then_inc(d_raw01, 16)
                sp.dma_start(raw01[:, 1, :], down[bass.ds(i, 1)].rearrange("a p n -> (a p) n")).then_inc(d_raw01, 16)

            def store(g):
                sp.wait_ge(v_x1, 2 * g + 2)
                sp.dma_start(out[bass.ds(g * L, L), :].rearrange("(t p) d -> p t d", p=P),
                             xall[:, bass.ds(g * LT, LT), :]).then_inc(d_x1, 16)
                sp.wait_ge(v_comb, g + 1)
                sp.dma_start(rows[bass.ds(g * L, L), :].rearrange("(t p) d -> p t d", p=P),
                             xr[:, :, :]).then_inc(d_rows, 16)

            load01(0)
            with sp.Fori(1, B) as i:
                load01(i)
                store(i - 1)
            store(B - 1)
            sp.wait_ge(d_x1, 16 * B)
            for e in range(2, NE):
                if e > 2:
                    sp.wait_ge(v_wlo, 8 + 4 * (e - 2))
                sp.dma_start(raw[:, 0:2048].rearrange("p (h n) -> p h n", h=2), up[2 * e:2 * e + 2].rearrange("h p n -> p h n")).then_inc(d_rawu, 16)
                sp.dma_start(raw[:, 2048:4096].rearrange("p (h n) -> p h n", h=2), down[2 * e:2 * e + 2].rearrange("h p n -> p h n")).then_inc(d_rawd, 16)

        @block.gpsimd
        def _(pool):
            g = nc.gpsimd
            g.memset(rw[:, :, :], 0.0).then_inc(g_rw, 1)
            g.memset(prime[:, 3:4], 0.0).then_inc(g_zero, 1)
            g.memset(zero_r[:, :].bitcast(F32), 0.0).then_inc(g_zero, 1)
            g.memset(nmx[:, :, :], 0.0).then_inc(g_zero, 1)
            g.memset(rdm[:, :, :], 0.0).then_inc(g_zero, 1)

            def rstd(out_, var_, n):
                return g.tensor_tensor(out_, var_, c("power")[:, 0:n], ALU.pow)

            def key_blocks(b):
                pool.wait_ge(a_k, 2)
                pool.wait_ge(v_k, 2)
                if not (isinstance(b, int) and b == 0):
                    pool.wait_ge(p_sT, 8 * b)
                for part, src in ((kbd_h, kT_h), (kbd_l, kT_l)):
                    for k in range(KD):
                        cols = src[:, k, bass.ds(b * S, S)].rearrange("p (a s) -> p a s", a=1)
                        g.tensor_tensor(part[:, k, :, :], cols.broadcast_to([P, 8, S]),
                                        c("head").rearrange("p (h a) -> p h a", a=1).broadcast_to([P, 8, S]),
                                        ALU.mult).then_inc(g_kbd, 1)

            def value_blocks(b):
                pool.wait_ge(a_v, 2)
                if not (isinstance(b, int) and b == 0):
                    pool.wait_ge(p_av, 16 * b)
                g.tensor_tensor(vbd[:, :, :].rearrange("p j (h e) -> p j h e", h=2),
                                v_all[:, bass.ds(b, 1), :].rearrange("p a (j h e) -> p (a j) h e", h=2, e=HE),
                                c("densel")[:, 0:2].rearrange("p (a h b) -> p a h b", a=1, b=1)
                                .broadcast_to([P, 8, 2, HE]), ALU.mult).then_inc(g_vbd, 1)

            def low01(i):
                pool.wait_ge(d_raw01, 32 * (i + 1))
                pool.wait_ge(a_w01, 2 * (i + 1))
                g.tensor_tensor(up_flat[:, 1, bass.ds(i, 1), :], raw01[:, 0:1, :],
                                up_flat[:, 0, bass.ds(i, 1), :].bitcast(F32), ALU.subtract).then_inc(g_w01, 1)
                g.tensor_tensor(dn_flat[:, bass.ds(4 * i, 4), 1, :],
                                raw01[:, 1, :].rearrange("p (c n) -> p c n", c=4),
                                dn_flat[:, bass.ds(4 * i, 4), 0, :].bitcast(F32), ALU.subtract).then_inc(g_w01, 1)

            up_flat = up_w[:, :, :, :, :].rearrange("p h b k n -> p h (b k) n")
            dn_flat = dn_w[:, :, :, :, :].rearrange("p b k h n -> p (b k) h n")

            def residual(b):
                pool.wait_ge(v_xn, LT * (b + 1))
                g.tensor_tensor(xall[:, bass.ds(b * LT, LT), :], xall[:, bass.ds(b * LT, LT), :],
                                be_b[:, :].rearrange("p (a n) -> p a n", a=1).broadcast_to([P, LT, D]),
                                ALU.add).then_inc(g_res, 1)

            pool.wait_ge(d_const, 16)
            pool.wait_ge(v_var1, 1)
            rstd(rstd1[:, 0:LT], var1[:, 0:LT], LT).then_inc(g_rstd1, 1)
            pool.wait_ge(g_zero, 4)
            key_blocks(0)
            pool.wait_ge(v_var1, 2)
            rstd(rstd1[:, LT:NTOK], var1[:, LT:NTOK], NTOK - LT).then_inc(g_rstd1, 1)
            value_blocks(0)
            pool.wait_ge(d_w, 48)
            residual(0)
            low01(0)
            def settle():
                g.tensor_tensor(prime[0:1, 2:3], prime[0:1, 3:4], prime[0:1, 3:4], ALU.add)

            with pool.Fori(1, B) as i:
                key_blocks(i)
                residual(i)
                pool.wait_ge(v_var2, i)
                rstd(rstd2[:, :], var2[:, :], LT).then_inc(g_rstd2, 1)
                value_blocks(i)
                low01(i)
            pool.wait_ge(v_var2, B)
            rstd(rstd2[:, :], var2[:, :], LT).then_inc(g_rstd2, 1)
            pool.wait_ge(v_slot, 2)
            pool.wait_ge(d_rows, 16 * B)
            pool.wait_ge(d_zero, 48)
            pool.wait_ge(d_x1, 16 * B)

            def gather(t, ring, nth, col=None):
                if col is None:
                    col = pool.value_load(tcol_i[:, bass.ds(t, 1)], min_val=0, max_val=MAPC - 1)
                if not (isinstance(t, int) and t < 2):
                    pool.wait_ge(d_gather[ring], 16 * nth)
                g.tensor_copy(idx_g[:, ring:ring + 1], slot[:, bass.ds(col, 1)]).then_inc(g_gi, 1)
                pool.wait_ge(g_gi, t + 1)
                if not (isinstance(t, int) and t < 2):
                    pool.wait_ge(p_fxT, t - 1)
                    pool.wait_ge(v_gate, t - 1)
                settle()
                g.indirect_dma_start(xr[:, ring, :], None, rows, bass.IndirectOffsetOnAxis(idx_g[:, ring:ring + 1], 0),
                                     bounds_check=T + P - 1).then_inc(d_gather[ring], 16)

            def add(t):
                col = pool.value_load(tcol_i[:, bass.ds(t, 1)], min_val=0, max_val=MAPC - 1)
                if not (isinstance(t, int) and t == 0):
                    pool.wait_ge(d_add, 16 * t)
                g.tensor_copy(idx_s[:, :], slot[:, bass.ds(col, 1)]).then_inc(g_si, 1)
                pool.wait_ge(g_si, t + 1)
                pool.wait_ge(v_y, t + 1)
                settle()
                g.indirect_dma_start(out, bass.IndirectOffsetOnAxis(idx_s[:, 0:1], 0), y, None,
                                     bounds_check=T + P - 1, compute_op=ALU.add).then_inc(d_add, 16)

            gather(0, 0, 0, col=0)
            gather(1, 1, 0, col=1)
            pool.wait_ge(v_tab, 1)
            nt = pool.value_load(nt_i, min_val=MINT * NE, max_val=NT)
            gather(2, 0, 1)
            gather(3, 1, 1)
            add(0)
            with pool.Fori(1, NT // 2) as u:
                t = 2 * u
                with pool.If(nt > t):
                    gather(t + 2, 0, u + 1)
                    add(t - 1)
                    with pool.If(nt > t + 1):
                        gather(t + 3, 1, u + 1)
                        add(t)
                        with pool.If(nt < t + 3):
                            add(t + 1)
                    with pool.If(nt < t + 2):
                        add(t)
            pool.wait_ge(d_add, 16 * nt)

        @block.scalar
        def _(act):
            a = nc.scalar

            def attention_constants():
                act.wait_ge(d_const, 16)
                a.activation(upper_bf[:, :], c("upper"), ACT.Identity).then_inc(a_const, 1)
                a.activation(ones_bf[:, :], c("ones"), ACT.Identity).then_inc(a_const, 1)
                act.wait_ge(d_sel, 16)
                a.activation(sel_r[:, :, :], c("sel").rearrange("p (j n) -> p j n", j=8), ACT.Identity)\
                    .then_inc(a_const, 1)
                a.activation(feat_r[:, :, :], c("feat").rearrange("p (j n) -> p j n", j=KD), ACT.Identity)\
                    .then_inc(a_const, 1)

            def weight_high(part, n):
                a.activation(part[:, :, :], wraw[:, n, :].rearrange("p (k n) -> p k n", k=KD), ACT.Identity)\
                    .then_inc(a_wsplit, 1)

            def keys():
                for k in range(KD):
                    act.wait_ge(p_kv, k + 1)
                    act.wait_ge(d_k, 48)
                    a.activation(kT_h[:, k, :].bitcast(F32R), bankC[:, k, 0:B * S], ACT.Identity, bias=bias[:, 1, k:k + 1]).then_inc(a_k, 1)

            def values():
                for n in range(2):
                    act.wait_ge(p_kv, 3 + n)
                    a.activation(v_all[:, 2 * n:2 * n + 2, :].rearrange("p b d -> p (b d)"), bankA[:, n, :], ACT.Identity).then_inc(a_v, 1)

            def x_high(b, n):
                act.wait_ge(p_xT, 2 * b + n + 1)
                a.activation(xnT_h[:, :, n * 256:(n + 1) * 256].rearrange("p k (t l) -> p t k l", t=2),
                     bankB1[:, :].rearrange("p (t k l) -> p t k l", t=2, k=KD), ACT.Identity).then_inc(a_xT, 1)

            def q_high(b):
                for n, k in enumerate((1, 0)):
                    act.wait_ge(p_q, KD * b + n + 1)
                    a.activation(q_h[:, k, :], bankB[k][:, :], ACT.Identity, bias=bias[:, 0, k:k + 1]).then_inc(a_q, 1)

            def max_turn(b):
                act.wait_ge(p_nmT, b + 1)
                a.activation(nmxT[:, :], bankC[:, 2, :], ACT.Identity).then_inc(a_nmT, 1)

            def exps(b, js):
                for j in js:
                    act.wait_ge(p_sT, 8 * b + j + 1)
                    if j >= 4:
                        act.wait_ge(p_av, 16 * b + 2 * (j - 3))
                    elif not (isinstance(b, int) and b == 0):
                        act.wait_ge(p_av, 16 * b)
                    a.activation(prob[:, j % 4, :], bankC[:, j % 3, :], ACT.Exp, scale=SCALE).then_inc(a_exp, 1)

            def den_copy(b):
                act.wait_ge(p_av, 16 * b + 16)
                a.activation(den[:, :], bankB0[:, :], ACT.Identity).then_inc(a_den, 1)

            def av_copy(b, k):
                act.wait_ge(p_av, 16 * b + 8 * k + 8)
                a.activation(av[:, k, :], bankA[:, k, :], ACT.Identity).then_inc(a_av, 1)

            def rden_turn(b):
                act.wait_ge(p_rdT, b + 1)
                a.activation(rdT[:, :], bankA[:, 1, :], ACT.Identity).then_inc(a_rdT, 1)

            def att_high(b):
                for k in range(KD):
                    act.wait_ge(v_att, KD * b + k + 1)
                    a.activation(at_h[:, k, :], av[:, k, :], ACT.Identity, bias=bias[:, 2, k:k + 1]).then_inc(a_at, 1)

            def x2_turn(b):
                for n in range(2):
                    act.wait_ge(p_x2T, 2 * b + n + 1)
                    a.activation(x2T[:, 2 * n:2 * n + 2, :, :].rearrange("p t k l -> p (t k l)"), bankA[:, n, :], ACT.Identity).then_inc(a_x2T, 1)

            def logit_copy(b):
                act.wait_ge(p_lg, b + 1)
                a.activation(lgT[:, :], bankB0[:, 0:P], ACT.Identity).then_inc(a_lgT, 1)

            def router_exp(b):
                act.wait_ge(v_lg, 3 * b + 3)
                a.activation(ex[:, :, :], lgs[:, :, :], ACT.Exp).then_inc(a_ex, 1)

            def high01(i):
                act.wait_ge(d_raw01, 32 * (i + 1))
                a.activation(up_flat[:, 0, bass.ds(i, 1), :], raw01[:, 0:1, :], ACT.Identity).then_inc(a_w01, 1)
                a.activation(dn_flat[:, bass.ds(4 * i, 4), 0, :], raw01[:, 1, :].rearrange("p (c n) -> p c n", c=4), ACT.Identity).then_inc(a_w01, 1)

            up_flat = up_w[:, :, :, :, :].rearrange("p h b k n -> p h (b k) n")
            dn_flat = dn_w[:, :, :, :, :].rearrange("p b k h n -> p (b k) h n")

            keys()
            act.wait_ge(d_q, 16)
            weight_high(wq_h, 0)
            x_high(0, 0)
            x_high(0, 1)
            q_high(0)
            values()
            attention_constants()
            act.wait_ge(d_we, 16)
            weight_high(we_h, 3)
            high01(0)
            max_turn(0)
            act.wait_ge(v_wsplit, 2)
            act.wait_ge(p_kv, 4)
            exps(0, range(4))

            def batch(i):
                av_copy(i - 1, 0)
                x_high(i, 0)
                exps(i - 1, range(4, 8))
                x_high(i, 1)
                den_copy(i - 1)
                av_copy(i - 1, 1)
                q_high(i)
                rden_turn(i - 1)
                att_high(i - 1)
                high01(i)
                max_turn(i)
                exps(i, range(4))
                x2_turn(i - 1)
                logit_copy(i - 1)
                router_exp(i - 1)

            with act.Fori(1, B) as i:
                batch(i)
            av_copy(B - 1, 0)
            exps(B - 1, range(4, 8))
            den_copy(B - 1)
            av_copy(B - 1, 1)
            rden_turn(B - 1)
            att_high(B - 1)
            x2_turn(B - 1)
            logit_copy(B - 1)
            router_exp(B - 1)

            a.activation(prime[:, 0:1], c("ones")[:, 0:1], ACT.Gelu).then_inc(a_whi, 8)

            def x_high_f(t):
                act.wait_ge(p_fxT, t + 1)
                a.activation(xT_h, bankA[:, 0, 0:D], ACT.Identity).then_inc(a_fxT, 1)

            def h_high(t):
                for n in range(2):
                    act.wait_ge(p_fhT, 2 * t + n + 1)
                    a.activation(hT_h[:, n * 512:(n + 1) * 512], bankB[n][:, :], ACT.Identity).then_inc(a_fhT, 1)

            def gelu(t, n):
                act.wait_ge(p_up, 2 * t + n + 1)
                a.activation(hbuf[:, n * 512:(n + 1) * 512], bankC[:, n, :], ACT.Gelu).then_inc(a_gelu, 1)

            def low_part(t):
                act.wait_ge(p_dn, t + 1)
                act.wait_ge(v_gate, t + 1)
                a.activation(osb, bankC[:, 2, D:2 * D], ACT.Identity, scale=gate[:, bass.ds(t, 1)]).then_inc(a_osb, 1)

            def weights_high(t, half):
                sp_e = act.value_load(tsp_i[:, bass.ds(t, 1)], min_val=0, max_val=NE - 1)
                with act.If(sp_e > 1):
                    nraw = act.value_load(traw_i[:, bass.ds(t, 1)], min_val=1, max_val=NE - 2)
                    par = act.value_load(tpar_i[:, bass.ds(t, 1)], min_val=0, max_val=1)
                    other = 1 - par
                    act.wait_ge(d_rawd if half else d_rawu, 16 * nraw)
                    for n in range(2):
                        if half:
                            a.activation(dn_w[:, bass.ds(other, 1), 4 * n:4 * n + 4, 0, :].rearrange("p a c n -> p (a c) n"),
                                 raw[:, 2048 + n * 1024:2048 + (n + 1) * 1024].rearrange("p (c n) -> p c n", c=4), ACT.Identity).then_inc(a_whi, 1)
                        else:
                            a.activation(up_w[:, 0, bass.ds(other, 1), n, :], raw[:, n * FF:(n + 1) * FF], ACT.Identity).then_inc(a_whi, 1)

            x_high_f(0)
            gelu(0, 0)
            x_high_f(1)
            gelu(0, 1)
            h_high(0)
            act.wait_ge(v_tab, 1)
            nt = act.value_load(nt_i, min_val=MINT * NE, max_val=NT)

            def tile(t):
                gelu(t, 0)
                x_high_f(t + 1)
                gelu(t, 1)
                weights_high(t, 0)
                low_part(t - 1)
                h_high(t)
                weights_high(t, 1)

            tile(1)
            with act.Fori(1, NT // 2) as u:
                t = 2 * u
                with act.If(nt > t):
                    tile(t)
                    with act.If(nt > t + 1):
                        tile(t + 1)
                        with act.If(nt < t + 3):
                            low_part(t + 1)
                    with act.If(nt < t + 2):
                        low_part(t)
        @block.vector
        def _(dve):
            v = nc.vector

            v.memset(seen[:, :], 0.0).then_inc(v_seen, 1)
            v.memset(seen_bf[:, :], 0.0).then_inc(v_seen, 1)

            def settle(n):
                v.memset(prime[:, n:n + 1], 0.0)

            def stats1(t0, n, tiles_per):
                for k in range(n):
                    v.bn_stats(stat1[:, t0 + k, :], xall[:, t0 + k, :]).then_inc(v_stat1, 1)

            def aggr1(t0, n, base):
                for k in range(n):
                    dve.wait_ge(v_stat1, base + k + 1)
                    v.bn_aggr(mv1[:, t0 + k, :], stat1[:, t0 + k, :]).then_inc(v_stat1, 1)
                dve.wait_ge(v_stat1, base + 2 * n)
                v.tensor_scalar(var1[:, t0:t0 + n], mv1[:, t0:t0 + n, 1], EPS, None, ALU.add).then_inc(v_var1, 1)

            def norm1(b):
                if isinstance(b, int) and b == 0:
                    dve.wait_ge(g_rstd1, 1)
                else:
                    dve.wait_ge(g_rstd1, 2)
                    dve.wait_ge(p_xT, 2 * b)
                for k in range(LT):
                    tt = b * LT + k
                    v.tensor_scalar(xn[:, k, :], xall[:, bass.ds(tt, 1), :].rearrange("p a d -> p (a d)"),
                                        mv1[:, bass.ds(tt, 1), 0], rstd1[:, bass.ds(tt, 1)],
                                        ALU.subtract, ALU.mult).then_inc(v_xn, 1)

            def x_low(b, n):
                dve.wait_ge(a_xT, 2 * b + n + 1)
                o = slice(n * 256, (n + 1) * 256)
                v.tensor_tensor(xnT_l[:, :, o].rearrange("p k (t l) -> p t k l", t=2),
                                    bankB1[:, :].rearrange("p (t k l) -> p t k l", t=2, k=KD),
                                    xnT_h[:, :, o].bitcast(F32).rearrange("p k (t l) -> p t k l", t=2),
                                    ALU.subtract).then_inc(v_xT, 1)

            def q_low(b):
                for n, k in enumerate((1, 0)):
                    dve.wait_ge(a_q, KD * b + n + 1)
                    v.scalar_tensor_tensor(out=q_l[:, k, :], in0=bankB[k][:, :], scalar=bias[:, 0, k:k + 1],
                                               in1=q_h[:, k, :].bitcast(F32), op0=ALU.add, op1=ALU.subtract).then_inc(v_q, 1)

            def maxima(b, t):
                for k in range(KD):
                    n = KD * t + k
                    dve.wait_ge(p_s, 8 * b + n + 1)
                    v.tensor_reduce(nmax[:, t, 8 * k:8 * k + 8],
                                        bankC[:, n % 3, :].rearrange("p (h s) -> p h s", h=8), AX_X, ALU.max,
                                        negate=True).then_inc(v_max, 1)

            def max_split(b):
                dve.wait_ge(v_max, 8 * b + 8)
                v.tensor_copy(nmx[:, :, 0:H].bitcast(F32R), nmax[:, :, :]).then_inc(v_nmh, 1)
                dve.wait_ge(v_nmh, b + 1)
                v.tensor_tensor(nmx[:, :, H:2 * H].bitcast(F32R), nmax[:, :, :], nmx[:, :, 0:H], ALU.subtract).then_inc(v_nml, 1)

            def rden_split(b):
                dve.wait_ge(p_denT, b + 1)
                dv = bankA[:, 0, :].rearrange("p (t i r) -> p t i r", t=LT, i=4)[:, :, :, 0:4]
                v.reciprocal(rden[:, :, :, :], dv).then_inc(v_rden, 1)
                dve.wait_ge(v_rden, b + 1)
                hi = rdm[:, :, 0:H].rearrange("p t (i r) -> p t i r", i=4)
                lo = rdm[:, :, H:2 * H].rearrange("p t (i r) -> p t i r", i=4)
                v.tensor_copy(hi.bitcast(F32R), rden[:, :, :, :]).then_inc(v_rdh, 1)
                dve.wait_ge(v_rdh, b + 1)
                v.tensor_tensor(lo.bitcast(F32R), rden[:, :, :, :], hi, ALU.subtract).then_inc(v_rdl, 1)

            def att(b):
                for k in range(KD):
                    dve.wait_ge(a_av, KD * b + k + 1)
                    dve.wait_ge(p_bc, KD * b + k + 1)
                    v.tensor_tensor(av[:, k, :], bankA[:, k, :], av[:, k, :], ALU.mult).then_inc(v_att, 1)

            def att_low(b):
                for k in range(KD):
                    dve.wait_ge(a_at, KD * b + k + 1)
                    v.scalar_tensor_tensor(out=at_l[:, k, :], in0=av[:, k, :], scalar=bias[:, 2, k:k + 1],
                                               in1=at_h[:, k, :].bitcast(F32), op0=ALU.add, op1=ALU.subtract).then_inc(v_at, 1)

            def residual_norm2(b):
                dve.wait_ge(g_res, b + 1)
                for n in range(2):
                    dve.wait_ge(p_proj, 2 * b + n + 1)
                    xs = xall[:, bass.ds(b * LT + 2 * n, 2), :]
                    v.tensor_tensor(xs, bankB[n][:, :].rearrange("p (t d) -> p t d", t=2), xs, ALU.add).then_inc(v_x1, 1)
                    dve.wait_ge(v_x1, 2 * b + n + 1)
                    settle(5)
                    for k in (2 * n, 2 * n + 1):
                        v.bn_stats(stat2[:, k, :], xall[:, bass.ds(b * LT + k, 1), :]
                                       .rearrange("p a d -> p (a d)")).then_inc(v_stat2, 1)
                dve.wait_ge(v_stat2, 8 * b + LT)
                settle(6)
                for k in range(LT):
                    v.bn_aggr(mv2[:, k, :], stat2[:, k, :]).then_inc(v_stat2, 1)
                dve.wait_ge(v_stat2, 8 * b + 8)
                v.tensor_scalar(var2[:, :], mv2[:, :, 1], EPS, None, ALU.add).then_inc(v_var2, 1)
                dve.wait_ge(g_rstd2, b + 1)
                if not (isinstance(b, int) and b == 0):
                    dve.wait_ge(d_rows, 16 * b)
                for k in range(LT):
                    v.tensor_scalar(xr[:, k, 0:D], xall[:, bass.ds(b * LT + k, 1), :].rearrange("p a d -> p (a d)"),
                                        mv2[:, k, 0:1], rstd2[:, k:k + 1], ALU.subtract, ALU.mult).then_inc(v_xn2, 1)

            def bc3(ap, n):
                return ap.rearrange("p (q a) -> p q a", a=1).broadcast_to([P, ap.shape[1], n])

            def logits(b):
                dve.wait_ge(p_lgT, b + 1)
                v.tensor_tensor(lg[:, :, :], bankB0[:, P:2 * P].rearrange("p (t e) -> p t e", t=LT)[:, :, 0:NE],
                                    rb[:, :].rearrange("p (a e) -> p a e", a=1).broadcast_to([P, LT, NE]), ALU.add).then_inc(v_lg, 1)
                dve.wait_ge(v_lg, 3 * b + 1)
                v.tensor_reduce(lmax[:, :], lg[:, :, :], AX_X, ALU.max, negate=True).then_inc(v_lg, 1)
                dve.wait_ge(v_lg, 3 * b + 2)
                v.tensor_tensor(lgs[:, :, :], lg[:, :, :], bc3(lmax[:, :], NE), ALU.add).then_inc(v_lg, 1)

            def router(b):
                dve.wait_ge(a_ex, b + 1)
                v.tensor_reduce(lsum[:, :], ex[:, :, :], AX_X, ALU.add).then_inc(v_pr, 1)
                dve.wait_ge(v_pr, 3 * b + 1)
                v.reciprocal(lrec[:, :], lsum[:, :]).then_inc(v_pr, 1)
                dve.wait_ge(v_pr, 3 * b + 2)
                v.tensor_tensor(pr[:, :, :], ex[:, :, :], bc3(lrec[:, :], NE), ALU.mult).then_inc(v_pr, 1)
                dve.wait_ge(v_pr, 3 * b + 3)
                settle(7)
                for t in range(LT):
                    v.max(out=v8[:, t, :], in_=pr[:, t, :]).then_inc(v_top, 1)
                dve.wait_ge(v_top, 8 * b + LT)
                settle(8)
                for t in range(LT):
                    v.max_index(i8[:, t, :], v8[:, t, :], pr[:, t, :]).then_inc(v_top, 1)
                dve.wait_ge(v_top, 8 * b + 8)
                v.tensor_copy(ef[:, :, :], i8[:, :, 0:TOPK].rearrange("p t k -> p k t")).then_inc(v_mk, 1)
                dve.wait_ge(v_mk, 2 * b + 1)
                v.tensor_tensor(mk[:, :, :, :].rearrange("p k t e -> p (k t) e"),
                                    c("expert").rearrange("p (a e) -> p a e", a=1).broadcast_to([P, TOPK * LT, NE]),
                                    bc3(ef[:, :, :].rearrange("p k t -> p (k t)"), NE), ALU.is_equal).then_inc(v_mk, 1)
                dve.wait_ge(v_mk, 2 * b + 2)
                v.tensor_tensor(msum_bf[:, :, :], mk[:, 0, :, :], mk[:, 1, :, :], ALU.add).then_inc(v_mbf, 1)
                v.tensor_tensor(msum[:, :, :], mk[:, 0, :, :], mk[:, 1, :, :], ALU.add).then_inc(v_msum, 1)
                dve.wait_ge(v_msum, b + 1)
                v.tensor_tensor(xr[:, :, D:XROW], pr[:, :, :], msum[:, :, :], ALU.mult).then_inc(v_comb, 1)

            def count(b):
                v.tensor_reduce(mtot[:, :], msum[:, :, :].rearrange("p t e -> p e t"), AX_X, ALU.add).then_inc(v_mtot, 1)
                dve.wait_ge(v_mtot, b + 1)
                dve.wait_ge(p_pos, b + 1)
                v.tensor_tensor(seen[:, :], seen[:, :], mtot[:, :], ALU.add).then_inc(v_seen, 1)
                dve.wait_ge(v_seen, 2 * b + 3)
                v.tensor_copy(seen_bf[:, :], seen[:, :]).then_inc(v_seen, 1)

            def ranks(b, counts):
                dve.wait_ge(p_pos, b + 1)
                v.tensor_tensor(pk[:, :, :, :], mk[:, :, :, :],
                                    counts[:, 0:LT * NE].rearrange("p (a t e) -> p a t e", a=1, t=LT)
                                    .broadcast_to([P, TOPK, LT, NE]), ALU.mult).then_inc(v_pos, 1)
                dve.wait_ge(v_pos, 4 * b + 1)
                v.tensor_reduce(rank[:, :], pk[:, :, :, :].rearrange("p k t e -> p (k t) e"), AX_X, ALU.add).then_inc(v_pos, 1)
                dve.wait_ge(v_pos, 4 * b + 2)
                v.tensor_tensor(cmp[:, :, :], bc3(rank[:, :], COLS - 1),
                                    c("step").rearrange("p (a n) -> p a n", a=1).broadcast_to([P, TOPK * LT, COLS - 1]),
                                    ALU.is_ge).then_inc(v_pos, 1)
                dve.wait_ge(v_pos, 4 * b + 3)
                v.tensor_reduce(ltile[:, :], cmp[:, :, :], AX_X, ALU.add).then_inc(v_pos, 1)
                dve.wait_ge(v_pos, 4 * b + 4)
                v.scalar_tensor_tensor(out=lrow[:, :], in0=ltile[:, :], scalar=-float(P), in1=rank[:, :],
                                           op0=ALU.mult, op1=ALU.add).then_inc(v_key, 1)
                v.scalar_tensor_tensor(out=key[:, :], in0=ef[:, :, :].rearrange("p k t -> p (k t)"),
                                           scalar=float(COLS), in1=ltile[:, :], op0=ALU.mult, op1=ALU.add).then_inc(v_key, 1)
                dve.wait_ge(v_key, 3 * b + 1)
                a0 = CONST["token"][0]
                tok = cst[:, bass.ds(a0 + b * LT, LT)].rearrange("p (a t) -> p a t", a=1).broadcast_to([P, TOPK, LT])
                v.tensor_tensor(val[:, :].rearrange("p (k t) -> p k t", k=TOPK), tok,
                                    lrow[:, :].rearrange("p (k t) -> p k t", k=TOPK), ALU.subtract).then_inc(v_key, 1)

            def puts(b, half):
                dve.wait_ge(v_key, 3 * b + 3)
                for q in range(4 * half, 4 * half + 4):
                    dve.wait_ge(p_map, 8 * b + max(q - 3, 0) + 1)
                    v.tensor_scalar(hot[:, q % 4, :], c("iota"), lrow[:, q:q + 1], None, ALU.is_equal).then_inc(v_hot, 1)
                    v.tensor_scalar(put[:, q % 4, :], c("iota"), key[:, q:q + 1], val[:, q:q + 1],
                                        ALU.is_equal, ALU.mult).then_inc(v_put, 1)

            dve.wait_ge(d_x0, 16)
            stats1(0, LT, LT)
            aggr1(0, LT, 0)
            norm1(0)
            for k in range(KD):
                dve.wait_ge(a_k, k + 1)
                v.scalar_tensor_tensor(out=kT_l[:, k, :].bitcast(F32R), in0=bankC[:, k, 0:B * S],
                                       scalar=bias[:, 1, k:k + 1], in1=kT_h[:, k, :],
                                       op0=ALU.add, op1=ALU.subtract).then_inc(v_k, 1)

            def weight_low(low, high, n):
                v.tensor_tensor(low[:, :, :], wraw[:, n, :].rearrange("p (k n) -> p k n", k=KD),
                                high[:, :, :].bitcast(F32), ALU.subtract).then_inc(v_wsplit, 1)

            dve.wait_ge(a_wsplit, 1)
            weight_low(wq_l, wq_h, 0)
            x_low(0, 0)
            x_low(0, 1)
            q_low(0)
            dve.wait_ge(d_x, 16)
            stats1(LT, NTOK - LT, LT)
            aggr1(LT, NTOK - LT, 2 * LT)
            dve.wait_ge(d_const, 16)
            dve.wait_ge(g_zero, 4)
            dve.wait_ge(v_seen, 2)
            for t in range(LT):
                maxima(0, t)
            max_split(0)
            dve.wait_ge(a_wsplit, 2)
            weight_low(we_l, we_h, 3)
            dve.wait_ge(d_w, 48)

            def batch(i, with_router):
                norm1(i)
                x_low(i, 0)
                if with_router:
                    router(i - 2)
                x_low(i, 1)
                if with_router:
                    ranks(i - 2, bankC[:, 2, :])
                    count(i - 2)
                    puts(i - 2, 0)
                q_low(i)
                rden_split(i - 1)
                maxima(i, 0)
                maxima(i, 1)
                att(i - 1)
                maxima(i, 2)
                att_low(i - 1)
                maxima(i, 3)
                max_split(i)
                residual_norm2(i - 1)
                if with_router:
                    puts(i - 2, 1)
                logits(i - 1)

            batch(1, False)
            with dve.Fori(2, B) as i:
                batch(i, True)
            router(B - 2)
            ranks(B - 2, bankB1)
            count(B - 2)
            puts(B - 2, 0)
            puts(B - 2, 1)
            rden_split(B - 1)
            att(B - 1)
            att_low(B - 1)
            residual_norm2(B - 1)
            logits(B - 1)
            router(B - 1)
            ranks(B - 1, bankB1)

            v.tensor_tensor(big[:, :, :], bc3(bankB1[:, LT * NE:(LT + 1) * NE], COLS - 1),
                                c("step").rearrange("p (a n) -> p a n", a=1).broadcast_to([P, NE, COLS - 1]),
                                ALU.is_gt).then_inc(v_done, 1)
            puts(B - 1, 0)
            puts(B - 1, 1)
            dve.wait_ge(p_fin, 1)
            v.tensor_scalar(slot[:, 0:NE * COLS], bankM[:, 0:NE * COLS], c("spare"), None, ALU.add).then_inc(v_slot, 1)
            v.tensor_scalar(slot[:, NE * COLS:MAPC], c("iota")[:, 0:32], 0.0, c("spare"), ALU.mult, ALU.add).then_inc(v_slot, 1)
            dve.wait_ge(v_done, 1)
            v.tensor_reduce(ntile[:, :], big[:, :, :], AX_X, ALU.add).then_inc(v_done, 1)
            dve.wait_ge(v_done, 2)
            v.tensor_scalar(ntile[:, :], ntile[:, :], 1.0, float(MINT), ALU.add, ALU.max).then_inc(v_done, 1)
            dve.wait_ge(v_done, 3)
            v.tensor_tensor_scan(tend[:, :], c("ones")[:, 0:NE], ntile[:, :], 0.0, ALU.mult, ALU.add).then_inc(v_done, 1)
            dve.wait_ge(v_done, 4)
            v.tensor_tensor(tbeg[:, :], tend[:, :], ntile[:, :], ALU.subtract).then_inc(v_done, 1)
            dve.wait_ge(v_done, 5)
            v.tensor_scalar(on[:, :], tbeg[:, :], c("tile"), None, ALU.is_le).then_inc(v_done, 1)
            v.scalar_tensor_tensor(out=onb[:, :], in0=tbeg[:, :], scalar=c("tile"), in1=tbeg[:, :],
                                       op0=ALU.is_le, op1=ALU.mult).then_inc(v_done, 1)
            v.scalar_tensor_tensor(out=onf[:, :], in0=tbeg[:, :], scalar=c("tile"), in1=c("flip"),
                                       op0=ALU.is_le, op1=ALU.mult).then_inc(v_done, 1)
            v.tensor_copy(pack[:, 5:8], tend[:, NE - 1:NE].broadcast_to([P, 3])).then_inc(v_done, 1)
            dve.wait_ge(v_done, 8)
            v.tensor_reduce(te1[:, :], on[:, :], AX_X, ALU.add).then_inc(v_done, 1)
            v.tensor_reduce(tb[:, :], onb[:, :], AX_X, ALU.max).then_inc(v_done, 1)
            v.tensor_reduce(pack[:, 2:3], onf[:, :], AX_X, ALU.add).then_inc(v_done, 1)
            dve.wait_ge(v_done, 11)
            v.tensor_scalar(tone[:, :], tb[:, :], -1.0, c("tile"), ALU.mult, ALU.add).then_inc(v_done, 1)
            v.tensor_scalar(tlt[:, :], te1[:, :], float(NE) - 0.5, None, ALU.is_lt).then_inc(v_done, 1)
            v.tensor_scalar(pack[:, 0:1], te1[:, :], -1.0, None, ALU.add).then_inc(v_done, 1)
            dve.wait_ge(v_done, 14)
            v.tensor_scalar(tsec[:, :], tone[:, :], 1.0, tlt[:, :], ALU.is_equal, ALU.mult).then_inc(v_done, 1)
            dve.wait_ge(v_done, 15)
            v.scalar_tensor_tensor(out=pack[:, 1:2], in0=pack[:, 0:1], scalar=float(COLS), in1=tone[:, :],
                                       op0=ALU.mult, op1=ALU.add).then_inc(v_done, 1)
            dve.wait_ge(v_done, 16)
            v.tensor_tensor(pack[:, 3:4], te1[:, :], tsec[:, :], ALU.mult).then_inc(v_done, 1)
            dve.wait_ge(v_done, 18)
            v.tensor_scalar(pack[:, 4:5], pack[:, 3:4], -1.0, None, ALU.add).then_inc(v_pack, 1)
            dve.wait_ge(p_tab, 1)
            v.tensor_copy(tab[:, :], bankA[0:8, 1, 0:NTAB]).then_inc(v_tab, 1)

            def x_low_f(t, ring, nth):
                e = 0 if isinstance(t, int) and t < MINT else dve.value_load(te_i[:, bass.ds(t, 1)], min_val=0, max_val=NE - 1)
                dve.wait_ge(d_gather[ring], 16 * (nth + 1))
                v.tensor_copy(gate[:, bass.ds(t, 1)], xr[:, ring, bass.ds(D + e, 1)]).then_inc(v_gate, 1)
                dve.wait_ge(a_fxT, t + 1)
                v.tensor_tensor(xT_l, bankA[:, 0, 0:D], xT_h.bitcast(F32), ALU.subtract).then_inc(v_fxT, 1)

            def h_low(t):
                for n in range(2):
                    dve.wait_ge(a_fhT, 2 * t + n + 1)
                    o = slice(n * 512, (n + 1) * 512)
                    v.tensor_tensor(hT_l[:, o], bankB[n][:, :], hT_h[:, o].bitcast(F32), ALU.subtract).then_inc(v_fhT, 1)

            def result(t):
                dve.wait_ge(a_osb, t + 1)
                if not (isinstance(t, int) and t == 0):
                    dve.wait_ge(d_add, 16 * t)
                v.scalar_tensor_tensor(out=y, in0=bankC[:, 2, 0:D], scalar=gate[:, bass.ds(t, 1)],
                                           in1=osb, op0=ALU.mult, op1=ALU.add).then_inc(v_y, 1)

            def weights_low(t, half):
                e = dve.value_load(tsp_i[:, bass.ds(t, 1)], min_val=0, max_val=NE - 1)
                with dve.If(e > 1):
                    par = dve.value_load(tpar_i[:, bass.ds(t, 1)], min_val=0, max_val=1)
                    other = 1 - par
                    for n in range(2):
                        dve.wait_ge(a_whi, 4 * e + 2 * half + n + 1)
                        settle(10 + 2 * half + n)
                        if half:
                            dst = dn_w[:, bass.ds(other, 1), 4 * n:4 * n + 4, :, :].rearrange("p a c h n -> p (a c) h n")
                            v.tensor_tensor(dst[:, :, 1, :],
                                                raw[:, 2048 + n * 1024:2048 + (n + 1) * 1024]
                                                .rearrange("p (c n) -> p c n", c=4),
                                                dst[:, :, 0, :].bitcast(F32), ALU.subtract).then_inc(v_wlo, 1)
                        else:
                            v.tensor_tensor(up_w[:, 1, bass.ds(other, 1), n, :].rearrange("p a n -> p (a n)"),
                                                raw[:, n * FF:(n + 1) * FF],
                                                up_w[:, 0, bass.ds(other, 1), n, :].bitcast(F32)
                                                .rearrange("p a n -> p (a n)"), ALU.subtract).then_inc(v_wlo, 1)

            dve.wait_ge(g_w01, 8)
            v.memset(prime[:, 1:2], 0.0).then_inc(v_wlo, 8)
            x_low_f(0, 0, 0)
            x_low_f(1, 1, 0)
            h_low(0)
            dve.wait_ge(v_tab, 1)
            nt = dve.value_load(nt_i, min_val=MINT * NE, max_val=NT)

            def tile(t, ring, nth):
                x_low_f(t + 1, ring, nth)
                weights_low(t, 0)
                result(t - 1)
                h_low(t)
                weights_low(t, 1)

            tile(1, 0, 1)
            with dve.Fori(1, NT // 2) as u:
                t = 2 * u
                with dve.If(nt > t):
                    tile(t, 1, u)
                    with dve.If(nt > t + 1):
                        tile(t + 1, 0, u + 1)
                        with dve.If(nt < t + 3):
                            result(t + 1)
                    with dve.If(nt < t + 2):
                        result(t)
        @block.tensor
        def _(pe):
            mm = nc.tensor.matmul
            ident = c("ident")

            def three(out_, left_h, left_l, right_h, right_l, first, last):
                mm(out_, left_h, right_h, start=first, stop=False)
                mm(out_, left_h, right_l, start=False, stop=False)
                return mm(out_, left_l, right_h, start=False, stop=last)

            def keys():
                pe.wait_ge(d_k, 48)
                for k in range(KD):
                    for d in range(KD):
                        last = mm(bankC[:, k, 0:B * S], wraw[:, 1, d * D + k * P:d * D + (k + 1) * P], ctxT[:, d, :],
                                  start=(d == 0), stop=(d == KD - 1))
                    last.then_inc(p_kv, 1)

            def values_of_all():
                pe.wait_ge(d_v, 32)
                for n in range(2):
                    for h in range(2):
                        for d in range(KD):
                            last = mm(bankA[:, n, h * D:(h + 1) * D], ctxT2[:, d, 2 * n + h, :],
                                      wraw[:, 2, d * D:(d + 1) * D], start=(d == 0), stop=(d == KD - 1))
                    last.then_inc(p_kv, 1)

            def x_turn(b, n):
                if not (isinstance(b, int) and b == 0 and n == 0):
                    pe.wait_ge(v_xT, 2 * b + n)
                for t in range(2):
                    pe.wait_ge(v_xn, LT * b + 2 * n + t + 1)
                    for k in range(KD):
                        o = (t * KD + k) * P
                        last = nc.tensor.transpose(bankB1[:, o:o + P], xn[:, 2 * n + t, k * P:(k + 1) * P], ident)
                last.then_inc(p_xT, 1)

            def project_q(b):
                pe.wait_ge(v_xT, 2 * b + 2)
                if isinstance(b, int) and b == 0:
                    pe.wait_ge(v_wsplit, 1)
                for k in (1, 0):
                    if k == 0 and not (isinstance(b, int) and b == 0):
                        pe.wait_ge(a_den, b)
                    o = slice(k * P, (k + 1) * P)
                    for d in range(KD):
                        last = three(bankB[k][:, :], wq_h[:, d, o], wq_l[:, d, o], xnT_h[:, d, :], xnT_l[:, d, :],
                                     d == 0, d == KD - 1)
                    last.then_inc(p_q, 1)

            def scores(b, t):
                for k in range(KD):
                    n = KD * t + k
                    if n == 0:
                        pe.wait_ge(v_q, KD * b + 2)
                        pe.wait_ge(g_kbd, 4 * b + 4)
                    if n >= 3:
                        pe.wait_ge(v_max, 8 * b + n - 2)
                    o = slice(t * P, (t + 1) * P)
                    three(bankC[:, n % 3, :], q_h[:, k, o], q_l[:, k, o],
                          kbd_h[:, k, :, :].rearrange("p h s -> p (h s)"), kbd_l[:, k, :, :].rearrange("p h s -> p (h s)"),
                          True, True).then_inc(p_s, 1)

            def max_turn(b):
                pe.wait_ge(v_nml, b + 1)
                for t in range(LT):
                    last = nc.tensor.transpose(bankC[:, 2, t * P:(t + 1) * P], nmx[:, t, :], ident)
                last.then_inc(p_nmT, 1)

            def scores_turned(b, js):
                for j in js:
                    k, i = j // 4, j % 4
                    if j == 0:
                        pe.wait_ge(a_nmT, b + 1)
                        pe.wait_ge(a_const, 4)
                    if j >= 3:
                        pe.wait_ge(a_exp, 8 * b + j - 2)
                    kh = kbd_h[:, k, 2 * i:2 * i + 2, :].rearrange("p h s -> p (h s)")
                    kl = kbd_l[:, k, 2 * i:2 * i + 2, :].rearrange("p h s -> p (h s)")
                    three(bankC[:, j % 3, :], kh, kl, q_h[:, k, :], q_l[:, k, :], True, False)
                    mm(bankC[:, j % 3, :], sel_r[:, j, :], nmxT[:, :], start=False, stop=True).then_inc(p_sT, 1)

            def values(b, js):
                for j in js:
                    k, i = j // 4, j % 4
                    if j == 0:
                        pe.wait_ge(g_vbd, b + 1)
                        if not (isinstance(b, int) and b == 0):
                            pe.wait_ge(v_lg, 3 * (b - 1) + 1)
                    pe.wait_ge(a_exp, 8 * b + j + 1)
                    o = slice(32 * i, 32 * i + 32)
                    mm(bankA[o, k, :], vbd[:, j, :], prob[:, i, :], start=True, stop=True).then_inc(p_av, 1)
                    mm(bankB0[o, :], c("densel")[:, 32 * k:32 * k + 32], prob[:, i, :], start=(k == 0),
                       stop=(k == 1), skip_group_check=True).then_inc(p_av, 1)

            def den_turn(b):
                pe.wait_ge(a_den, b + 1)
                pe.wait_ge(a_av, KD * b + 1)
                for t in range(LT):
                    last = nc.tensor.transpose(bankA[:, 0, t * P:(t + 1) * P], den[:, t * P:(t + 1) * P], ident)
                last.then_inc(p_denT, 1)

            def rden_turn(b):
                pe.wait_ge(v_rdl, b + 1)
                pe.wait_ge(a_av, KD * b + 2)
                for t in range(LT):
                    last = nc.tensor.transpose(bankA[:, 1, t * P:(t + 1) * P], rdm[:, t, :], ident)
                last.then_inc(p_rdT, 1)

            def spread(b):
                pe.wait_ge(a_rdT, b + 1)
                pe.wait_ge(a_av, KD * b + 2)
                for k in range(KD):
                    mm(bankA[:, k, :], feat_r[:, k, :], rdT[:, :], start=True, stop=True).then_inc(p_bc, 1)

            def project_out(b):
                pe.wait_ge(v_at, KD * b + 2)
                for n in range(2):
                    for h in range(2):
                        o = slice((2 * n + h) * P, (2 * n + h + 1) * P)
                        for k in range(KD):
                            last = three(bankB[n][:, h * D:(h + 1) * D], at_h[:, k, o], at_l[:, k, o],
                                         we_h[:, k, :], we_l[:, k, :], k == 0, k == KD - 1)
                    last.then_inc(p_proj, 1)

            def x2_turn(b):
                for n in range(2):
                    for t in range(2):
                        pe.wait_ge(v_xn2, LT * b + 2 * n + t + 1)
                        for k in range(KD):
                            o = (t * KD + k) * P
                            last = nc.tensor.transpose(bankA[:, n, o:o + P], xr[:, 2 * n + t, k * P:(k + 1) * P], ident)
                    last.then_inc(p_x2T, 1)

            def logits(b):
                pe.wait_ge(v_x1, 2 * b + 2)
                for k in range(KD):
                    for t in range(LT):
                        pe.wait_ge(a_x2T, 2 * b + t // 2 + 1)
                        last = mm(bankB0[32 * t:32 * t + 32, 0:P], rw[:, k, :], x2T[:, t, k, :],
                                  start=(k == 0), stop=(k == KD - 1), skip_group_check=True)
                last.then_inc(p_lg, 1)
                pe.wait_ge(a_lgT, b + 1)
                nc.tensor.transpose(bankB0[:, P:2 * P], lgT[:, :], ident).then_inc(p_lgT, 1)

            def positions(b, counts):
                pe.wait_ge(v_mbf, b + 1)
                pe.wait_ge(v_seen, 2 * b + 2)
                last_batch = isinstance(b, int) and b == B - 1
                flat = msum_bf[:, :, :].rearrange("p t e -> p (t e)")
                if last_batch:
                    everyone = counts[:, LT * NE:(LT + 1) * NE]
                    mm(everyone, ones_bf[:, :], seen_bf[:, :], start=True, stop=False, skip_group_check=True)
                    for t in range(LT):
                        mm(everyone, ones_bf[:, :], msum_bf[:, t, :], start=False, stop=(t == LT - 1),
                           skip_group_check=True)
                mm(counts[:, 0:LT * NE], upper_bf[:, :], flat, start=True, stop=False, skip_group_check=True)
                for d in range(1, LT):
                    mm(counts[:, d * NE:LT * NE], ones_bf[:, :], flat[:, 0:(LT - d) * NE], start=False,
                       stop=False, skip_group_check=True)
                mm(counts[:, 0:LT * NE], ones_bf[:, :],
                   seen_bf[:, :].rearrange("p (a e) -> p a e", a=1).broadcast_to([P, LT, NE]), start=False,
                   stop=True, skip_group_check=True).then_inc(p_pos, 1)

            def slots(b, half):
                for q in range(4 * half, 4 * half + 4):
                    pe.wait_ge(v_hot, 8 * b + q + 1)
                    pe.wait_ge(v_put, 8 * b + q + 1)
                    mm(bankM[:, 0:P], hot[:, q % 4, :], put[:, q % 4, :], start=False, stop=False,
                       skip_group_check=True).then_inc(p_map, 1)

            keys()
            pe.wait_ge(g_zero, 4)
            mm(bankM[:, 0:P], zero_r[:, :], zero_r[:, :], start=True, stop=False, skip_group_check=True)\
                .then_inc(p_map, 1)
            pe.wait_ge(d_const, 16)
            x_turn(0, 0)
            x_turn(0, 1)
            project_q(0)
            values_of_all()
            for t in range(LT):
                scores(0, t)
            max_turn(0)
            scores_turned(0, range(4))

            def batch(i, router):
                values(i - 1, range(4))
                x_turn(i, 0)
                scores_turned(i - 1, range(4, 8))
                x_turn(i, 1)
                if router:
                    pe.wait_ge(a_exp, 8 * i - 2)
                    positions(i - 2, bankC[:, 2, :])
                values(i - 1, range(4, 8))
                project_q(i)
                den_turn(i - 1)
                if router:
                    slots(i - 2, 0)
                scores(i, 0)
                rden_turn(i - 1)
                scores(i, 1)
                spread(i - 1)
                scores(i, 2)
                scores(i, 3)
                project_out(i - 1)
                max_turn(i)
                scores_turned(i, range(4))
                x2_turn(i - 1)
                if router:
                    slots(i - 2, 1)
                logits(i - 1)

            batch(1, False)
            with pe.Fori(2, B) as i:
                batch(i, True)
            values(B - 1, range(4))
            positions(B - 2, bankB1)
            scores_turned(B - 1, range(4, 8))
            slots(B - 2, 0)
            slots(B - 2, 1)
            values(B - 1, range(4, 8))
            den_turn(B - 1)
            rden_turn(B - 1)
            spread(B - 1)
            project_out(B - 1)
            x2_turn(B - 1)
            logits(B - 1)
            positions(B - 1, bankB1)
            pe.wait_ge(v_done, 1)
            slots(B - 1, 0)
            slots(B - 1, 1)
            mm(bankM[:, 0:P], zero_r[:, :], zero_r[:, :], start=False, stop=True, skip_group_check=True)\
                .then_inc(p_fin, 1)

            def x_turn_f(t, ring, nth):
                pe.wait_ge(d_gather[ring], 16 * (nth + 1))
                for k in range(KD):
                    last = nc.tensor.transpose(bankA[:, 0, k * P:(k + 1) * P], xr[:, ring, k * P:(k + 1) * P], ident)
                last.then_inc(p_fxT, 1)

            def h_turn(t):
                for n in range(2):
                    pe.wait_ge(a_gelu, 2 * t + n + 1)
                    for m in range(4):
                        o = (4 * n + m) * P
                        last = nc.tensor.transpose(bankB[n][:, m * P:(m + 1) * P], hbuf[:, o:o + P], ident)
                    last.then_inc(p_fhT, 1)

            def up_product(t, par):
                pe.wait_ge(v_fxT, t + 1)
                for n in range(2):
                    o = slice(n * 512, (n + 1) * 512)
                    for k in range(KD):
                        x_o = slice(k * P, (k + 1) * P)
                        last = three(bankC[:, n, :], xT_h[:, x_o], xT_l[:, x_o],
                                     up_w[:, 0, bass.ds(par, 1), k, o].rearrange("p a n -> p (a n)"),
                                     up_w[:, 1, bass.ds(par, 1), k, o].rearrange("p a n -> p (a n)"),
                                     k == 0, k == KD - 1)
                    last.then_inc(p_up, 1)

            def down_product(t, par):
                for m in range(KF):
                    if m % 4 == 0:
                        pe.wait_ge(v_fhT, 2 * t + m // 4 + 1)
                    o = slice(m * P, (m + 1) * P)
                    wd = dn_w[:, bass.ds(par, 1), m, :, :].rearrange("p a h n -> p (a h n)")
                    mm(bankC[:, 2, :], hT_h[:, o], wd, start=(m == 0), stop=False)
                    last = mm(bankC[:, 2, 0:D], hT_l[:, o], wd[:, 0:D], start=False, stop=(m == KF - 1))
                last.then_inc(p_dn, 1)

            pe.wait_ge(v_pack, 1)
            nc.tensor.transpose(bankA[0:8, 1, 0:NTAB], pack[0:NTAB, :], ident[0:NTAB, 0:NTAB]).then_inc(p_tab, 1)
            pe.wait_ge(v_wlo, 8)
            x_turn_f(0, 0, 0)
            up_product(0, 0)
            x_turn_f(1, 1, 0)
            h_turn(0)
            up_product(1, 0)
            pe.wait_ge(v_tab, 1)
            nt = pe.value_load(nt_i, min_val=MINT * NE, max_val=NT)

            def tile(t, ring, nth):
                x_turn_f(t + 1, ring, nth)
                par_before = pe.value_load(tpar_i[:, bass.ds(t - 1, 1)], min_val=0, max_val=1)
                down_product(t - 1, par_before)
                h_turn(t)

            def next_up(t):
                e = pe.value_load(te_i[:, bass.ds(t, 1)], min_val=0, max_val=NE - 1)
                par = pe.value_load(tpar_i[:, bass.ds(t, 1)], min_val=0, max_val=1)
                pe.wait_ge(v_wlo, 4 * e + 4)
                up_product(t, par)

            def last_down(t):
                par = pe.value_load(tpar_i[:, bass.ds(t, 1)], min_val=0, max_val=1)
                down_product(t, par)

            tile(1, 0, 1)
            next_up(2)
            with pe.Fori(1, NT // 2) as u:
                t = 2 * u
                with pe.If(nt > t):
                    tile(t, 1, u)
                    with pe.If(nt > t + 1):
                        next_up(t + 1)
                        tile(t + 1, 0, u + 1)
                        with pe.If(nt > t + 2):
                            next_up(t + 2)
                        with pe.If(nt < t + 3):
                            last_down(t + 1)
                    with pe.If(nt < t + 2):
                        last_down(t)


def kernel(**inputs):
    import numpy as np
    import concourse.bacc as bacc
    from concourse.bass_utils import run_bass_kernel_spmd

    a = {k: np.asarray(v_) for k, v_ in inputs.items()}
    ctx_ = a["ctx_1024"]
    up = a["L0_ffn_expert_up"].transpose(0, 2, 1).reshape(2 * NE, P, FF)
    down = a["L0_ffn_expert_down"].transpose(0, 2, 1).reshape(NE, 2, 4, P, D).transpose(0, 1, 3, 2, 4)
    arrays = {
        "x": a["x"].reshape(T, D),
        "ctx_t": ctx_.transpose(2, 0, 1).reshape(D, B * S),
        "ctx_t2": np.concatenate([ctx_, ctx_], axis=1).transpose(2, 0, 1).reshape(D, B * 2 * S),
        "wq": a["L0_xattn_Wq"], "wk": a["L0_xattn_Wk"], "wv": a["L0_xattn_Wv"], "we": a["L0_xattn_We"],
        "bqkv": np.stack([a[f"L0_xattn_b{n}"].reshape(KD, P) for n in "qkv"]).transpose(2, 0, 1).reshape(P, 3 * KD),
        "be": a["L0_xattn_be"],
        "router_w": a["L0_ffn_router_w"], "router_b": a["L0_ffn_router_b"],
        "up": up, "down": down.reshape(2 * NE, P, 4 * D),
        "const": constants(),
    }
    arrays = {k: np.ascontiguousarray(v_) for k, v_ in arrays.items()}
    nc = bacc.Bacc("TRN2", target_bir_lowering=False, num_devices=1)
    args = [nc.dram_tensor(k, v_.shape, mybir.dt.from_np(v_.dtype), kind="ExternalInput").ap()
            for k, v_ in arrays.items()]
    out = nc.dram_tensor("out", (T + P, D), F32, kind="ExternalOutput").ap()
    rows = nc.dram_tensor("rows", (T + P, XROW), F32, kind="Internal").ap()
    build(nc, *args, out, rows)
    r = run_bass_kernel_spmd(nc, [arrays], core_ids=[0])
    return r.results[0]["out"][0:T].reshape(B, L, D)
```

```python
from contextlib import ExitStack

import concourse.bass as bass
from concourse import mybir
from concourse.alu_op_type import AluOpType as ALU

F32 = mybir.dt.float32
F32R = mybir.dt.float32r
BF16 = mybir.dt.bfloat16
I32 = mybir.dt.int32
U32 = mybir.dt.uint32
ACT = mybir.ActivationFunctionType
AX_X = mybir.AxisListType.X

P = 128
B, L, D = 4, 512, 256
S, H, HE = 64, 16, 16
NE, FF, TOPK = 8, 1024, 2
T = B * L
LT = L // P
NTOK = T // P
KD = D // P
KF = FF // P
MINT = 2
NT = T * TOPK // P + MINT * (NE - TOPK)
NTAB = NT + 3
EPS = 1e-5
SCALE = HE ** -0.5
XROW = D + NE
COLS = NTOK
MAPC = NE * COLS + 32

_at = 0
CONST = {}
for _name, _n in (("ident", P), ("iota", P), ("upper", P), ("ones", P), ("head", 8), ("densel", 2 * 32),
                  ("tile", 1), ("tile2", 1), ("step", COLS - 1), ("flip", NE), ("token", NTOK), ("spare", 1),
                  ("power", 16), ("expert", NE), ("sel", 8 * P), ("feat", KD * P)):
    CONST[_name] = (_at, _at + _n)
    _at += _n
NCONST = _at
EARLY = CONST["sel"][0]


def constants():
    import numpy as np

    c = np.zeros((P, NCONST), np.float32)
    p = np.arange(P)

    def part(name):
        a, b = CONST[name]
        return c[:, a:b]

    part("ident")[:] = np.eye(P)
    part("iota")[:] = np.arange(P)
    part("upper")[:] = p[:, None] < p[None, :]
    part("ones")[:] = 1
    part("head")[:] = p[:, None] // HE == np.arange(8)
    sel = part("sel").reshape(P, 8, P)
    feat = part("feat").reshape(P, KD, P)
    for r in range(32):
        for j in range(8):
            sel[r, j] = (r % H) == 2 * j + p // S
        head = 8 * (r // 2 % 2) + 2 * (r // 4 % 4) + r % 2
        for k in range(KD):
            feat[r, k] = head == 8 * k + p // HE
    for k in range(2):
        for h in range(2):
            part("densel").reshape(P, 2, 32)[h * S:(h + 1) * S, k, 2 * k + h] = 1
    part("tile")[:] = p[:, None]
    part("tile2")[:] = p[:, None] - 2
    part("step")[:] = P * np.arange(1, COLS)
    part("flip")[:] = [0] + [1 if e % 2 else -1 for e in range(1, NE)]
    part("token")[:] = P * np.arange(NTOK) + p[:, None] - T
    part("spare")[:] = T + p[:, None]
    part("power")[:] = -0.5
    part("expert")[:] = np.arange(NE)
    return c


def build(nc, x, ctx_t, ctx_t2, wq, wk, wv, we, bqk, bv, be, router_w, router_b, up, down, const, out, rows):
    with ExitStack() as ctx:
        def sb(name, shape, dt=F32):
            return ctx.enter_context(nc.sbuf_tensor(name, shape, dt))

        def ps(name, shape, dt=F32):
            return ctx.enter_context(nc.psum_tensor(name, shape, dt))

        def sem(name):
            return ctx.enter_context(nc.semaphore(name))

        cst = sb("cst", [P, NCONST])

        def c(name):
            a, b = CONST[name]
            return cst[:, a:b]

        sel_r = sb("sel_r", [P, 8, P], F32R)
        feat_r = sb("feat_r", [P, KD, P], F32R)
        zero_r = sb("zero_r", [P, P], F32R)
        upper_bf = sb("upper_bf", [P, P], BF16)
        ones_bf = sb("ones_bf", [P, P], BF16)
        wq_h, wq_l = sb("wq_h", [P, KD, D], F32R), sb("wq_l", [P, KD, D], F32R)
        we_h, we_l = sb("we_h", [P, KD, D], F32R), sb("we_l", [P, KD, D], F32R)
        rw = sb("rw", [P, KD, 32])
        rb = sb("rb", [P, NE])
        be_b = sb("be_b", [P, D])
        bias = sb("bias", [P, 2, KD])
        bv_b = sb("bv_b", [P, D])
        v_b = sb("v_b", [P, D])
        ctxT = sb("ctxT", [P, KD, B * S])
        ctxT2 = sb("ctxT2", [P, KD, B, 2 * S])
        kT_h, kT_l = sb("kT_h", [P, KD, B * S]), sb("kT_l", [P, KD, B * S])
        v_all = sb("v_all", [P, B, D])
        xall = sb("xall", [P, NTOK, D])
        stat1 = sb("stat1", [P, NTOK, 6])
        mv1 = sb("mv1", [P, NTOK, 2])
        var1 = sb("var1", [P, NTOK])
        rstd1 = sb("rstd1", [P, NTOK])
        xn = sb("xn", [P, LT, D])
        xnT_h, xnT_l = sb("xnT_h", [P, KD, L], F32R), sb("xnT_l", [P, KD, L], F32R)
        q_h, q_l = sb("q_h", [P, KD, L], F32R), sb("q_l", [P, KD, L], F32R)
        kbd_h, kbd_l = sb("kbd_h", [P, KD, 8, S], F32R), sb("kbd_l", [P, KD, 8, S], F32R)
        vbd = sb("vbd", [P, 8, 32])
        nmax = sb("nmax", [P, LT, H])
        nmx = sb("nmx", [P, LT, P])
        nmxT = sb("nmxT", [P, L], F32R)
        prob = sb("prob", [P, 4, L])
        wraw = prob
        av = sb("av", [P, KD, L])
        den = sb("den", [P, L])
        rden = sb("rden", [P, LT, 4, 4])
        rdm = sb("rdm", [P, LT, P])
        rdT = sb("rdT", [P, L], F32R)
        at_h, at_l = sb("at_h", [P, KD, L], F32R), sb("at_l", [P, KD, L], F32R)
        stat2 = sb("stat2", [P, LT, 6])
        mv2 = sb("mv2", [P, LT, 2])
        var2 = sb("var2", [P, LT])
        rstd2 = sb("rstd2", [P, LT])
        xr = sb("xr", [P, LT, XROW])
        x2T = sb("x2T", [P, LT, KD, P])
        lg, lgs, ex, pr = (sb(n, [P, LT, NE]) for n in ("lg", "lgs", "ex", "pr"))
        lmax, lsum, lrec = (sb(n, [P, LT]) for n in ("lmax", "lsum", "lrec"))
        v8 = sb("v8", [P, LT, 8])
        i8 = sb("i8", [P, LT, 8], U32)
        ef = sb("ef", [P, TOPK, LT])
        mk = sb("mk", [P, TOPK, LT, NE])
        msum = sb("msum", [P, LT, NE])
        msum_bf = sb("msum_bf", [P, LT, NE], BF16)
        mtot = sb("mtot", [P, NE])
        seen = sb("seen", [P, NE])
        seen_bf = sb("seen_bf", [P, NE], BF16)
        lgT = sb("lgT", [P, P])
        pk = sb("pk", [P, TOPK, LT, NE])
        rank = sb("rank", [P, TOPK * LT])
        cmp = sb("cmp", [P, TOPK * LT, COLS - 1])
        ltile, lrow, key, val = (sb(n, [P, TOPK * LT]) for n in ("ltile", "lrow", "key", "val"))
        hot = sb("hot", [P, 4, P], F32R)
        put = sb("put", [P, 4, P], F32R)
        slot = sb("slot", [P, MAPC], I32)
        ntile, tend, tbeg = (sb(n, [P, NE]) for n in ("ntile", "tend", "tbeg"))
        big = sb("big", [P, NE, COLS - 1])
        on = sb("on", [P, NE])
        onb = sb("onb", [P, NE])
        onf = sb("onf", [P, NE])
        onf2 = sb("onf2", [P, NE])
        te1, tb, tone, tsec, tlt, par2, tsp, traw, pair = (
            sb(n, [P, 1]) for n in ("te1", "tb", "tone", "tsec", "tlt", "par2", "tsp", "traw", "pair"))
        pack = sb("pack", [P, 8])
        tab = sb("tab", [8, NTAB], I32)
        w_i, tcol_i, split_i, te_i, tpar_i = (tab[i:i + 1, :] for i in range(5))
        nt_i = tab[5:6, 0:1]
        raw01 = sb("raw01", [P, 2, 1024])
        up_w = sb("up_w", [P, 2, 2, KD, FF], F32R)
        dn_w = sb("dn_w", [P, 2, KF, 2, D], F32R)
        idx_g = sb("idx_g", [P, 2], I32)
        idx_s = sb("idx_s", [P, 1], I32)
        gate = sb("gate", [P, NTAB])
        prime = sb("prime", [P, 14])
        raw = xall[:, :, :].rearrange("p t d -> p (t d)")
        hbuf = raw01[:, 0, :]
        y = x2T[:, 0, :, :].rearrange("p k l -> p (k l)")
        osb = x2T[:, 1, :, :].rearrange("p k l -> p (k l)")
        xT_h, xT_l = xnT_h[:, 0, 0:D], xnT_l[:, 0, 0:D]
        hT_h = q_h[:, :, :].rearrange("p k l -> p (k l)")
        hT_l = q_l[:, :, :].rearrange("p k l -> p (k l)")

        bankM = ps("bankM", [P, 512])
        bankA = ps("bankA", [P, 2, 512])
        bankB0 = ps("bankB0", [P, 512])
        bankB1 = ps("bankB1", [P, 512])
        bankC = ps("bankC", [P, 3, 512])
        bankB = [bankB0, bankB1]

        d_const, d_sel, d_x0, d_x, d_zero = (sem(n) for n in ("d_const", "d_sel", "d_x0", "d_x", "d_zero"))
        d_k, d_q, d_v, d_we, d_w = (sem(n) for n in ("d_k", "d_q", "d_v", "d_we", "d_w"))
        d_x1, d_rows = sem("d_x1"), sem("d_rows")
        d_raw01, d_rawu, d_rawd = sem("d_raw01"), sem("d_rawu"), sem("d_rawd")
        d_gather = [sem("d_gather0"), sem("d_gather1")]
        d_add = sem("d_add")
        a_const, a_wsplit, a_k, a_v, a_xT, a_q, a_nmT, a_exp = (
            sem(n) for n in "a_const a_wsplit a_k a_v a_xT a_q a_nmT a_exp".split())
        a_av, a_den, a_rdT, a_at, a_x2T, a_ex, a_lgT, a_w01 = (
            sem(n) for n in "a_av a_den a_rdT a_at a_x2T a_ex a_lgT a_w01".split())
        a_fxT, a_fhT, a_gelu, a_osb, a_whi = (
            sem(n) for n in "a_fxT a_fhT a_gelu a_osb a_whi".split())
        v_wsplit, v_k, v_stat1, v_var1, v_xn, v_xT, v_q, v_max = (
            sem(n) for n in "v_wsplit v_k v_stat1 v_var1 v_xn v_xT v_q v_max".split())
        v_nmh, v_nml, v_rden, v_rdh, v_rdl, v_att, v_at, v_x1 = (
            sem(n) for n in "v_nmh v_nml v_rden v_rdh v_rdl v_att v_at v_x1".split())
        v_stat2, v_var2, v_xn2, v_lg, v_pr, v_top, v_mk, v_msum = (
            sem(n) for n in "v_stat2 v_var2 v_xn2 v_lg v_pr v_top v_mk v_msum".split())
        v_seen, v_comb, v_mbf, v_mtot, v_pos, v_key, v_hot, v_put = (
            sem(n) for n in "v_seen v_comb v_mbf v_mtot v_pos v_key v_hot v_put".split())
        v_pack, v_tab, v_slot, v_done, v_fxT, v_gate, v_fhT, v_y = (
            sem(n) for n in "v_pack v_tab v_slot v_done v_fxT v_gate v_fhT v_y".split())
        v_wlo, = (
            sem(n) for n in "v_wlo".split())
        g_zero, g_kbd, g_vbd, g_rstd1, g_res, g_rstd2, g_rw, g_w01 = (
            sem(n) for n in "g_zero g_kbd g_vbd g_rstd1 g_res g_rstd2 g_rw g_w01".split())
        g_gi, g_si, g_at, g_vb = (
            sem(n) for n in "g_gi g_si g_at g_vb".split())
        p_kv, p_xT, p_q, p_s, p_nmT, p_sT, p_av, p_denT = (
            sem(n) for n in "p_kv p_xT p_q p_s p_nmT p_sT p_av p_denT".split())
        p_rdT, p_bc, p_proj, p_x2T, p_lg, p_pos, p_map, p_lgT = (
            sem(n) for n in "p_rdT p_bc p_proj p_x2T p_lg p_pos p_map p_lgT".split())
        p_fin, p_tab, p_fxT, p_fhT, p_up, p_dn = (
            sem(n) for n in "p_fin p_tab p_fxT p_fhT p_up p_dn".split())

        block = ctx.enter_context(nc.Block())

        @block.sync
        def _(sp):
            x_t = x.rearrange("(t p) d -> p t d", p=P)
            sp.dma_start(xall[:, 0:LT, :], x_t[:, 0:LT, :]).then_inc(d_x0, 16)
            sp.dma_start(cst[:, 0:EARLY], const[:, 0:EARLY]).then_inc(d_const, 16)

            def rows_of(a):
                return a.rearrange("(k p) n -> p k n", p=P)

            def raw_w(n):
                return wraw[:, n, :].rearrange("p (k n) -> p k n", k=KD)

            sp.dma_start(raw_w(1), rows_of(wk)).then_inc(d_k, 16)
            sp.dma_start(ctxT[:, :, :], rows_of(ctx_t)).then_inc(d_k, 16)
            sp.dma_start(bias[:, :, :], bqk.rearrange("p (j k) -> p j k", k=KD)).then_inc(d_k, 16)
            sp.dma_start(raw_w(0), rows_of(wq)).then_inc(d_q, 16)
            sp.dma_start(xall[:, LT:NTOK, :], x_t[:, LT:NTOK, :]).then_inc(d_x, 16)
            sp.dma_start(raw_w(2), rows_of(wv)).then_inc(d_v, 16)
            sp.dma_start(ctxT2[:, :, :, :].rearrange("p k b s -> p k (b s)"), rows_of(ctx_t2)).then_inc(d_v, 16)
            sp.dma_start(raw_w(3), rows_of(we)).then_inc(d_we, 16)
            sp.dma_start(cst[:, EARLY:NCONST], const[:, EARLY:NCONST]).then_inc(d_sel, 16)
            sp.wait_ge(g_rw, 1)
            sp.dma_start(rw[:, :, 0:NE], rows_of(router_w)).then_inc(d_w, 16)
            sp.dma_start(bv_b[:, :], bv.rearrange("(a n) -> a n", a=1).broadcast_to([P, D])).then_inc(d_w, 16)
            sp.dma_start(be_b[:, :], be.rearrange("(a n) -> a n", a=1).broadcast_to([P, D])).then_inc(d_w, 16)
            sp.dma_start(rb[:, :], router_b.rearrange("(a n) -> a n", a=1).broadcast_to([P, NE])).then_inc(d_w, 16)
            sp.wait_ge(g_zero, 2)
            zeros = zero_r[:, :].bitcast(F32)
            zeros_d = zeros.rearrange("p (a n) -> p a n", a=1).broadcast_to([P, KD, P])
            sp.dma_start(rows[T:T + P, 0:D].rearrange("p (a n) -> p a n", a=KD), zeros_d).then_inc(d_zero, 16)
            sp.dma_start(rows[T:T + P, D:XROW], zeros[:, 0:NE]).then_inc(d_zero, 16)
            sp.dma_start(out[T:T + P, :].rearrange("p (a n) -> p a n", a=KD), zeros_d).then_inc(d_zero, 16)

            def load01(i):
                if not (isinstance(i, int) and i == 0):
                    sp.wait_ge(g_w01, 2 * i)
                sp.dma_start(raw01[:, 0, :], up[bass.ds(i, 1)].rearrange("a p n -> (a p) n")).then_inc(d_raw01, 16)
                sp.dma_start(raw01[:, 1, :], down[bass.ds(i, 1)].rearrange("a p n -> (a p) n")).then_inc(d_raw01, 16)

            def store(g):
                sp.wait_ge(v_x1, 2 * g + 2)
                sp.dma_start(out[bass.ds(g * L, L), :].rearrange("(t p) d -> p t d", p=P),
                             xall[:, bass.ds(g * LT, LT), :]).then_inc(d_x1, 16)
                sp.wait_ge(v_comb, g + 1)
                sp.dma_start(rows[bass.ds(g * L, L), :].rearrange("(t p) d -> p t d", p=P),
                             xr[:, :, :]).then_inc(d_rows, 16)

            load01(0)
            with sp.Fori(1, B) as i:
                load01(i)
                store(i - 1)
            store(B - 1)
            sp.wait_ge(d_x1, 16 * B)
            for e in range(2, NE):
                if e > 2:
                    sp.wait_ge(v_wlo, 8 + 4 * (e - 2))
                sp.dma_start(raw[:, 0:2048].rearrange("p (h n) -> p h n", h=2), up[2 * e:2 * e + 2].rearrange("h p n -> p h n"))\
                    .then_inc(d_rawu, 16)
                sp.dma_start(raw[:, 2048:4096].rearrange("p (h n) -> p h n", h=2), down[2 * e:2 * e + 2].rearrange("h p n -> p h n"))\
                    .then_inc(d_rawd, 16)

        @block.gpsimd
        def _(pool):
            g = nc.gpsimd
            g.memset(rw[:, :, :], 0.0).then_inc(g_rw, 1)
            g.memset(prime[:, 3:4], 0.0).then_inc(g_zero, 1)
            g.memset(zero_r[:, :].bitcast(F32), 0.0).then_inc(g_zero, 1)
            g.memset(nmx[:, :, :], 0.0).then_inc(g_zero, 1)
            g.memset(rdm[:, :, :], 0.0).then_inc(g_zero, 1)

            def rstd(out_, var_, n):
                return g.tensor_tensor(out_, var_, c("power")[:, 0:n], ALU.pow)

            def att_low(b):
                pool.wait_ge(a_at, KD * b + 2)
                g.tensor_tensor(at_l[:, 1, :], av[:, 1, :], at_h[:, 1, :].bitcast(F32), ALU.subtract)\
                    .then_inc(g_at, 1)

            def halves_rstd2(b):
                for n in range(2):
                    pool.wait_ge(v_var2, 2 * b + n + 1)
                    rstd(rstd2[:, 2 * n:2 * n + 2], var2[:, 2 * n:2 * n + 2], 2).then_inc(g_rstd2, 1)

            def key_blocks(b):
                pool.wait_ge(a_k, 2)
                pool.wait_ge(v_k, 2)
                if not (isinstance(b, int) and b == 0):
                    pool.wait_ge(p_sT, 8 * b)
                for part, src in ((kbd_h, kT_h), (kbd_l, kT_l)):
                    for k in range(KD):
                        cols = src[:, k, bass.ds(b * S, S)].rearrange("p (a s) -> p a s", a=1)
                        g.tensor_tensor(part[:, k, :, :], cols.broadcast_to([P, 8, S]),
                                        c("head").rearrange("p (h a) -> p h a", a=1).broadcast_to([P, 8, S]),
                                        ALU.mult).then_inc(g_kbd, 1)

            def value_blocks(b):
                pool.wait_ge(a_v, 2)
                if not (isinstance(b, int) and b == 0):
                    pool.wait_ge(p_av, 16 * b)
                g.tensor_tensor(v_b[:, :], v_all[:, bass.ds(b, 1), :].rearrange("p a n -> p (a n)"), bv_b[:, :], ALU.add)\
                    .then_inc(g_vb, 1)
                pool.wait_ge(g_vb, b + 1)
                g.tensor_tensor(vbd[:, :, :].rearrange("p j (h e) -> p j h e", h=2),
                                v_b[:, :].rearrange("p (j h e) -> p j h e", h=2, e=HE),
                                c("densel")[:, 0:2].rearrange("p (a h b) -> p a h b", a=1, b=1)
                                .broadcast_to([P, 8, 2, HE]), ALU.mult).then_inc(g_vbd, 1)

            def low01(i):
                pool.wait_ge(d_raw01, 32 * (i + 1))
                pool.wait_ge(a_w01, 2 * (i + 1))
                g.tensor_tensor(up_flat[:, 1, bass.ds(i, 1), :], raw01[:, 0:1, :],
                                up_flat[:, 0, bass.ds(i, 1), :].bitcast(F32), ALU.subtract).then_inc(g_w01, 1)
                g.tensor_tensor(dn_flat[:, bass.ds(4 * i, 4), 1, :],
                                raw01[:, 1, :].rearrange("p (c n) -> p c n", c=4),
                                dn_flat[:, bass.ds(4 * i, 4), 0, :].bitcast(F32), ALU.subtract).then_inc(g_w01, 1)

            up_flat = up_w[:, :, :, :, :].rearrange("p h b k n -> p h (b k) n")
            dn_flat = dn_w[:, :, :, :, :].rearrange("p b k h n -> p (b k) h n")

            def residual(b):
                pool.wait_ge(v_xn, LT * (b + 1))
                g.tensor_tensor(xall[:, bass.ds(b * LT, LT), :], xall[:, bass.ds(b * LT, LT), :],
                                be_b[:, :].rearrange("p (a n) -> p a n", a=1).broadcast_to([P, LT, D]),
                                ALU.add).then_inc(g_res, 1)

            pool.wait_ge(d_const, 16)
            pool.wait_ge(v_var1, 1)
            rstd(rstd1[:, 0:LT], var1[:, 0:LT], LT).then_inc(g_rstd1, 1)
            pool.wait_ge(g_zero, 4)
            key_blocks(0)
            pool.wait_ge(d_w, 64)
            residual(0)
            value_blocks(0)
            pool.wait_ge(v_var1, 2)
            rstd(rstd1[:, LT:NTOK], var1[:, LT:NTOK], NTOK - LT).then_inc(g_rstd1, 1)
            low01(0)
            def settle():
                g.tensor_tensor(prime[0:1, 2:3], prime[0:1, 3:4], prime[0:1, 3:4], ALU.add)

            with pool.Fori(1, B) as i:
                key_blocks(i)
                residual(i)
                att_low(i - 1)
                halves_rstd2(i - 1)
                value_blocks(i)
                low01(i)
            halves_rstd2(B - 1)
            pool.wait_ge(v_slot, 2)
            pool.wait_ge(d_rows, 16 * B)
            pool.wait_ge(d_zero, 48)
            pool.wait_ge(d_x1, 16 * B)

            def gather(t, ring, nth, col=None):
                if col is None:
                    col = pool.value_load(tcol_i[:, bass.ds(t, 1)], min_val=0, max_val=MAPC - 1)
                if not (isinstance(t, int) and t < 2):
                    pool.wait_ge(d_gather[ring], 16 * nth)
                g.tensor_copy(idx_g[:, ring:ring + 1], slot[:, bass.ds(col, 1)]).then_inc(g_gi, 1)
                pool.wait_ge(g_gi, t + 1)
                if not (isinstance(t, int) and t < 2):
                    pool.wait_ge(p_fxT, t - 1)
                    pool.wait_ge(v_gate, t - 1)
                settle()
                g.indirect_dma_start(xr[:, ring, :], None, rows, bass.IndirectOffsetOnAxis(idx_g[:, ring:ring + 1], 0),
                                     bounds_check=T + P - 1).then_inc(d_gather[ring], 16)

            def add(t):
                col = pool.value_load(tcol_i[:, bass.ds(t, 1)], min_val=0, max_val=MAPC - 1)
                if not (isinstance(t, int) and t == 0):
                    pool.wait_ge(d_add, 16 * t)
                g.tensor_copy(idx_s[:, :], slot[:, bass.ds(col, 1)]).then_inc(g_si, 1)
                pool.wait_ge(g_si, t + 1)
                pool.wait_ge(v_y, t + 1)
                settle()
                g.indirect_dma_start(out, bass.IndirectOffsetOnAxis(idx_s[:, 0:1], 0), y, None,
                                     bounds_check=T + P - 1, compute_op=ALU.add).then_inc(d_add, 16)

            gather(0, 0, 0, col=0)
            gather(1, 1, 0, col=1)
            pool.wait_ge(v_tab, 1)
            nt = pool.value_load(nt_i, min_val=MINT * NE, max_val=NT)
            gather(2, 0, 1)
            gather(3, 1, 1)
            add(0)
            with pool.Fori(1, NT // 2) as u:
                t = 2 * u
                with pool.If(nt > t):
                    gather(t + 2, 0, u + 1)
                    add(t - 1)
                    with pool.If(nt > t + 1):
                        gather(t + 3, 1, u + 1)
                        add(t)
                        with pool.If(nt < t + 3):
                            add(t + 1)
                    with pool.Else():
                        add(t)
            pool.wait_ge(d_add, 16 * nt)

        @block.scalar
        def _(act):
            a = nc.scalar

            def attention_constants():
                act.wait_ge(d_const, 16)
                a.activation(upper_bf[:, :], c("upper"), ACT.Identity).then_inc(a_const, 1)
                a.activation(ones_bf[:, :], c("ones"), ACT.Identity).then_inc(a_const, 1)
                act.wait_ge(d_sel, 16)
                a.activation(sel_r[:, :, :], c("sel").rearrange("p (j n) -> p j n", j=8), ACT.Identity)\
                    .then_inc(a_const, 1)
                a.activation(feat_r[:, :, :], c("feat").rearrange("p (j n) -> p j n", j=KD), ACT.Identity)\
                    .then_inc(a_const, 1)

            def weight_high(part, n):
                a.activation(part[:, :, :], wraw[:, n, :].rearrange("p (k n) -> p k n", k=KD), ACT.Identity)\
                    .then_inc(a_wsplit, 1)

            def keys():
                for k in range(KD):
                    act.wait_ge(p_kv, k + 1)
                    act.wait_ge(d_k, 48)
                    a.activation(kT_h[:, k, :].bitcast(F32R), bankC[:, k, 0:B * S], ACT.Identity, bias=bias[:, 1, k:k + 1])\
                        .then_inc(a_k, 1)

            def values(n):
                act.wait_ge(p_kv, 3 + n)
                a.activation(v_all[:, 2 * n:2 * n + 2, :].rearrange("p b d -> p (b d)"), bankA[:, n, :], ACT.Identity)\
                    .then_inc(a_v, 1)

            def x_high(b, n):
                act.wait_ge(p_xT, 2 * b + n + 1)
                a.activation(xnT_h[:, :, n * 256:(n + 1) * 256].rearrange("p k (t l) -> p t k l", t=2),
                     bankB1[:, :].rearrange("p (t k l) -> p t k l", t=2, k=KD), ACT.Identity).then_inc(a_xT, 1)

            def q_high(b):
                for n, k in enumerate((1, 0)):
                    act.wait_ge(p_q, KD * b + n + 1)
                    a.activation(q_h[:, k, :], bankB[k][:, :], ACT.Identity, bias=bias[:, 0, k:k + 1])\
                        .then_inc(a_q, 1)

            def max_turn(b):
                act.wait_ge(p_nmT, b + 1)
                a.activation(nmxT[:, :], bankC[:, 2, :], ACT.Identity).then_inc(a_nmT, 1)

            def exps(b, js):
                for j in js:
                    act.wait_ge(p_sT, 8 * b + j + 1)
                    if j >= 4:
                        act.wait_ge(p_av, 16 * b + 2 * (j - 3))
                    elif not (isinstance(b, int) and b == 0):
                        act.wait_ge(p_av, 16 * b)
                    a.activation(prob[:, j % 4, :], bankC[:, j % 3, :], ACT.Exp, scale=SCALE).then_inc(a_exp, 1)

            def den_copy(b):
                act.wait_ge(p_av, 16 * b + 16)
                a.activation(den[:, :], bankB0[:, :], ACT.Identity).then_inc(a_den, 1)

            def av_copy(b, k):
                act.wait_ge(p_av, 16 * b + 8 * k + 8)
                a.activation(av[:, k, :], bankA[:, k, :], ACT.Identity).then_inc(a_av, 1)

            def rden_turn(b):
                act.wait_ge(p_rdT, b + 1)
                a.activation(rdT[:, :], bankA[:, 1, :], ACT.Identity).then_inc(a_rdT, 1)

            def att_high(b):
                for k in range(KD):
                    act.wait_ge(v_att, KD * b + k + 1)
                    a.activation(at_h[:, k, :], av[:, k, :], ACT.Identity).then_inc(a_at, 1)

            def x2_turn(b):
                for n in range(2):
                    act.wait_ge(p_x2T, 2 * b + n + 1)
                    a.activation(x2T[:, 2 * n:2 * n + 2, :, :].rearrange("p t k l -> p (t k l)"), bankA[:, n, :], ACT.Identity)\
                        .then_inc(a_x2T, 1)

            def logit_copy(b):
                act.wait_ge(p_lg, b + 1)
                a.activation(lgT[:, :], bankB0[:, 0:P], ACT.Identity).then_inc(a_lgT, 1)

            def router_exp(b):
                act.wait_ge(v_lg, 3 * b + 3)
                a.activation(ex[:, :, :], lgs[:, :, :], ACT.Exp).then_inc(a_ex, 1)

            def high01(i):
                act.wait_ge(d_raw01, 32 * (i + 1))
                a.activation(up_flat[:, 0, bass.ds(i, 1), :], raw01[:, 0:1, :], ACT.Identity).then_inc(a_w01, 1)
                a.activation(dn_flat[:, bass.ds(4 * i, 4), 0, :], raw01[:, 1, :].rearrange("p (c n) -> p c n", c=4), ACT.Identity)\
                    .then_inc(a_w01, 1)

            up_flat = up_w[:, :, :, :, :].rearrange("p h b k n -> p h (b k) n")
            dn_flat = dn_w[:, :, :, :, :].rearrange("p b k h n -> p (b k) h n")

            keys()
            act.wait_ge(d_q, 16)
            weight_high(wq_h, 0)
            x_high(0, 0)
            x_high(0, 1)
            q_high(0)
            values(0)
            attention_constants()
            act.wait_ge(d_we, 16)
            weight_high(we_h, 3)
            high01(0)
            values(1)
            max_turn(0)
            act.wait_ge(v_wsplit, 2)
            act.wait_ge(p_kv, 4)
            exps(0, range(4))

            def batch(i):
                av_copy(i - 1, 0)
                x_high(i, 0)
                exps(i - 1, range(4, 8))
                x_high(i, 1)
                den_copy(i - 1)
                av_copy(i - 1, 1)
                q_high(i)
                rden_turn(i - 1)
                att_high(i - 1)
                high01(i)
                max_turn(i)
                exps(i, range(4))
                x2_turn(i - 1)
                logit_copy(i - 1)
                router_exp(i - 1)

            with act.Fori(1, B) as i:
                batch(i)
            av_copy(B - 1, 0)
            exps(B - 1, range(4, 8))
            den_copy(B - 1)
            av_copy(B - 1, 1)
            rden_turn(B - 1)
            att_high(B - 1)
            x2_turn(B - 1)
            logit_copy(B - 1)
            router_exp(B - 1)

            a.activation(prime[:, 0:1], c("ones")[:, 0:1], ACT.Gelu).then_inc(a_whi, 8)

            def x_high_f(t):
                act.wait_ge(p_fxT, t + 1)
                a.activation(xT_h, bankA[:, 0, 0:D], ACT.Identity).then_inc(a_fxT, 1)

            def h_high(t):
                for n in range(2):
                    act.wait_ge(p_fhT, 2 * t + n + 1)
                    a.activation(hT_h[:, n * 512:(n + 1) * 512], bankB[n][:, :], ACT.Identity).then_inc(a_fhT, 1)

            def gelu(t, n):
                act.wait_ge(p_up, 2 * t + n + 1)
                a.activation(hbuf[:, n * 512:(n + 1) * 512], bankC[:, n, :], ACT.Gelu).then_inc(a_gelu, 1)

            def low_part(t):
                act.wait_ge(p_dn, t + 1)
                act.wait_ge(v_gate, t + 1)
                a.activation(osb, bankC[:, 2, D:2 * D], ACT.Identity, scale=gate[:, bass.ds(t, 1)]).then_inc(a_osb, 1)

            def weights_high(sp_e, other, nraw, half):
                with act.If(sp_e > 1):
                    act.wait_ge(d_rawd if half else d_rawu, 16 * nraw)
                    for n in range(2):
                        if half:
                            a.activation(dn_w[:, bass.ds(other, 1), 4 * n:4 * n + 4, 0, :].rearrange("p a c n -> p (a c) n"),
                                 raw[:, 2048 + n * 1024:2048 + (n + 1) * 1024].rearrange("p (c n) -> p c n", c=4), ACT.Identity)\
                                     .then_inc(a_whi, 1)
                        else:
                            a.activation(up_w[:, 0, bass.ds(other, 1), n, :], raw[:, n * FF:(n + 1) * FF], ACT.Identity)\
                                .then_inc(a_whi, 1)

            x_high_f(0)
            gelu(0, 0)
            x_high_f(1)
            gelu(0, 1)
            h_high(0)
            act.wait_ge(v_tab, 1)
            nt = act.value_load(nt_i, min_val=MINT * NE, max_val=NT)

            def tile(t):
                gelu(t, 0)
                x_high_f(t + 1)
                gelu(t, 1)
                split = act.value_load(split_i[:, bass.ds(t, 1)], min_val=2, max_val=127)
                sp_e, other, nraw = split // 16, 1 - split % 2, split // 2 % 8
                weights_high(sp_e, other, nraw, 0)
                low_part(t - 1)
                h_high(t)
                weights_high(sp_e, other, nraw, 1)

            tile(1)
            with act.Fori(1, NT // 2) as u:
                t = 2 * u
                with act.If(nt > t):
                    tile(t)
                    with act.If(nt > t + 1):
                        tile(t + 1)
                        with act.If(nt < t + 3):
                            low_part(t + 1)
                    with act.Else():
                        low_part(t)
        @block.vector
        def _(dve):
            v = nc.vector

            v.memset(seen[:, :], 0.0).then_inc(v_seen, 1)
            v.memset(seen_bf[:, :], 0.0).then_inc(v_seen, 1)

            def settle(n):
                v.memset(prime[:, n:n + 1], 0.0)

            def stats1(t0, n, tiles_per):
                for k in range(n):
                    v.bn_stats(stat1[:, t0 + k, :], xall[:, t0 + k, :]).then_inc(v_stat1, 1)

            def aggr1(t0, n, base):
                for k in range(n):
                    dve.wait_ge(v_stat1, base + k + 1)
                    v.bn_aggr(mv1[:, t0 + k, :], stat1[:, t0 + k, :]).then_inc(v_stat1, 1)
                dve.wait_ge(v_stat1, base + 2 * n)
                v.tensor_scalar(var1[:, t0:t0 + n], mv1[:, t0:t0 + n, 1], EPS, None, ALU.add).then_inc(v_var1, 1)

            def norm1(b):
                if isinstance(b, int) and b == 0:
                    dve.wait_ge(g_rstd1, 1)
                else:
                    dve.wait_ge(g_rstd1, 2)
                    dve.wait_ge(p_xT, 2 * b)
                for k in range(LT):
                    tt = b * LT + k
                    v.tensor_scalar(xn[:, k, :], xall[:, bass.ds(tt, 1), :].rearrange("p a d -> p (a d)"),
                                        mv1[:, bass.ds(tt, 1), 0], rstd1[:, bass.ds(tt, 1)],
                                        ALU.subtract, ALU.mult).then_inc(v_xn, 1)

            def x_low(b, n):
                dve.wait_ge(a_xT, 2 * b + n + 1)
                o = slice(n * 256, (n + 1) * 256)
                v.tensor_tensor(xnT_l[:, :, o].rearrange("p k (t l) -> p t k l", t=2),
                                    bankB1[:, :].rearrange("p (t k l) -> p t k l", t=2, k=KD),
                                    xnT_h[:, :, o].bitcast(F32).rearrange("p k (t l) -> p t k l", t=2),
                                    ALU.subtract).then_inc(v_xT, 1)

            def q_low(b):
                for n, k in enumerate((1, 0)):
                    dve.wait_ge(a_q, KD * b + n + 1)
                    v.scalar_tensor_tensor(out=q_l[:, k, :], in0=bankB[k][:, :], scalar=bias[:, 0, k:k + 1],
                                               in1=q_h[:, k, :].bitcast(F32), op0=ALU.add, op1=ALU.subtract)\
                                                   .then_inc(v_q, 1)

            def maxima(b, t):
                for k in range(KD):
                    n = KD * t + k
                    dve.wait_ge(p_s, 8 * b + n + 1)
                    v.tensor_reduce(nmax[:, t, 8 * k:8 * k + 8],
                                        bankC[:, n % 3, :].rearrange("p (h s) -> p h s", h=8), AX_X, ALU.max,
                                        negate=True).then_inc(v_max, 1)

            def max_split(b):
                dve.wait_ge(v_max, 8 * b + 8)
                v.tensor_copy(nmx[:, :, 0:H].bitcast(F32R), nmax[:, :, :]).then_inc(v_nmh, 1)
                dve.wait_ge(v_nmh, b + 1)
                v.tensor_tensor(nmx[:, :, H:2 * H].bitcast(F32R), nmax[:, :, :], nmx[:, :, 0:H], ALU.subtract)\
                    .then_inc(v_nml, 1)

            def rden_split(b):
                dve.wait_ge(p_denT, b + 1)
                dv = bankA[:, 0, :].rearrange("p (t i r) -> p t i r", t=LT, i=4)[:, :, :, 0:4]
                v.reciprocal(rden[:, :, :, :], dv).then_inc(v_rden, 1)
                dve.wait_ge(v_rden, b + 1)
                hi = rdm[:, :, 0:H].rearrange("p t (i r) -> p t i r", i=4)
                lo = rdm[:, :, H:2 * H].rearrange("p t (i r) -> p t i r", i=4)
                v.tensor_copy(hi.bitcast(F32R), rden[:, :, :, :]).then_inc(v_rdh, 1)
                dve.wait_ge(v_rdh, b + 1)
                v.tensor_tensor(lo.bitcast(F32R), rden[:, :, :, :], hi, ALU.subtract).then_inc(v_rdl, 1)

            def att(b):
                for k in range(KD):
                    dve.wait_ge(a_av, KD * b + k + 1)
                    dve.wait_ge(p_bc, KD * b + k + 1)
                    v.tensor_tensor(av[:, k, :], bankA[:, k, :], av[:, k, :], ALU.mult).then_inc(v_att, 1)

            def att_low(b, parts):
                for k in parts:
                    dve.wait_ge(a_at, KD * b + k + 1)
                    v.tensor_tensor(at_l[:, k, :], av[:, k, :], at_h[:, k, :].bitcast(F32), ALU.subtract)\
                        .then_inc(v_at, 1)

            def residual_norm2(b):
                dve.wait_ge(g_res, b + 1)
                for n in range(2):
                    dve.wait_ge(p_proj, 2 * b + n + 1)
                    xs = xall[:, bass.ds(b * LT + 2 * n, 2), :]
                    v.tensor_tensor(xs, bankB[n][:, :].rearrange("p (t d) -> p t d", t=2), xs, ALU.add)\
                        .then_inc(v_x1, 1)
                    dve.wait_ge(v_x1, 2 * b + n + 1)
                    settle(5)
                    for k in (2 * n, 2 * n + 1):
                        v.bn_stats(stat2[:, k, :], xall[:, bass.ds(b * LT + k, 1), :]
                                   .rearrange("p a d -> p (a d)")).then_inc(v_stat2, 1)
                    dve.wait_ge(v_stat2, 8 * b + 4 * n + 2)
                    settle(6)
                    for k in (2 * n, 2 * n + 1):
                        v.bn_aggr(mv2[:, k, :], stat2[:, k, :]).then_inc(v_stat2, 1)
                    dve.wait_ge(v_stat2, 8 * b + 4 * n + 4)
                    v.tensor_scalar(var2[:, 2 * n:2 * n + 2], mv2[:, 2 * n:2 * n + 2, 1], EPS, None, ALU.add)\
                        .then_inc(v_var2, 1)
                if not (isinstance(b, int) and b == 0):
                    dve.wait_ge(d_rows, 16 * b)
                for k in range(LT):
                    dve.wait_ge(g_rstd2, 2 * b + k // 2 + 1)
                    v.tensor_scalar(xr[:, k, 0:D], xall[:, bass.ds(b * LT + k, 1), :].rearrange("p a d -> p (a d)"),
                                    mv2[:, k, 0:1], rstd2[:, k:k + 1], ALU.subtract, ALU.mult).then_inc(v_xn2, 1)

            def bc3(ap, n):
                return ap.rearrange("p (q a) -> p q a", a=1).broadcast_to([P, ap.shape[1], n])

            def logits(b):
                dve.wait_ge(p_lgT, b + 1)
                v.tensor_tensor(lg[:, :, :], bankB0[:, P:2 * P].rearrange("p (t e) -> p t e", t=LT)[:, :, 0:NE],
                                    rb[:, :].rearrange("p (a e) -> p a e", a=1).broadcast_to([P, LT, NE]), ALU.add)\
                                        .then_inc(v_lg, 1)
                dve.wait_ge(v_lg, 3 * b + 1)
                v.tensor_reduce(lmax[:, :], lg[:, :, :], AX_X, ALU.max, negate=True).then_inc(v_lg, 1)
                dve.wait_ge(v_lg, 3 * b + 2)
                v.tensor_tensor(lgs[:, :, :], lg[:, :, :], bc3(lmax[:, :], NE), ALU.add).then_inc(v_lg, 1)

            def router(b):
                dve.wait_ge(a_ex, b + 1)
                v.tensor_reduce(lsum[:, :], ex[:, :, :], AX_X, ALU.add).then_inc(v_pr, 1)
                dve.wait_ge(v_pr, 3 * b + 1)
                v.reciprocal(lrec[:, :], lsum[:, :]).then_inc(v_pr, 1)
                dve.wait_ge(v_pr, 3 * b + 2)
                v.tensor_tensor(pr[:, :, :], ex[:, :, :], bc3(lrec[:, :], NE), ALU.mult).then_inc(v_pr, 1)
                dve.wait_ge(v_pr, 3 * b + 3)
                settle(7)
                for t in range(LT):
                    v.max(out=v8[:, t, :], in_=pr[:, t, :]).then_inc(v_top, 1)
                dve.wait_ge(v_top, 8 * b + LT)
                settle(8)
                for t in range(LT):
                    v.max_index(i8[:, t, :], v8[:, t, :], pr[:, t, :]).then_inc(v_top, 1)
                dve.wait_ge(v_top, 8 * b + 8)
                v.tensor_copy(ef[:, :, :], i8[:, :, 0:TOPK].rearrange("p t k -> p k t")).then_inc(v_mk, 1)
                dve.wait_ge(v_mk, 2 * b + 1)
                v.tensor_tensor(mk[:, :, :, :].rearrange("p k t e -> p (k t) e"),
                                    c("expert").rearrange("p (a e) -> p a e", a=1).broadcast_to([P, TOPK * LT, NE]),
                                    bc3(ef[:, :, :].rearrange("p k t -> p (k t)"), NE), ALU.is_equal)\
                                        .then_inc(v_mk, 1)
                dve.wait_ge(v_mk, 2 * b + 2)
                v.tensor_tensor(msum_bf[:, :, :], mk[:, 0, :, :], mk[:, 1, :, :], ALU.add).then_inc(v_mbf, 1)
                v.tensor_tensor(msum[:, :, :], mk[:, 0, :, :], mk[:, 1, :, :], ALU.add).then_inc(v_msum, 1)
                dve.wait_ge(v_msum, b + 1)
                v.tensor_tensor(xr[:, :, D:XROW], pr[:, :, :], msum[:, :, :], ALU.mult).then_inc(v_comb, 1)

            def count(b):
                v.tensor_reduce(mtot[:, :], msum[:, :, :].rearrange("p t e -> p e t"), AX_X, ALU.add)\
                    .then_inc(v_mtot, 1)
                dve.wait_ge(v_mtot, b + 1)
                dve.wait_ge(p_pos, b + 1)
                v.tensor_tensor(seen[:, :], seen[:, :], mtot[:, :], ALU.add).then_inc(v_seen, 1)
                dve.wait_ge(v_seen, 2 * b + 3)
                v.tensor_copy(seen_bf[:, :], seen[:, :]).then_inc(v_seen, 1)

            def ranks(b, counts):
                dve.wait_ge(p_pos, b + 1)
                v.tensor_tensor(pk[:, :, :, :], mk[:, :, :, :],
                                    counts[:, 0:LT * NE].rearrange("p (a t e) -> p a t e", a=1, t=LT)
                                    .broadcast_to([P, TOPK, LT, NE]), ALU.mult).then_inc(v_pos, 1)
                dve.wait_ge(v_pos, 4 * b + 1)
                v.tensor_reduce(rank[:, :], pk[:, :, :, :].rearrange("p k t e -> p (k t) e"), AX_X, ALU.add)\
                    .then_inc(v_pos, 1)
                dve.wait_ge(v_pos, 4 * b + 2)
                v.tensor_tensor(cmp[:, :, :], bc3(rank[:, :], COLS - 1),
                                    c("step").rearrange("p (a n) -> p a n", a=1).broadcast_to([P, TOPK * LT, COLS - 1]),
                                    ALU.is_ge).then_inc(v_pos, 1)
                dve.wait_ge(v_pos, 4 * b + 3)
                v.tensor_reduce(ltile[:, :], cmp[:, :, :], AX_X, ALU.add).then_inc(v_pos, 1)
                dve.wait_ge(v_pos, 4 * b + 4)
                v.scalar_tensor_tensor(out=lrow[:, :], in0=ltile[:, :], scalar=-float(P), in1=rank[:, :],
                                           op0=ALU.mult, op1=ALU.add).then_inc(v_key, 1)
                v.scalar_tensor_tensor(out=key[:, :], in0=ef[:, :, :].rearrange("p k t -> p (k t)"),
                                           scalar=float(COLS), in1=ltile[:, :], op0=ALU.mult, op1=ALU.add)\
                                               .then_inc(v_key, 1)
                dve.wait_ge(v_key, 3 * b + 1)
                a0 = CONST["token"][0]
                tok = cst[:, bass.ds(a0 + b * LT, LT)].rearrange("p (a t) -> p a t", a=1).broadcast_to([P, TOPK, LT])
                v.tensor_tensor(val[:, :].rearrange("p (k t) -> p k t", k=TOPK), tok,
                                    lrow[:, :].rearrange("p (k t) -> p k t", k=TOPK), ALU.subtract).then_inc(v_key, 1)

            def puts(b, half):
                dve.wait_ge(v_key, 3 * b + 3)
                for q in range(4 * half, 4 * half + 4):
                    dve.wait_ge(p_map, 8 * b + max(q - 3, 0) + 1)
                    v.tensor_scalar(hot[:, q % 4, :], c("iota"), lrow[:, q:q + 1], None, ALU.is_equal)\
                        .then_inc(v_hot, 1)
                    v.tensor_scalar(put[:, q % 4, :], c("iota"), key[:, q:q + 1], val[:, q:q + 1],
                                        ALU.is_equal, ALU.mult).then_inc(v_put, 1)

            dve.wait_ge(d_x0, 16)
            stats1(0, LT, LT)
            aggr1(0, LT, 0)
            norm1(0)
            for k in range(KD):
                dve.wait_ge(a_k, k + 1)
                v.scalar_tensor_tensor(out=kT_l[:, k, :].bitcast(F32R), in0=bankC[:, k, 0:B * S],
                                       scalar=bias[:, 1, k:k + 1], in1=kT_h[:, k, :],
                                       op0=ALU.add, op1=ALU.subtract).then_inc(v_k, 1)

            def weight_low(low, high, n):
                v.tensor_tensor(low[:, :, :], wraw[:, n, :].rearrange("p (k n) -> p k n", k=KD),
                                high[:, :, :].bitcast(F32), ALU.subtract).then_inc(v_wsplit, 1)

            dve.wait_ge(a_wsplit, 1)
            weight_low(wq_l, wq_h, 0)
            x_low(0, 0)
            x_low(0, 1)
            q_low(0)
            dve.wait_ge(d_const, 16)
            dve.wait_ge(g_zero, 4)
            dve.wait_ge(v_seen, 2)
            for t in range(LT):
                maxima(0, t)
            max_split(0)
            dve.wait_ge(a_wsplit, 2)
            weight_low(we_l, we_h, 3)
            dve.wait_ge(d_x, 16)
            stats1(LT, NTOK - LT, LT)
            aggr1(LT, NTOK - LT, 2 * LT)
            dve.wait_ge(d_w, 64)

            def batch(i, with_router):
                norm1(i)
                x_low(i, 0)
                if with_router:
                    router(i - 2)
                x_low(i, 1)
                if with_router:
                    ranks(i - 2, bankC[:, 2, :])
                    count(i - 2)
                q_low(i)
                rden_split(i - 1)
                maxima(i, 0)
                maxima(i, 1)
                att(i - 1)
                maxima(i, 2)
                att_low(i - 1, (0,))
                maxima(i, 3)
                max_split(i)
                residual_norm2(i - 1)
                if with_router:
                    puts(i - 2, 0)
                    puts(i - 2, 1)
                logits(i - 1)

            batch(1, False)
            with dve.Fori(2, B) as i:
                batch(i, True)
            router(B - 2)
            ranks(B - 2, bankB1)
            count(B - 2)
            puts(B - 2, 0)
            puts(B - 2, 1)
            rden_split(B - 1)
            att(B - 1)
            att_low(B - 1, range(KD))
            residual_norm2(B - 1)
            logits(B - 1)
            router(B - 1)
            ranks(B - 1, bankB1)

            v.tensor_tensor(big[:, :, :], bc3(bankB1[:, LT * NE:(LT + 1) * NE], COLS - 1),
                                c("step").rearrange("p (a n) -> p a n", a=1).broadcast_to([P, NE, COLS - 1]),
                                ALU.is_gt).then_inc(v_done, 1)
            puts(B - 1, 0)
            puts(B - 1, 1)
            dve.wait_ge(p_fin, 1)
            v.tensor_scalar(slot[:, 0:NE * COLS], bankM[:, 0:NE * COLS], c("spare"), None, ALU.add)\
                .then_inc(v_slot, 1)
            v.tensor_scalar(slot[:, NE * COLS:MAPC], c("iota")[:, 0:32], 0.0, c("spare"), ALU.mult, ALU.add)\
                .then_inc(v_slot, 1)
            dve.wait_ge(v_done, 1)
            v.tensor_reduce(ntile[:, :], big[:, :, :], AX_X, ALU.add).then_inc(v_done, 1)
            dve.wait_ge(v_done, 2)
            v.tensor_scalar(ntile[:, :], ntile[:, :], 1.0, float(MINT), ALU.add, ALU.max).then_inc(v_done, 1)
            dve.wait_ge(v_done, 3)
            v.tensor_tensor_scan(tend[:, :], c("ones")[:, 0:NE], ntile[:, :], 0.0, ALU.mult, ALU.add)\
                .then_inc(v_done, 1)
            dve.wait_ge(v_done, 4)
            v.tensor_tensor(tbeg[:, :], tend[:, :], ntile[:, :], ALU.subtract).then_inc(v_done, 1)
            dve.wait_ge(v_done, 5)
            v.tensor_scalar(on[:, :], tbeg[:, :], c("tile"), None, ALU.is_le).then_inc(v_done, 1)
            v.scalar_tensor_tensor(out=onb[:, :], in0=tbeg[:, :], scalar=c("tile"), in1=tbeg[:, :],
                                   op0=ALU.is_le, op1=ALU.mult).then_inc(v_done, 1)
            v.scalar_tensor_tensor(out=onf[:, :], in0=tbeg[:, :], scalar=c("tile"), in1=c("flip"),
                                   op0=ALU.is_le, op1=ALU.mult).then_inc(v_done, 1)
            v.scalar_tensor_tensor(out=onf2[:, :], in0=tbeg[:, :], scalar=c("tile2"), in1=c("flip"),
                                   op0=ALU.is_le, op1=ALU.mult).then_inc(v_done, 1)
            v.tensor_copy(pack[:, 5:8], tend[:, NE - 1:NE].broadcast_to([P, 3])).then_inc(v_done, 1)
            dve.wait_ge(v_done, 9)
            v.tensor_reduce(te1[:, :], on[:, :], AX_X, ALU.add).then_inc(v_done, 1)
            v.tensor_reduce(tb[:, :], onb[:, :], AX_X, ALU.max).then_inc(v_done, 1)
            v.tensor_reduce(pack[:, 4:5], onf[:, :], AX_X, ALU.add).then_inc(v_done, 1)
            v.tensor_reduce(par2[:, :], onf2[:, :], AX_X, ALU.add).then_inc(v_done, 1)
            dve.wait_ge(v_done, 12)
            v.tensor_scalar(tone[:, :], tb[:, :], -1.0, c("tile"), ALU.mult, ALU.add).then_inc(v_done, 1)
            v.tensor_scalar(tlt[:, :], te1[:, :], float(NE) - 0.5, None, ALU.is_lt).then_inc(v_done, 1)
            v.tensor_scalar(pack[:, 3:4], te1[:, :], -1.0, None, ALU.add).then_inc(v_done, 1)
            dve.wait_ge(v_done, 16)
            v.tensor_scalar(tsec[:, :], tone[:, :], 1.0, tlt[:, :], ALU.is_equal, ALU.mult).then_inc(v_done, 1)
            v.scalar_tensor_tensor(out=pair[:, :], in0=pack[:, 4:5], scalar=2.0, in1=par2[:, :],
                                   op0=ALU.mult, op1=ALU.add).then_inc(v_done, 1)
            dve.wait_ge(v_done, 17)
            v.scalar_tensor_tensor(out=pack[:, 1:2], in0=pack[:, 3:4], scalar=float(COLS), in1=tone[:, :],
                                   op0=ALU.mult, op1=ALU.add).then_inc(v_done, 1)
            dve.wait_ge(v_done, 18)
            v.tensor_tensor(tsp[:, :], te1[:, :], tsec[:, :], ALU.mult).then_inc(v_done, 1)
            dve.wait_ge(v_done, 19)
            v.scalar_tensor_tensor(out=pack[:, 0:1], in0=pack[:, 3:4], scalar=4.0, in1=pair[:, :],
                                   op0=ALU.mult, op1=ALU.add).then_inc(v_done, 1)
            dve.wait_ge(v_done, 21)
            v.tensor_scalar(traw[:, :], tsp[:, :], -1.0, 1.0, ALU.add, ALU.max).then_inc(v_done, 1)
            v.scalar_tensor_tensor(out=tsp[:, :], in0=tsp[:, :], scalar=16.0, in1=pack[:, 4:5],
                                   op0=ALU.mult, op1=ALU.add).then_inc(v_done, 1)
            dve.wait_ge(v_done, 24)
            v.scalar_tensor_tensor(out=pack[:, 2:3], in0=traw[:, :], scalar=2.0, in1=tsp[:, :],
                                   op0=ALU.mult, op1=ALU.add).then_inc(v_pack, 1)
            dve.wait_ge(p_tab, 1)
            v.tensor_copy(tab[:, :], bankA[0:8, 1, 0:NTAB]).then_inc(v_tab, 1)

            def x_low_f(t, ring, nth):
                e = 0 if isinstance(t, int) and t < MINT else dve.value_load(te_i[:, bass.ds(t, 1)], min_val=0, max_val=NE - 1)
                dve.wait_ge(d_gather[ring], 16 * (nth + 1))
                v.tensor_copy(gate[:, bass.ds(t, 1)], xr[:, ring, bass.ds(D + e, 1)]).then_inc(v_gate, 1)
                dve.wait_ge(a_fxT, t + 1)
                v.tensor_tensor(xT_l, bankA[:, 0, 0:D], xT_h.bitcast(F32), ALU.subtract).then_inc(v_fxT, 1)

            def h_low(t):
                for n in range(2):
                    dve.wait_ge(a_fhT, 2 * t + n + 1)
                    o = slice(n * 512, (n + 1) * 512)
                    v.tensor_tensor(hT_l[:, o], bankB[n][:, :], hT_h[:, o].bitcast(F32), ALU.subtract)\
                        .then_inc(v_fhT, 1)

            def result(t):
                dve.wait_ge(a_osb, t + 1)
                if not (isinstance(t, int) and t == 0):
                    dve.wait_ge(d_add, 16 * t)
                v.scalar_tensor_tensor(out=y, in0=bankC[:, 2, 0:D], scalar=gate[:, bass.ds(t, 1)],
                                           in1=osb, op0=ALU.mult, op1=ALU.add).then_inc(v_y, 1)

            def weights_low(e, other, half):
                with dve.If(e > 1):
                    for n in range(2):
                        dve.wait_ge(a_whi, 4 * e + 2 * half + n + 1)
                        settle(10 + 2 * half + n)
                        if half:
                            dst = dn_w[:, bass.ds(other, 1), 4 * n:4 * n + 4, :, :].rearrange("p a c h n -> p (a c) h n")
                            v.tensor_tensor(dst[:, :, 1, :],
                                                raw[:, 2048 + n * 1024:2048 + (n + 1) * 1024]
                                                .rearrange("p (c n) -> p c n", c=4),
                                                dst[:, :, 0, :].bitcast(F32), ALU.subtract).then_inc(v_wlo, 1)
                        else:
                            v.tensor_tensor(up_w[:, 1, bass.ds(other, 1), n, :].rearrange("p a n -> p (a n)"),
                                                raw[:, n * FF:(n + 1) * FF],
                                                up_w[:, 0, bass.ds(other, 1), n, :].bitcast(F32)
                                                .rearrange("p a n -> p (a n)"), ALU.subtract).then_inc(v_wlo, 1)

            dve.wait_ge(g_w01, 8)
            v.memset(prime[:, 1:2], 0.0).then_inc(v_wlo, 8)
            x_low_f(0, 0, 0)
            x_low_f(1, 1, 0)
            h_low(0)
            dve.wait_ge(v_tab, 1)
            nt = dve.value_load(nt_i, min_val=MINT * NE, max_val=NT)

            def tile(t, ring, nth):
                x_low_f(t + 1, ring, nth)
                split = dve.value_load(split_i[:, bass.ds(t, 1)], min_val=2, max_val=127)
                sp_e, other = split // 16, 1 - split % 2
                weights_low(sp_e, other, 0)
                result(t - 1)
                h_low(t)
                weights_low(sp_e, other, 1)

            tile(1, 0, 1)
            with dve.Fori(1, NT // 2) as u:
                t = 2 * u
                with dve.If(nt > t):
                    tile(t, 1, u)
                    with dve.If(nt > t + 1):
                        tile(t + 1, 0, u + 1)
                        with dve.If(nt < t + 3):
                            result(t + 1)
                    with dve.Else():
                        result(t)
        @block.tensor
        def _(pe):
            mm = nc.tensor.matmul
            ident = c("ident")

            def three(out_, left_h, left_l, right_h, right_l, first, last):
                mm(out_, left_h, right_h, start=first, stop=False)
                mm(out_, left_h, right_l, start=False, stop=False)
                return mm(out_, left_l, right_h, start=False, stop=last)

            def keys():
                pe.wait_ge(d_k, 48)
                for k in range(KD):
                    for d in range(KD):
                        last = mm(bankC[:, k, 0:B * S], wraw[:, 1, d * D + k * P:d * D + (k + 1) * P], ctxT[:, d, :],
                                  start=(d == 0), stop=(d == KD - 1))
                    last.then_inc(p_kv, 1)

            def values_of_two(n):
                pe.wait_ge(d_v, 32)
                for h in range(2):
                    for d in range(KD):
                        last = mm(bankA[:, n, h * D:(h + 1) * D], ctxT2[:, d, 2 * n + h, :],
                                  wraw[:, 2, d * D:(d + 1) * D], start=(d == 0), stop=(d == KD - 1))
                last.then_inc(p_kv, 1)

            def x_turn(b, n):
                if not (isinstance(b, int) and b == 0 and n == 0):
                    pe.wait_ge(v_xT, 2 * b + n)
                for t in range(2):
                    pe.wait_ge(v_xn, LT * b + 2 * n + t + 1)
                    for k in range(KD):
                        o = (t * KD + k) * P
                        last = nc.tensor.transpose(bankB1[:, o:o + P], xn[:, 2 * n + t, k * P:(k + 1) * P], ident)
                last.then_inc(p_xT, 1)

            def project_q(b):
                pe.wait_ge(v_xT, 2 * b + 2)
                if isinstance(b, int) and b == 0:
                    pe.wait_ge(v_wsplit, 1)
                for k in (1, 0):
                    if k == 0 and not (isinstance(b, int) and b == 0):
                        pe.wait_ge(a_den, b)
                    o = slice(k * P, (k + 1) * P)
                    for d in range(KD):
                        last = three(bankB[k][:, :], wq_h[:, d, o], wq_l[:, d, o], xnT_h[:, d, :], xnT_l[:, d, :],
                                     d == 0, d == KD - 1)
                    last.then_inc(p_q, 1)

            def scores(b, t):
                for k in range(KD):
                    n = KD * t + k
                    if n == 0:
                        pe.wait_ge(v_q, KD * b + 2)
                        pe.wait_ge(g_kbd, 4 * b + 4)
                    if n >= 3:
                        pe.wait_ge(v_max, 8 * b + n - 2)
                    o = slice(t * P, (t + 1) * P)
                    three(bankC[:, n % 3, :], q_h[:, k, o], q_l[:, k, o],
                          kbd_h[:, k, :, :].rearrange("p h s -> p (h s)"), kbd_l[:, k, :, :].rearrange("p h s -> p (h s)"),
                          True, True).then_inc(p_s, 1)

            def max_turn(b):
                pe.wait_ge(v_nml, b + 1)
                for t in range(LT):
                    last = nc.tensor.transpose(bankC[:, 2, t * P:(t + 1) * P], nmx[:, t, :], ident)
                last.then_inc(p_nmT, 1)

            def scores_turned(b, js):
                for j in js:
                    k, i = j // 4, j % 4
                    if j == 0:
                        pe.wait_ge(a_nmT, b + 1)
                        pe.wait_ge(a_const, 4)
                    if j >= 3:
                        pe.wait_ge(a_exp, 8 * b + j - 2)
                    kh = kbd_h[:, k, 2 * i:2 * i + 2, :].rearrange("p h s -> p (h s)")
                    kl = kbd_l[:, k, 2 * i:2 * i + 2, :].rearrange("p h s -> p (h s)")
                    three(bankC[:, j % 3, :], kh, kl, q_h[:, k, :], q_l[:, k, :], True, False)
                    mm(bankC[:, j % 3, :], sel_r[:, j, :], nmxT[:, :], start=False, stop=True).then_inc(p_sT, 1)

            def values(b, js):
                for j in js:
                    k, i = j // 4, j % 4
                    if j == 0:
                        pe.wait_ge(g_vbd, b + 1)
                        if not (isinstance(b, int) and b == 0):
                            pe.wait_ge(v_lg, 3 * (b - 1) + 1)
                    pe.wait_ge(a_exp, 8 * b + j + 1)
                    o = slice(32 * i, 32 * i + 32)
                    mm(bankA[o, k, :], vbd[:, j, :], prob[:, i, :], start=True, stop=True).then_inc(p_av, 1)
                    mm(bankB0[o, :], c("densel")[:, 32 * k:32 * k + 32], prob[:, i, :], start=(k == 0),
                       stop=(k == 1), skip_group_check=True).then_inc(p_av, 1)

            def den_turn(b):
                pe.wait_ge(a_den, b + 1)
                pe.wait_ge(a_av, KD * b + 1)
                for t in range(LT):
                    last = nc.tensor.transpose(bankA[:, 0, t * P:(t + 1) * P], den[:, t * P:(t + 1) * P], ident)
                last.then_inc(p_denT, 1)

            def rden_turn(b):
                pe.wait_ge(v_rdl, b + 1)
                pe.wait_ge(a_av, KD * b + 2)
                for t in range(LT):
                    last = nc.tensor.transpose(bankA[:, 1, t * P:(t + 1) * P], rdm[:, t, :], ident)
                last.then_inc(p_rdT, 1)

            def spread(b):
                pe.wait_ge(a_rdT, b + 1)
                pe.wait_ge(a_av, KD * b + 2)
                for k in range(KD):
                    mm(bankA[:, k, :], feat_r[:, k, :], rdT[:, :], start=True, stop=True).then_inc(p_bc, 1)

            def project_out(b):
                if isinstance(b, int) and b == B - 1:
                    pe.wait_ge(v_at, b + KD)
                else:
                    pe.wait_ge(v_at, b + 1)
                    pe.wait_ge(g_at, b + 1)
                for n in range(2):
                    for h in range(2):
                        o = slice((2 * n + h) * P, (2 * n + h + 1) * P)
                        for k in range(KD):
                            last = three(bankB[n][:, h * D:(h + 1) * D], at_h[:, k, o], at_l[:, k, o],
                                         we_h[:, k, :], we_l[:, k, :], k == 0, k == KD - 1)
                    last.then_inc(p_proj, 1)

            def x2_turn(b):
                for n in range(2):
                    for t in range(2):
                        pe.wait_ge(v_xn2, LT * b + 2 * n + t + 1)
                        for k in range(KD):
                            o = (t * KD + k) * P
                            last = nc.tensor.transpose(bankA[:, n, o:o + P], xr[:, 2 * n + t, k * P:(k + 1) * P], ident)
                    last.then_inc(p_x2T, 1)

            def logits(b):
                pe.wait_ge(v_x1, 2 * b + 2)
                for k in range(KD):
                    for t in range(LT):
                        pe.wait_ge(a_x2T, 2 * b + t // 2 + 1)
                        last = mm(bankB0[32 * t:32 * t + 32, 0:P], rw[:, k, :], x2T[:, t, k, :],
                                  start=(k == 0), stop=(k == KD - 1), skip_group_check=True)
                last.then_inc(p_lg, 1)

            def logits_turn(b):
                pe.wait_ge(a_lgT, b + 1)
                nc.tensor.transpose(bankB0[:, P:2 * P], lgT[:, :], ident).then_inc(p_lgT, 1)

            def positions(b, counts):
                pe.wait_ge(v_mbf, b + 1)
                pe.wait_ge(v_seen, 2 * b + 2)
                last_batch = isinstance(b, int) and b == B - 1
                flat = msum_bf[:, :, :].rearrange("p t e -> p (t e)")
                if last_batch:
                    everyone = counts[:, LT * NE:(LT + 1) * NE]
                    mm(everyone, ones_bf[:, :], seen_bf[:, :], start=True, stop=False, skip_group_check=True)
                    for t in range(LT):
                        mm(everyone, ones_bf[:, :], msum_bf[:, t, :], start=False, stop=(t == LT - 1),
                           skip_group_check=True)
                mm(counts[:, 0:LT * NE], upper_bf[:, :], flat, start=True, stop=False, skip_group_check=True)
                for d in range(1, LT):
                    mm(counts[:, d * NE:LT * NE], ones_bf[:, :], flat[:, 0:(LT - d) * NE], start=False,
                       stop=False, skip_group_check=True)
                mm(counts[:, 0:LT * NE], ones_bf[:, :],
                   seen_bf[:, :].rearrange("p (a e) -> p a e", a=1).broadcast_to([P, LT, NE]), start=False,
                   stop=True, skip_group_check=True).then_inc(p_pos, 1)

            def slots(b, half):
                for q in range(4 * half, 4 * half + 4):
                    pe.wait_ge(v_hot, 8 * b + q + 1)
                    pe.wait_ge(v_put, 8 * b + q + 1)
                    mm(bankM[:, 0:P], hot[:, q % 4, :], put[:, q % 4, :], start=False, stop=False,
                       skip_group_check=True).then_inc(p_map, 1)

            keys()
            pe.wait_ge(g_zero, 4)
            mm(bankM[:, 0:P], zero_r[:, :], zero_r[:, :], start=True, stop=False, skip_group_check=True)\
                .then_inc(p_map, 1)
            pe.wait_ge(d_const, 16)
            x_turn(0, 0)
            x_turn(0, 1)
            project_q(0)
            values_of_two(0)
            for t in range(LT):
                scores(0, t)
            values_of_two(1)
            max_turn(0)
            scores_turned(0, range(4))

            def batch(i, router):
                values(i - 1, range(4))
                x_turn(i, 0)
                scores_turned(i - 1, range(4, 8))
                x_turn(i, 1)
                if router:
                    pe.wait_ge(a_exp, 8 * i - 2)
                    positions(i - 2, bankC[:, 2, :])
                values(i - 1, range(4, 8))
                project_q(i)
                den_turn(i - 1)
                scores(i, 0)
                rden_turn(i - 1)
                scores(i, 1)
                spread(i - 1)
                scores(i, 2)
                scores(i, 3)
                project_out(i - 1)
                max_turn(i)
                scores_turned(i, range(4))
                x2_turn(i - 1)
                if router:
                    slots(i - 2, 0)
                logits(i - 1)
                logits_turn(i - 1)
                if router:
                    slots(i - 2, 1)

            batch(1, False)
            with pe.Fori(2, B) as i:
                batch(i, True)
            values(B - 1, range(4))
            positions(B - 2, bankB1)
            scores_turned(B - 1, range(4, 8))
            slots(B - 2, 0)
            slots(B - 2, 1)
            values(B - 1, range(4, 8))
            den_turn(B - 1)
            rden_turn(B - 1)
            spread(B - 1)
            project_out(B - 1)
            x2_turn(B - 1)
            logits(B - 1)
            logits_turn(B - 1)
            positions(B - 1, bankB1)
            pe.wait_ge(v_done, 1)
            slots(B - 1, 0)
            slots(B - 1, 1)
            mm(bankM[:, 0:P], zero_r[:, :], zero_r[:, :], start=False, stop=True, skip_group_check=True)\
                .then_inc(p_fin, 1)

            def x_turn_f(t, ring, nth):
                pe.wait_ge(d_gather[ring], 16 * (nth + 1))
                for k in range(KD):
                    last = nc.tensor.transpose(bankA[:, 0, k * P:(k + 1) * P], xr[:, ring, k * P:(k + 1) * P], ident)
                last.then_inc(p_fxT, 1)

            def h_turn(t):
                for n in range(2):
                    pe.wait_ge(a_gelu, 2 * t + n + 1)
                    for m in range(4):
                        o = (4 * n + m) * P
                        last = nc.tensor.transpose(bankB[n][:, m * P:(m + 1) * P], hbuf[:, o:o + P], ident)
                    last.then_inc(p_fhT, 1)

            def up_product(t, par):
                pe.wait_ge(v_fxT, t + 1)
                for n in range(2):
                    o = slice(n * 512, (n + 1) * 512)
                    for k in range(KD):
                        x_o = slice(k * P, (k + 1) * P)
                        last = three(bankC[:, n, :], xT_h[:, x_o], xT_l[:, x_o],
                                     up_w[:, 0, bass.ds(par, 1), k, o].rearrange("p a n -> p (a n)"),
                                     up_w[:, 1, bass.ds(par, 1), k, o].rearrange("p a n -> p (a n)"),
                                     k == 0, k == KD - 1)
                    last.then_inc(p_up, 1)

            def down_product(t, par):
                for m in range(KF):
                    if m % 4 == 0:
                        pe.wait_ge(v_fhT, 2 * t + m // 4 + 1)
                    o = slice(m * P, (m + 1) * P)
                    wd = dn_w[:, bass.ds(par, 1), m, :, :].rearrange("p a h n -> p (a h n)")
                    mm(bankC[:, 2, :], hT_h[:, o], wd, start=(m == 0), stop=False)
                    last = mm(bankC[:, 2, 0:D], hT_l[:, o], wd[:, 0:D], start=False, stop=(m == KF - 1))
                last.then_inc(p_dn, 1)

            pe.wait_ge(v_pack, 1)
            nc.tensor.transpose(bankA[0:8, 1, 0:NTAB], pack[0:NTAB, :], ident[0:NTAB, 0:NTAB]).then_inc(p_tab, 1)
            pe.wait_ge(v_wlo, 8)
            x_turn_f(0, 0, 0)
            up_product(0, 0)
            x_turn_f(1, 1, 0)
            h_turn(0)
            up_product(1, 0)
            pe.wait_ge(v_tab, 1)
            nt = pe.value_load(nt_i, min_val=MINT * NE, max_val=NT)

            def tile(t, ring, nth):
                word = pe.value_load(w_i[:, bass.ds(t + 1, 1)], min_val=0, max_val=4 * NE - 1)
                x_turn_f(t + 1, ring, nth)
                down_product(t - 1, word % 2)
                h_turn(t)
                return word

            def next_up(t, word):
                pe.wait_ge(v_wlo, 4 * (word // 4) + 4)
                up_product(t, word // 2 % 2)

            def last_down(t):
                par = pe.value_load(tpar_i[:, bass.ds(t, 1)], min_val=0, max_val=1)
                down_product(t, par)

            word = tile(1, 0, 1)
            next_up(2, word)
            with pe.Fori(1, NT // 2) as u:
                t = 2 * u
                with pe.If(nt > t):
                    word = tile(t, 1, u)
                    with pe.If(nt > t + 1):
                        next_up(t + 1, word)
                        word = tile(t + 1, 0, u + 1)
                        with pe.If(nt > t + 2):
                            next_up(t + 2, word)
                        with pe.Else():
                            last_down(t + 1)
                    with pe.Else():
                        last_down(t)


def kernel(**inputs):
    import numpy as np
    import concourse.bacc as bacc
    from concourse.bass_utils import run_bass_kernel_spmd

    a = {k: np.asarray(v_) for k, v_ in inputs.items()}
    ctx_ = a["ctx_1024"]
    up = a["L0_ffn_expert_up"].transpose(0, 2, 1).reshape(2 * NE, P, FF)
    down = a["L0_ffn_expert_down"].transpose(0, 2, 1).reshape(NE, 2, 4, P, D).transpose(0, 1, 3, 2, 4)
    arrays = {
        "x": a["x"].reshape(T, D),
        "ctx_t": ctx_.transpose(2, 0, 1).reshape(D, B * S),
        "ctx_t2": np.concatenate([ctx_, ctx_], axis=1).transpose(2, 0, 1).reshape(D, B * 2 * S),
        "wq": a["L0_xattn_Wq"], "wk": a["L0_xattn_Wk"], "wv": a["L0_xattn_Wv"], "we": a["L0_xattn_We"],
        "bqk": np.stack([a[f"L0_xattn_b{n}"].reshape(KD, P) for n in "qk"]).transpose(2, 0, 1).reshape(P, 2 * KD),
        "bv": a["L0_xattn_bv"],
        "be": a["L0_xattn_be"],
        "router_w": a["L0_ffn_router_w"], "router_b": a["L0_ffn_router_b"],
        "up": up, "down": down.reshape(2 * NE, P, 4 * D),
        "const": constants(),
    }
    arrays = {k: np.ascontiguousarray(v_) for k, v_ in arrays.items()}
    nc = bacc.Bacc("TRN2", target_bir_lowering=False, num_devices=1)
    args = [nc.dram_tensor(k, v_.shape, mybir.dt.from_np(v_.dtype), kind="ExternalInput").ap()
            for k, v_ in arrays.items()]
    out = nc.dram_tensor("out", (T + P, D), F32, kind="ExternalOutput").ap()
    rows = nc.dram_tensor("rows", (T + P, XROW), F32, kind="Internal").ap()
    build(nc, *args, out, rows)
    r = run_bass_kernel_spmd(nc, [arrays], core_ids=[0])
    return r.results[0]["out"][0:T].reshape(B, L, D)
```
